# Optimizing a Trainium2 kernel written in Bass

```python
import numpy as np
import jax
import jax.numpy as jnp

def _softmax(x, axis=-1):
    return jax.nn.softmax(x, axis=axis)

def _gelu(x):
    return jax.nn.gelu(x, approximate=True)

def _silu(x):
    return jax.nn.silu(x)

def _sigmoid(x):
    return jax.nn.sigmoid(x)

def _layernorm(x, axis=-1, eps=1e-05):
    m = jnp.mean(x, axis=axis, keepdims=True)
    v = jnp.var(x, axis=axis, keepdims=True)
    return (x - m) / jnp.sqrt(v + eps)

def _scatter_add(tgt, idx, src, axis=0):
    return tgt.at[idx].add(src)

def _segment_sum(src, seg, n):
    return jax.ops.segment_sum(src, seg, n)
kernel_name = 'mk_hybrid_d1_jaxref_r8_e7793c'

def setup_inputs(seed: int=0):
    np.random.seed(seed)
    _w = jnp.asarray

    def _L0_attn_a_setup():
        import jax, jax.numpy as jnp
        import numpy as np
        D_MODEL = 128
        D_QK = 128
        NUM_HEADS = 16
        HEAD_DIM = D_QK // NUM_HEADS
        V_DIM = D_MODEL // NUM_HEADS
        B, S = (2, 256)
        key = jax.random.key(seed)
        ks = jax.random.split(key, 9)
        sc = 0.02
        return {'x': jax.random.normal(ks[0], (B, S, D_MODEL), dtype=jnp.float32), 'Wqk': jax.random.normal(ks[1], (D_MODEL, 2 * D_QK), dtype=jnp.float32) * sc, 'bqk': jax.random.normal(ks[2], (2 * D_QK,), dtype=jnp.float32) * sc, 'Wv': jax.random.normal(ks[3], (D_MODEL, D_MODEL), dtype=jnp.float32) * sc, 'bv': jax.random.normal(ks[4], (D_MODEL,), dtype=jnp.float32) * sc, 'Wn': jax.random.normal(ks[5], (D_MODEL, NUM_HEADS), dtype=jnp.float32) * sc, 'bn': jax.random.normal(ks[6], (NUM_HEADS,), dtype=jnp.float32) * sc, 'Wo': jax.random.normal(ks[7], (D_MODEL, D_MODEL), dtype=jnp.float32) * sc, 'bo': jax.random.normal(ks[8], (D_MODEL,), dtype=jnp.float32) * sc}
    _L0_attn_a_in = _L0_attn_a_setup()

    def _L0_attn_b_setup():
        import jax, jax.numpy as jnp
        import numpy as np
        D_MODEL = 128
        N_HEADS = 16
        key = jax.random.key(seed)
        ks = jax.random.split(key, 9)
        B, L, D = (4, 256, D_MODEL)
        s = 1.0 / np.sqrt(D)
        return {'x': jax.random.normal(ks[0], (B, L, D), dtype=jnp.float32), 'wq': jax.random.normal(ks[1], (D, D), dtype=jnp.float32) * s, 'bq': jnp.zeros((D,), dtype=jnp.float32), 'wk': jax.random.normal(ks[2], (D, D), dtype=jnp.float32) * s, 'bk': jnp.zeros((D,), dtype=jnp.float32), 'wv': jax.random.normal(ks[3], (D, D), dtype=jnp.float32) * s, 'bv': jnp.zeros((D,), dtype=jnp.float32), 'wo': jax.random.normal(ks[4], (D, D), dtype=jnp.float32) * s, 'bo': jnp.zeros((D,), dtype=jnp.float32)}
    _L0_attn_b_in = _L0_attn_b_setup()

    def _L0_ffn_setup():
        import math
        import jax, jax.numpy as jnp
        from jax import lax
        import numpy as np
        E = 16
        K = 2
        CF = 1.25
        key = jax.random.key(seed)
        k0, k1, k2, k3, k4 = jax.random.split(key, 5)
        B, S, D, H = (2, 256, 128, 128)
        scale = 0.02
        return {'x': jax.random.normal(k0, (B, S, D), dtype=jnp.float32), 'router_w': jax.random.normal(k1, (D, E), dtype=jnp.float32) * scale, 'gate_w': jax.random.normal(k2, (E, D, H), dtype=jnp.float32) * scale, 'up_w': jax.random.normal(k3, (E, D, H), dtype=jnp.float32) * scale, 'down_w': jax.random.normal(k4, (E, H, D), dtype=jnp.float32) * scale}
    _L0_ffn_in = _L0_ffn_setup()
    _d = {'L0_attn_a_x': _L0_attn_a_in['x'], 'L0_attn_a_Wqk': _L0_attn_a_in['Wqk'], 'L0_attn_a_bqk': _L0_attn_a_in['bqk'], 'L0_attn_a_Wv': _L0_attn_a_in['Wv'], 'L0_attn_a_bv': _L0_attn_a_in['bv'], 'L0_attn_a_Wn': _L0_attn_a_in['Wn'], 'L0_attn_a_bn': _L0_attn_a_in['bn'], 'L0_attn_a_Wo': _L0_attn_a_in['Wo'], 'L0_attn_a_bo': _L0_attn_a_in['bo'], 'L0_attn_b_wq': _L0_attn_b_in['wq'], 'L0_attn_b_bq': _L0_attn_b_in['bq'], 'L0_attn_b_wk': _L0_attn_b_in['wk'], 'L0_attn_b_bk': _L0_attn_b_in['bk'], 'L0_attn_b_wv': _L0_attn_b_in['wv'], 'L0_attn_b_bv': _L0_attn_b_in['bv'], 'L0_attn_b_wo': _L0_attn_b_in['wo'], 'L0_attn_b_bo': _L0_attn_b_in['bo'], 'L0_ffn_router_w': _L0_ffn_in['router_w'], 'L0_ffn_gate_w': _L0_ffn_in['gate_w'], 'L0_ffn_up_w': _L0_ffn_in['up_w'], 'L0_ffn_down_w': _L0_ffn_in['down_w']}
    _x0 = _d['L0_attn_a_x']
    _d['L0_attn_a_x'] = jax.random.normal(jax.random.fold_in(jax.random.key(seed), 1), (16, 512, 128), dtype=_x0.dtype)
    del _x0
    return _d

def reference(L0_attn_a_x, L0_attn_a_Wqk, L0_attn_a_bqk, L0_attn_a_Wv, L0_attn_a_bv, L0_attn_a_Wn, L0_attn_a_bn, L0_attn_a_Wo, L0_attn_a_bo, L0_attn_b_wq, L0_attn_b_bq, L0_attn_b_wk, L0_attn_b_bk, L0_attn_b_wv, L0_attn_b_bv, L0_attn_b_wo, L0_attn_b_bo, L0_ffn_router_w, L0_ffn_gate_w, L0_ffn_up_w, L0_ffn_down_w):

    def _L0_attn_a_ref(x, Wqk, bqk, Wv, bv, Wn, bn, Wo, bo):
        import jax, jax.numpy as jnp
        import numpy as np
        D_MODEL = 128
        D_QK = 128
        NUM_HEADS = 16
        HEAD_DIM = D_QK // NUM_HEADS
        V_DIM = D_MODEL // NUM_HEADS
        B, S = (2, 256)
        b, s, _ = x.shape
        qk = x @ Wqk + bqk
        v = x @ Wv + bv
        n = x @ Wn + bn
        qk = qk.reshape(b, s, 2, NUM_HEADS, HEAD_DIM)
        q, k = (qk[:, :, 0], qk[:, :, 1])
        v = v.reshape(b, s, NUM_HEADS, V_DIM)
        scores = jnp.einsum('bthd,bshd->bhts', q, k)
        mask = jnp.tril(jnp.ones((s, s), dtype=scores.dtype))
        n_exp = jnp.exp(jnp.transpose(n, (0, 2, 1)))
        attn = scores * mask / n_exp[:, :, :, None]
        ctx = jnp.einsum('bhts,bshd->bthd', attn, v)
        ctx = ctx.reshape(b, s, D_MODEL)
        return ctx @ Wo + bo

    def _L0_attn_b_ref(x, wq, bq, wk, bk, wv, bv, wo, bo):
        import jax, jax.numpy as jnp
        import numpy as np
        D_MODEL = 128
        N_HEADS = 16
        B, L, D = x.shape
        H = N_HEADS
        d_k = D // H
        scale = 1.0 / np.sqrt(d_k).astype(np.float32)

        def proj(w, b):
            return (x @ w.T + b).reshape(B, L, H, d_k).transpose(0, 2, 1, 3)
        Q = proj(wq, bq)
        K = proj(wk, bk)
        V = proj(wv, bv)
        scores = jnp.einsum('bhqd,bhkd->bhqk', Q, K) * scale
        u = min(L, max(1, int(np.log(L))))
        top_u = jax.lax.top_k(scores.max(axis=-1), u)[1]
        q_sel = jnp.take_along_axis(Q, top_u[..., None], axis=2)
        attn = jax.nn.softmax(jnp.einsum('bhud,bhkd->bhuk', q_sel, K) * scale, axis=-1)
        ctx = jnp.einsum('bhuk,bhkd->bhud', attn, V)
        bi = jnp.arange(B)[:, None, None]
        hi = jnp.arange(H)[None, :, None]
        padded = jnp.zeros((B, H, L, d_k), dtype=x.dtype).at[bi, hi, top_u].set(ctx)
        out = padded.transpose(0, 2, 1, 3).reshape(B, L, D)
        return out @ wo.T + bo

    def _L0_ffn_ref(x, router_w, gate_w, up_w, down_w):
        import math
        import jax, jax.numpy as jnp
        from jax import lax
        import numpy as np
        E = 16
        K = 2
        CF = 1.25
        B, S, D = x.shape
        xf = x.reshape(-1, D)
        T = B * S
        capacity = max(1, math.ceil(T * K / E * CF))
        Cbuf = K * capacity
        logits = xf @ router_w
        probs = jax.nn.softmax(logits, axis=-1)
        w, idx = lax.top_k(probs, K)
        oh = jax.nn.one_hot(idx, E, dtype=w.dtype)
        rank = jnp.cumsum(oh, axis=0) - oh
        myrank = jnp.sum(rank * oh, axis=-1)
        keep = myrank < capacity
        w = jnp.where(keep, w, 0.0)
        flat_e = idx.reshape(-1)
        flat_w = w.reshape(-1)
        keep_f = keep.reshape(-1)
        tok = jnp.repeat(jnp.arange(T, dtype=jnp.int32), K)
        ohk = jax.nn.one_hot(flat_e, E, dtype=jnp.int32) * keep_f[:, None].astype(jnp.int32)
        pos = jnp.cumsum(ohk, axis=0) - ohk
        slot = jnp.sum(pos * ohk, axis=-1)
        e_idx = jnp.where(keep_f, flat_e, E)
        dispatch = jnp.full((E + 1, Cbuf), T, dtype=jnp.int32).at[e_idx, slot].set(tok)
        wbuf = jnp.zeros((E + 1, Cbuf), dtype=w.dtype).at[e_idx, slot].set(flat_w)
        dispatch = dispatch[:E]
        wbuf = wbuf[:E]
        x_pad = jnp.concatenate([xf, jnp.zeros((1, D), xf.dtype)], axis=0)
        xe = x_pad[dispatch]
        gate = jnp.einsum('ecd,edh->ech', xe, gate_w)
        up = jnp.einsum('ecd,edh->ech', xe, up_w)
        hidden = jax.nn.silu(gate) * up
        out = jnp.einsum('ech,ehd->ecd', hidden, down_w)
        out = out * wbuf[:, :, None]
        combined = jnp.zeros((T + 1, D), dtype=xf.dtype).at[dispatch.reshape(-1)].add(out.reshape(-1, D))
        return combined[:T].reshape(B, S, D)
    x = L0_attn_a_x
    x = x + _L0_attn_a_ref(_layernorm(x, axis=-1), L0_attn_a_Wqk, L0_attn_a_bqk, L0_attn_a_Wv, L0_attn_a_bv, L0_attn_a_Wn, L0_attn_a_bn, L0_attn_a_Wo, L0_attn_a_bo)
    x = x + _L0_ffn_ref(_layernorm(x, axis=-1), L0_ffn_router_w, L0_ffn_gate_w, L0_ffn_up_w, L0_ffn_down_w)
    x = x + _L0_attn_b_ref(_layernorm(x, axis=-1), L0_attn_b_wq, L0_attn_b_bq, L0_attn_b_wk, L0_attn_b_bk, L0_attn_b_wv, L0_attn_b_bv, L0_attn_b_wo, L0_attn_b_bo)
    x = x + _L0_ffn_ref(_layernorm(x, axis=-1), L0_ffn_router_w, L0_ffn_gate_w, L0_ffn_up_w, L0_ffn_down_w)
    return x

_drawn_inputs = setup_inputs


def setup_inputs(seed=0):
    import zlib

    import numpy as np

    out = dict(_drawn_inputs(seed))
    spreads = {'L0_attn_b_bq': (0.0, 0.609),
     'L0_attn_b_bk': (0.0, 0.601),
     'L0_attn_b_bv': (0.0, 0.743),
     'L0_attn_b_bo': (0.0, 0.1)}
    factors = {'L0_attn_a_bn': 8.0,
     'L0_attn_a_bo': 2.681,
     'L0_ffn_router_w': 8.0,
     'L0_ffn_gate_w': 8.0,
     'L0_ffn_up_w': 8.0,
     'L0_ffn_down_w': 8.0}
    for name, (base, spread) in spreads.items():
        noise = np.random.default_rng([zlib.crc32(name.encode()), seed]).standard_normal(out[name].shape)
        drawn = base * np.exp(spread * noise) if base else spread * noise
        out[name] = jnp.asarray(drawn.astype(out[name].dtype))
    for name, factor in factors.items():
        out[name] = (out[name] * factor).astype(out[name].dtype)
    return out
```

```python
from contextlib import ExitStack

import concourse.bass as bass
from concourse import mybir

F32 = mybir.dt.float32
BF16 = mybir.dt.bfloat16
I32 = mybir.dt.int32
U32 = mybir.dt.uint32
ALU = mybir.AluOpType
ACT = mybir.ActivationFunctionType
AX = mybir.AxisListType

P = 128
D = 128
H = 16
DH = D // H
GH = 4
NG = H // GH
E = 16
K = 2
B = 16
SEQ = 512
TB = SEQ // P
T = B * SEQ
NT = T // P
CAP = -(-T * K * 5 // (E * 4))
SPAN = K * CAP + P
GT = 4
TILES = -(-(T * K // P + E - 1) // (2 * GT)) * 2 * GT
DUMMY = E * SPAN
UNSENT = DUMMY + P
ZROW = TILES * P
GROUPS = TILES // GT
TOPU = 6
SLOTU = 8
EPS = 1e-5
SCALE = float(DH) ** -0.5
LNMAX = 20


def build(nc, w, out):
    ctx = ExitStack()
    with ctx:
        def sb(name, shape, dt=F32):
            return ctx.enter_context(nc.sbuf_tensor(name, shape, dt))

        def pb(name):
            return ctx.enter_context(nc.psum_tensor(name, [P, 512], F32))

        def sem(name):
            return ctx.enter_context(nc.semaphore(name))

        disp = nc.dram_tensor("disp", [DUMMY + P, D], F32).ap()
        ybuf = nc.dram_tensor("ybuf", [ZROW + P, D], F32).ap()

        xs = sb("xs", [P, NT, D])
        sent = sb("sent", [P, NT * K])
        expt = sb("expt", [P, NT * K])
        slots = sb("slots", [P, NT * K], I32)
        wts = sb("wts", [P, NT * K])
        gu_w = sb("gu_w", [P, E, 2 * D])
        dn_w = sb("dn_w", [P, E, D])
        rt_w = sb("rt_w", [P, E])
        a_wq = sb("a_wq", [P, D])
        a_wk = sb("a_wk", [P, D])
        a_wkv = sb("a_wkv", [P, 2 * D])
        a_wn = sb("a_wn", [P, E])
        a_wnr = sb("a_wnr", [P, D])
        a_wo = sb("a_wo", [P, D])
        b_wq = sb("b_wq", [P, D])
        b_wk = sb("b_wk", [P, D])
        b_wqv = sb("b_wqv", [P, 2 * D])
        b_wo = sb("b_wo", [P, D])
        cols = sb("cols", [P, 6])
        a_kvb = sb("a_kvb", [P, 2 * D])
        b_qvb = sb("b_qvb", [P, 2 * D])
        a_bo = sb("a_bo", [P, D])
        b_bo = sb("b_bo", [P, D])

        ident = sb("ident", [P, P])
        ones = sb("ones", [P, P])
        zeros = sb("zeros", [P, D])
        onesb = sb("onesb", [P, P], BF16)
        before = sb("before", [P, P], BF16)
        causal = sb("causal", [P, P])
        block8 = sb("block8", [P, P])
        inhead = sb("inhead", [P, GH])
        headrow = sb("headrow", [H, H, SLOTU])
        eiota = sb("eiota", [P, E])
        tokcol = sb("tokcol", [P, TB])
        tokrow = sb("tokrow", [P, SEQ])
        tilecol = sb("tilecol", [P, 2])
        mstep = sb("mstep", [P, LNMAX])
        ebase = sb("ebase", [P, E])
        ksign = sb("ksign", [P, TB, K])
        kbase = sb("kbase", [P, TB, K])

        st = sb("st", [P, TB, 6])
        mv = sb("mv", [P, TB, 2])
        rstd = sb("rstd", [P, TB])
        lnv = sb("lnv", [P, TB])
        lnh = sb("lnh", [P, TB])
        lny = [sb(f"lny{h}", [P, TB]) for h in range(2)]
        lnt = sb("lnt", [P, TB])
        lnu = sb("lnu", [P, TB])
        xna = sb("xna", [P, TB, D])
        xnT = sb("xnT", [P, SEQ])
        xnf = [sb(f"xnf{h}", [P, TB, D]) for h in range(2)]
        xfT = sb("xfT", [P, SEQ])
        lmax = sb("lmax", [P, TB])
        lsub = sb("lsub", [P, TB, E])
        lexp = sb("lexp", [P, TB, E])
        lsum = sb("lsum", [P, TB])
        linv = sb("linv", [P, TB])
        top8 = sb("top8", [P, TB, 8])
        top8i = sb("top8i", [P, TB, 8], U32)
        topf = sb("topf", [P, TB, K])
        topw = sb("topw", [P, TB, K])
        oneh = sb("oneh", [P, TB, K, E], BF16)
        ohnew = sb("ohnew", [P, K * E])
        ohsum = sb("ohsum", [P, K * E], BF16)
        rkoh = sb("rkoh", [P, TB * K, E])
        rank = sb("rank", [P, TB, K])
        keep = sb("keep", [P, TB, K])
        sbase = sb("sbase", [P, TB, K])
        soff = sb("soff", [P, TB, K])
        sval = sb("sval", [P, TB, K])
        sgo = sb("sgo", [P, TB, K])
        sli = [sb(f"sli{h}", [P, TB * K], I32) for h in range(2)]
        slg = [sb(f"slg{h}", [P, TB * K], I32) for h in range(2)]
        yg = [sb(f"yg{h}", [P, TB * K, D]) for h in range(2)]

        cnt = sb("cnt", [P, K, E])
        ntok = sb("ntok", [P, E])
        over = sb("over", [P, E, LNMAX])
        ntile = sb("ntile", [P, E])
        tend = sb("tend", [P, E])
        tstart = sb("tstart", [P, E])
        rowof = sb("rowof", [P, E])
        past = sb("past", [P, 2, E])
        reached = sb("reached", [P, 2, E])
        here = sb("here", [P, 2, E])
        hsum = sb("hsum", [P, 2])
        texp = sb("texp", [P, 2])
        texpc = sb("texpc", [P, 2])
        toff = sb("toff", [P, 2, E])
        toffs = sb("toffs", [P, 2])
        tlin = sb("tlin", [P, 2])
        tlin2 = sb("tlin2", [P, 2])
        trow = sb("trow", [P, 2])
        whose = sb("whose", [P, NT * K, E])
        shift = sb("shift", [P, NT * K])
        kept = sb("kept", [P, NT * K])
        tailf = sb("tailf", [P, E])
        table = sb("table", [1, 2 * TILES], I32)
        tails = sb("tails", [1, E], I32)
        xe = [sb(f"xe{h}", [P, GT, D]) for h in range(2)]
        xeT = [sb(f"xeT{h}", [P, GT, D]) for h in range(2)]
        sg = [sb(f"sg{h}", [P, GT, D]) for h in range(2)]
        hid = [sb(f"hid{h}", [P, GT, D]) for h in range(2)]
        hidT = [sb(f"hidT{h}", [P, GT, D]) for h in range(2)]
        ye = [sb(f"ye{h}", [P, GT, D]) for h in range(2)]

        einv = sb("einv", [P, SEQ])
        qT = sb("qT", [P, SEQ])
        kT = sb("kT", [P, SEQ])
        qm = sb("qm", [P, GH, SEQ])
        tok = sb("tok", [P, TB, 2 * D])
        VSTEP = D + DH
        vm = sb("vm", [P, TB, GH * VSTEP])
        pT = [sb(f"pT{h}", [P, NG, GH, P]) for h in range(2)]
        stm = [sb(f"stm{h}", [P, D]) for h in range(2)]
        ctxT = sb("ctxT", [P, SEQ])
        smax = sb("smax", [P, TB, H])
        mT = sb("mT", [H, SEQ])
        m8 = sb("m8", [H, SLOTU])
        m8i = sb("m8i", [H, SLOTU], U32)
        m8f = sb("m8f", [H, SLOTU])
        idg = sb("idg", [H, H, SLOTU])
        idc = sb("idc", [P, 1])
        selT = sb("selT", [P, TB, P])
        sel = sb("sel", [P, SEQ])
        qsel = sb("qsel", [P, P])
        amax = sb("amax", [P, 1])
        aneg = sb("aneg", [P, 1])
        aexp = sb("aexp", [P, SEQ])
        asum = sb("asum", [P, 1])
        ainv = sb("ainv", [P, 1])
        aexpT = sb("aexpT", [P, SEQ])
        cxm = sb("cxm", [P, P])
        cwo = sb("cwo", [P, D])

        bank = [pb(f"bank{i}") for i in range(8)]

        names = ("w_in w_in2 consts0 consts1 consts2 consts3 ms0 ms1 wnr x_in0 x_in1 stats moments rs xn_ready tp_done xT_ready bias_added "
                 "x1_ready logits_done lmax_done lsub_done lexp_done lsum_done linv_done top_done topi_done topf_done oneh_done "
                 "rank_done rkoh_done rk_done ohnew_done ohsum_done keep_done sbase_done soff_done sval_done sgo_done slots_ready "
                 "w_ready sent0 sent1 counts_done tb table_done tables tails_in zeroed stored_all "
                 "xe_in0 xe_in1 xe_tp xeT_ready gu_done silu_done hid_done hid_tp hidT_ready y_done y_ready y_out0 y_out1 "
                 "slg_ready got0 got1 comb0 combined "
                 "proj_done einv_ready qT_ready kT_ready qm_ready tok_ready vm_ready sc_done pT_ready state_done stm_ready ctx_done ctxT_ready o_done "
                 "bproj_done bqT_ready bqm_ready btok_ready bsc_done bmax_done mT_done mTs_done m8_done m8i_done m8f_done idg_done "
                 "idx_done idc_done sel_done qsel_done qsel_ready att_done amax_done aneg_done aexp_done aeT_done aeT_ready cx_done cx_ready "
                 "cw_done ainv_done cw_ready bo_done x_out settled xnf_free fetched")
        s = {n: sem(n) for n in names.split()}

        block = ctx.enter_context(nc.Block())

        def tiles_of(b):
            return bass.ds(b * TB, TB)

        x_b = w["x"].rearrange("b (t p) d -> b p t d", p=P)
        out_b = out.rearrange("b (t p) d -> b p t d", p=P)
        WLOADS = 20

        def settle(eng):
            eng.sem_inc(s["settled"], 1)

        AHEAD = 16

        @block.sync
        def _(sp):
            for h in range(2):
                sp.sem_inc(s[f"y_out{h}"], AHEAD)
            for dst, src in ((a_wq[:, :], w["a_Wqk"][:, 0:D]), (a_wk[:, :], w["a_Wqk"][:, D:2 * D]),
                             (a_wkv[:, 0:D], w["a_Wqk"][:, D:2 * D]), (a_wkv[:, D:2 * D], w["a_Wv"]),
                             (a_wn[:, :], w["a_Wn"]), (a_wo[:, :], w["a_Wo"]),
                             (cols[:, 0:1], w["a_bqk"][0:D].rearrange("(p a) -> p a", a=1)),
                             (cols[:, 1:2], w["a_bqk"][D:2 * D].rearrange("(p a) -> p a", a=1)),
                             (cols[:, 5:6], w["a_bnr"].rearrange("(p a) -> p a", a=1)),
                             (a_kvb[:, 0:D], w["a_bqk"][D:2 * D].rearrange("(a n) -> a n", a=1).to_broadcast([P, D])),
                             (a_kvb[:, D:2 * D], w["a_bv"].rearrange("(a n) -> a n", a=1).to_broadcast([P, D])),
                             (a_bo[:, :], w["a_bo"].rearrange("(a n) -> a n", a=1).to_broadcast([P, D])),
                             (rt_w[:, :], w["f_router"])):
                sp.dma_start(dst, src).then_inc(s["w_in"], 16)
            for h in range(2):
                sp.dma_start(xs[:, tiles_of(h), :], x_b[h]).then_inc(s[f"x_in{h}"], 16)
            with sp.Fori(1, B // 2) as i:
                for h in range(2):
                    sp.wait_ge(s[f"x_in{h}"], i * 16)
                    sp.dma_start(xs[:, tiles_of(2 * i + h), :], x_b[2 * i + h]).then_inc(s[f"x_in{h}"], 16)
            for dst, src in ((gu_w[:, :, 0:D], w["f_gate"].rearrange("e d h -> d e h")),
                             (gu_w[:, :, D:2 * D], w["f_up"].rearrange("e d h -> d e h")),
                             (dn_w[:, :, :], w["f_down"].rearrange("e d h -> d e h")),
                             (b_wq[:, :], w["b_wqT"]), (b_wk[:, :], w["b_wkT"]),
                             (b_wqv[:, 0:D], w["b_wqT"]), (b_wqv[:, D:2 * D], w["b_wvT"]), (b_wo[:, :], w["b_woT"]),
                             (cols[:, 3:4], w["b_bq"].rearrange("(p a) -> p a", a=1)),
                             (cols[:, 4:5], w["b_bk"].rearrange("(p a) -> p a", a=1)),
                             (b_qvb[:, 0:D], w["b_bq"].rearrange("(a n) -> a n", a=1).to_broadcast([P, D])),
                             (b_qvb[:, D:2 * D], w["b_bv"].rearrange("(a n) -> a n", a=1).to_broadcast([P, D])),
                             (b_bo[:, :], w["b_bo"].rearrange("(a n) -> a n", a=1).to_broadcast([P, D]))):
                sp.dma_start(dst, src).then_inc(s["w_in2"], 16)
            sp.wait_ge(s["consts1"], 1)
            sp.dma_start(disp[DUMMY:DUMMY + P, :], zeros[:, :]).then_inc(s["zeroed"], 16)
            sp.dma_start(ybuf[ZROW:ZROW + P, :], zeros[:, :]).then_inc(s["zeroed"], 16)

            def experts(layer):
                sp.wait_ge(s["tables"], 2 * (layer + 1))
                for e in range(E):
                    row = sp.value_load(tails[0:1, e:e + 1], min_val=0, max_val=DUMMY - P)
                    sp.dma_start(disp[bass.ds(row, P), :], zeros[:, :]).then_inc(s["zeroed"], 16)
                sp.wait_ge(s["zeroed"], 16 * (2 + E * (layer + 1)))
                for h in range(2):
                    sp.wait_ge(s[f"sent{h}"], 16 * TB * K * (B // 2) * (layer + 1))

                def row_in(g, j):
                    return sp.value_load(table[0:1, bass.ds(g * GT + j, 1)], min_val=0, max_val=DUMMY)


                def load(g, h):
                    for j in range(GT):
                        sp.dma_start(xe[h][:, j, :], disp[bass.ds(row_in(g, j), P), :]).then_inc(s[f"xe_in{h}"], 16)

                def store(g, h):
                    sp.wait_ge(s["y_ready"], g + 2 + layer * GROUPS)
                    sp.dma_start(ybuf[bass.ds(g * (GT * P), GT * P), :].rearrange("(j p) d -> p j d", p=P),
                                 ye[h][:, :, :]).then_inc(s[f"y_out{h}"], 16)

                def reload(g, h):
                    sp.wait_ge(s["xe_tp"], g + 1 + layer * GROUPS)
                    load(g + 2, h)

                load(0, 0)
                load(1, 1)
                reload(0, 0)
                reload(1, 1)
                store(0, 0)
                with sp.Fori(1, GROUPS // 2 - 1) as i:
                    for h in range(2):
                        reload(2 * i + h, h)
                        store(2 * i + h - 1, 1 - h)
                store(GROUPS - 3, 1)
                store(GROUPS - 2, 0)
                store(GROUPS - 1, 1)
                for h in range(2):
                    sp.wait_ge(s[f"y_out{h}"], AHEAD + 16 * (GROUPS // 2) * (layer + 1))
                sp.sem_inc(s["stored_all"], 1)

            experts(0)
            experts(1)
            with sp.Fori(0, B) as i:
                sp.wait_ge(s["combined"], i + 1 + B)
                sp.dma_start(out_b[i], xs[:, tiles_of(i), :]).then_inc(s["x_out"], 16)
            sp.wait_ge(s["x_out"], 16 * B)

        @block.gpsimd
        def _(pool):
            pool.sem_inc(s["xnf_free"], 2)
            pool.memset(ident[:, :], 0.0)
            pool.memset(ones[:, :], 1.0)
            pool.memset(onesb[:, :], 1.0)
            pool.memset(zeros[:, :], 0.0).then_inc(s["consts1"], 1)
            pool.memset(block8[:, :], 1.0)
            pool.memset(causal[:, :], 1.0)
            pool.memset(before[:, :], 1.0)
            pool.memset(headrow[:, :, :], 0.0)
            pool.memset(ohsum[:, :], 0.0)
            pool.memset(vm[:, :, :], 0.0)
            pool.memset(m8f[:, :], -1.0)
            for k in range(K):
                pool.memset(ksign[:, :, k], 2.0 * k - 1.0)
                pool.memset(kbase[:, :, k], float(CAP - 1 + k)).then_inc(s["ms0"], 1)
            pool.wait_ge(s["ms0"], K)
            pool.affine_select(out=ident[:, :], in_=ident[:, :], compare_op=ALU.not_equal, fill=1.0, base=0,
                               pattern=[[-1, P]], channel_multiplier=1)
            pool.affine_select(out=causal[:, :], in_=causal[:, :], compare_op=ALU.is_ge, fill=0.0, base=0,
                               pattern=[[1, P]], channel_multiplier=-1)
            pool.affine_select(out=before[:, :], in_=before[:, :], compare_op=ALU.is_ge, fill=0.0, base=-1,
                               pattern=[[1, P]], channel_multiplier=-1)
            pool.affine_select(out=headrow[:, :, :], in_=headrow[:, :, :], compare_op=ALU.not_equal, fill=1.0, base=0,
                               pattern=[[-1, H], [0, SLOTU]], channel_multiplier=1)
            bv = block8[:, :].rearrange("p (h d) -> p h d", d=DH)
            pool.affine_select(out=bv, in_=bv, compare_op=ALU.is_ge, fill=0.0, base=0,
                               pattern=[[-DH, H], [0, DH]], channel_multiplier=1).then_inc(s["ms1"], 1)
            pool.wait_ge(s["ms1"], 1)
            pool.affine_select(out=bv, in_=bv, compare_op=ALU.is_ge, fill=0.0, base=DH - 1,
                               pattern=[[DH, H], [0, DH]], channel_multiplier=-1)

            def iota(t, base, pattern, cm):
                return pool.iota(t, base=base, pattern=pattern, channel_multiplier=cm,
                                 allow_small_or_imprecise_dtypes=True)
            iota(eiota[:, :], 0, [[1, E]], 0)
            iota(tokcol[:, :], 0, [[P, TB]], 1)
            iota(tokrow[:, :], 0, [[1, SEQ]], 0)
            iota(tilecol[:, :], 0, [[P, 2]], 1)
            iota(mstep[:, :], 0, [[P, LNMAX]], 0)
            iota(ebase[:, :], CAP, [[SPAN, E]], 0).then_inc(s["consts2"], 1)

            def send(g, i, h):
                pool.wait_ge(s["slots_ready"], g + 1)
                settle(pool)
                for j in range(TB):
                    for k in range(K):
                        pool.indirect_dma_start(
                            out=disp, out_offset=bass.IndirectOffsetOnAxis(ap=sli[h][:, K * j + k:K * j + k + 1], axis=0),
                            in_=xnf[h][:, j, :], in_offset=None, bounds_check=DUMMY - 1, oob_is_err=False,
                        ).then_inc(s[f"sent{h}"], 16)
                pool.wait_ge(s[f"sent{h}"], (i + 1) * 16 * TB * K)
                pool.sem_inc(s["xnf_free"], 1)

            def fetch(g, i, h):
                pool.wait_ge(s["slg_ready"], g + 1)
                settle(pool)
                for j in range(TB * K):
                    pool.indirect_dma_start(
                        out=yg[h][:, j, :], out_offset=None, in_=ybuf,
                        in_offset=bass.IndirectOffsetOnAxis(ap=slg[h][:, j:j + 1], axis=0),
                    ).then_inc(s[f"got{h}"], 16)
                pool.wait_ge(s[f"got{h}"], (i + 1) * 16 * TB * K)
                pool.sem_inc(s["fetched"], 1)

            def add_bias(b, g, row):
                pool.wait_ge(s["xn_ready"], 2 * g + 1)
                settle(pool)
                xb = xs[:, tiles_of(b), :]
                pool.tensor_tensor(xb, xb, row[:, :].unsqueeze(1).to_broadcast([P, TB, D]), ALU.add).then_inc(s["bias_added"], 1)

            pool.wait_ge(s["w_in"], 16 * 13)
            with pool.Fori(0, B // 2) as i:
                for h in range(2):
                    b = 2 * i + h
                    add_bias(b, b, a_bo)
                    pool.wait_ge(s["tok_ready"], b + 1)
                    settle(pool)
                    for j in range(TB):
                        dst = vm[:, j, :].rearrange("p (j x) -> p j x", x=VSTEP)[:, :, 0:D].rearrange(
                            "p j (g y) -> p j g y", y=GH * DH)[:, :, :, 0:DH]
                        src = tok[:, j, D:2 * D].rearrange("p (g j d) -> p j g d", g=NG, j=GH)
                        last = pool.tensor_copy(dst, src)
                    last.then_inc(s["vm_ready"], 1)
                    send(b, i, h)
            pool.wait_ge(s["w_in2"], 16 * 13)
            pool.wait_ge(s["stored_all"], 1)
            fetch(0, 0, 0)
            with pool.Fori(0, B // 2 - 1) as i:
                for h in range(2):
                    b = 2 * i + h
                    fetch(b + 1, i + h, 1 - h)
                    add_bias(b, b + B, b_bo)
                    send(b + B, i + B // 2, h)
            fetch(B - 1, B // 2 - 1, 1)
            for h in range(2):
                add_bias(B - 2 + h, 2 * B - 2 + h, b_bo)
                send(2 * B - 2 + h, B - 1, h)
            pool.wait_ge(s["stored_all"], 2)
            with pool.Fori(0, B // 2) as i:
                for h in range(2):
                    b = 2 * i + h
                    fetch(b + B, i + B // 2, h)

        @block.scalar
        def _(act):
            act.sem_inc(s["hidT_ready"], 1)
            act.wait_ge(s["w_in"], 16 * 13)
            act.activation(a_wnr[:, :].rearrange("p (h d) -> p h d", d=DH),
                           a_wn[:, :].unsqueeze(2).to_broadcast([P, H, DH]), ACT.Copy).then_inc(s["wnr"], 1)
            act.activation(cols[:, 2:3], cols[:, 5:6], ACT.Copy, scale=-1.0).then_inc(s["wnr"], 1)
            act.wait_ge(s["wnr"], 2)

            def turned(n, dst):
                act.wait_ge(s["tp_done"], n + 1)
                act.activation(dst[:, :], bank[0][:, :], ACT.Copy).then_inc(s["xT_ready"], 1)

            def route_exp(g):
                act.wait_ge(s["lsub_done"], g + 1)
                act.activation(lexp[:, :, :], lsub[:, :, :], ACT.Exp).then_inc(s["lexp_done"], 1)

            act.wait_ge(s["consts3"], 1)
            with act.Fori(0, B) as b:
                turned(2 * b, xnT)
                act.wait_ge(s["proj_done"], b + 1)
                act.activation(einv[:, :], bank[5][:, :], ACT.Exp, bias=cols[:, 2:3], scale=-1.0).then_inc(s["einv_ready"], 1)
                act.activation(kT[:, :], bank[6][:, :], ACT.Identity, bias=cols[:, 1:2]).then_inc(s["kT_ready"], 1)
                act.wait_ge(s["qT_ready"], b + 1)
                for j in range(GH):
                    last = act.activation(qm[:, j, :], qT[:, :], ACT.Copy, scale=inhead[:, j:j + 1])
                last.then_inc(s["qm_ready"], 1)
                act.wait_ge(s["ctx_done"], b + 1)
                act.activation(ctxT[:, :], bank[1][:, :], ACT.Copy).then_inc(s["ctxT_ready"], 1)
                turned(2 * b + 1, xfT)
                route_exp(b)

            def experts(layer):
                base = layer * GROUPS

                def xT(g, h):
                    act.wait_ge(s["xe_tp"], g + 1 + base)
                    act.activation(xeT[h][:, :, :].rearrange("p j d -> p (j d)"), bank[0][:, :], ACT.Copy).then_inc(s["xeT_ready"], 1)

                def silu(g, h):
                    act.wait_ge(s["gu_done"], g + 1 + base)
                    for q in range(2):
                        src = bank[3 + 2 * h + q][:, :].rearrange("p (j n) -> p j n", j=2)[:, :, 0:D]
                        last = act.activation(sg[h][:, 2 * q:2 * q + 2, :], src, ACT.Silu)
                    last.then_inc(s["silu_done"], 1)

                def hT(g, h):
                    act.wait_ge(s["hid_tp"], g + 1 + base)
                    act.activation(hidT[h][:, :, :].rearrange("p j d -> p (j d)"), bank[1][:, :], ACT.Copy).then_inc(s["hidT_ready"], 1)

                xT(0, 0)
                silu(0, 0)
                xT(1, 1)
                silu(1, 1)
                xT(2, 0)
                hT(0, 0)
                with act.Fori(1, GROUPS // 2 - 1) as i:
                    for h in range(2):
                        silu(2 * i + h, h)
                        xT(2 * i + h + 1, 1 - h)
                        hT(2 * i + h - 1, 1 - h)
                silu(GROUPS - 2, 0)
                xT(GROUPS - 1, 1)
                hT(GROUPS - 3, 1)
                silu(GROUPS - 1, 1)
                hT(GROUPS - 2, 0)
                hT(GROUPS - 1, 1)

            experts(0)
            act.wait_ge(s["w_in2"], 16 * 13)
            with act.Fori(0, B) as b:
                turned(2 * (b + B), xnT)
                act.wait_ge(s["bproj_done"], b + 1)
                act.activation(qT[:, :], bank[2][:, :], ACT.Identity, bias=cols[:, 3:4]).then_inc(s["bqT_ready"], 1)
                act.activation(kT[:, :], bank[3][:, :], ACT.Identity, bias=cols[:, 4:5])
                act.wait_ge(s["bqT_ready"], b + 1)
                for j in range(GH):
                    last = act.activation(qm[:, j, :], qT[:, :], ACT.Copy, scale=inhead[:, j:j + 1])
                last.then_inc(s["bqm_ready"], 1)
                act.wait_ge(s["aneg_done"], b + 1)
                act.activation(aexp[:, :], bank[1][:, :], ACT.Exp, bias=aneg[:, 0:1], scale=SCALE,
                               accum_out=asum[:, 0:1]).then_inc(s["aexp_done"], 1)
                act.wait_ge(s["aeT_done"], b + 1)
                act.activation(aexpT[:, :], bank[0][:, :], ACT.Copy).then_inc(s["aeT_ready"], 1)
                turned(2 * (b + B) + 1, xfT)
                route_exp(b + B)
            experts(1)

        @block.vector
        def _(dve):
            dve.sem_inc(s["y_ready"], 1)
            dve.wait_ge(s["consts2"], 1)
            dve.tensor_reduce(inhead[:, :], block8[:, :].rearrange("p (g j d) -> p j g d", g=NG, j=GH)[:, :, :, 0],
                              AX.X, ALU.add).then_inc(s["consts3"], 1)

            def norm(b, n, dst):
                settle(dve)
                for j in range(TB):
                    last = dve.bn_stats(st[:, j, :], xs[:, b * TB + j, :])
                last.then_inc(s["stats"], 1)
                dve.wait_ge(s["stats"], n + 1)
                settle(dve)
                for j in range(TB):
                    last = dve.bn_aggr(mv[:, j, :], st[:, j, :])
                last.then_inc(s["moments"], 1)
                dve.wait_ge(s["moments"], n + 1)
                dve.tensor_scalar(lnv[:, :], mv[:, :, 1], EPS, None, ALU.add).then_inc(s["rs"], 1)
                dve.tensor_scalar(lnh[:, :], mv[:, :, 1], EPS, -0.5, ALU.add, ALU.mult)
                dve.wait_ge(s["rs"], n * 11 + 1)
                dve.tensor_scalar(lny[0][:, :].bitcast(I32), lnv[:, :].bitcast(I32), -0.5, float(0x5f3759df),
                                  ALU.mult, ALU.add).then_inc(s["rs"], 1)
                for r in range(3):
                    y, z = lny[r % 2], (lny[1 - r % 2] if r < 2 else rstd)
                    dve.wait_ge(s["rs"], n * 11 + 2 + 3 * r)
                    dve.tensor_tensor(lnt[:, :], y[:, :], y[:, :], ALU.mult).then_inc(s["rs"], 1)
                    dve.wait_ge(s["rs"], n * 11 + 3 + 3 * r)
                    dve.tensor_tensor(lnu[:, :], lnt[:, :], lnh[:, :], ALU.mult).then_inc(s["rs"], 1)
                    dve.wait_ge(s["rs"], n * 11 + 4 + 3 * r)
                    dve.scalar_tensor_tensor(out=z[:, :], in0=lnu[:, :], scalar=1.5, in1=y[:, :],
                                             op0=ALU.add, op1=ALU.mult).then_inc(s["rs"], 1)
                dve.wait_ge(s["rs"], n * 11 + 11)
                for j in range(TB):
                    last = dve.tensor_scalar(dst[:, j, :], xs[:, b * TB + j, :], mv[:, j, 0:1], rstd[:, j:j + 1],
                                             ALU.subtract, ALU.mult)
                last.then_inc(s["xn_ready"], 1)

            def route(b, g, h):
                lg = bank[2][:, 0:TB * E].rearrange("p (t e) -> p t e", e=E)
                dve.wait_ge(s["logits_done"], g + 1)
                dve.tensor_reduce(lmax[:, :], lg, AX.X, ALU.max).then_inc(s["lmax_done"], 1)
                dve.wait_ge(s["lmax_done"], g + 1)
                dve.tensor_tensor(lsub[:, :, :], lg, lmax[:, :].unsqueeze(2).to_broadcast([P, TB, E]),
                                  ALU.subtract).then_inc(s["lsub_done"], 1)
                dve.wait_ge(s["lexp_done"], g + 1)
                settle(dve)
                for j in range(TB):
                    last = dve.max(top8[:, j, :], lexp[:, j, :])
                last.then_inc(s["top_done"], 1)
                dve.tensor_reduce(lsum[:, :], lexp[:, :, :], AX.X, ALU.add).then_inc(s["lsum_done"], 1)
                dve.wait_ge(s["top_done"], g + 1)
                settle(dve)
                for j in range(TB):
                    last = dve.max_index(top8i[:, j, :], top8[:, j, :], lexp[:, j, :])
                last.then_inc(s["topi_done"], 1)
                dve.wait_ge(s["lsum_done"], g + 1)
                dve.reciprocal(linv[:, :], lsum[:, :]).then_inc(s["linv_done"], 1)
                dve.wait_ge(s["topi_done"], g + 1)
                dve.tensor_copy(topf[:, :, :], top8i[:, :, 0:K]).then_inc(s["topf_done"], 1)
                dve.wait_ge(s["linv_done"], g + 1)
                dve.tensor_tensor(topw[:, :, :], top8[:, :, 0:K], linv[:, :].unsqueeze(2).to_broadcast([P, TB, K]), ALU.mult)
                dve.wait_ge(s["topf_done"], g + 1)
                for k in range(K):
                    last = dve.tensor_tensor(oneh[:, :, k, :], eiota[:, :].unsqueeze(1).to_broadcast([P, TB, E]),
                                             topf[:, :, k:k + 1].to_broadcast([P, TB, E]), ALU.is_equal)
                last.then_inc(s["oneh_done"], 1)
                dve.wait_ge(s["oneh_done"], g + 1)
                dve.tensor_reduce(ohnew[:, :], oneh[:, :, :, :].rearrange("p t k e -> p (k e) t"), AX.X,
                                  ALU.add).then_inc(s["ohnew_done"], 1)
                dve.tensor_scalar(sbase[:, :, :], topf[:, :, :], float(SPAN), None, ALU.mult).then_inc(s["sbase_done"], 1)
                dve.wait_ge(s["rank_done"], g + 1)
                dve.tensor_tensor(rkoh[:, :, :], bank[2][:, P:2 * P].rearrange("p (t e) -> p t e", e=E),
                                  oneh[:, :, :, :].rearrange("p t k e -> p (t k) e"), ALU.mult).then_inc(s["rkoh_done"], 1)
                dve.wait_ge(s["ohnew_done"], g + 1)
                dve.tensor_tensor(ohsum[:, :], ohsum[:, :], ohnew[:, :], ALU.add).then_inc(s["ohsum_done"], 1)
                dve.wait_ge(s["rkoh_done"], g + 1)
                dve.tensor_reduce(rank[:, :, :].rearrange("p t k -> p (t k)"), rkoh[:, :, :], AX.X, ALU.add).then_inc(s["rk_done"], 1)
                dve.wait_ge(s["rk_done"], g + 1)
                dve.tensor_scalar(keep[:, :, :], rank[:, :, :], float(CAP), None, ALU.is_lt)
                dve.tensor_tensor(soff[:, :, :], rank[:, :, :], ksign[:, :, :], ALU.mult).then_inc(s["soff_done"], 1)
                dve.wait_ge(s["sbase_done"], g + 1)
                dve.wait_ge(s["soff_done"], g + 1)
                dve.scalar_tensor_tensor(out=sval[:, :, :], in0=sbase[:, :, :], scalar=float(-UNSENT), in1=soff[:, :, :],
                                         op0=ALU.add, op1=ALU.add).then_inc(s["sval_done"], 1)
                dve.tensor_tensor(wts[:, bass.ds(b * TB * K, TB * K)].rearrange("p (t k) -> p t k", k=K),
                                  topw[:, :, :], keep[:, :, :], ALU.mult)
                dve.wait_ge(s["sval_done"], g + 1)
                dve.tensor_tensor(sgo[:, :, :], sval[:, :, :], kbase[:, :, :], ALU.add).then_inc(s["sgo_done"], 1)
                dve.wait_ge(s["sgo_done"], g + 1)
                dve.tensor_tensor(soff[:, :, :], sgo[:, :, :], keep[:, :, :], ALU.mult).then_inc(s["keep_done"], 1)
                dve.wait_ge(s["keep_done"], g + 1)
                dve.tensor_scalar(sli[h][:, :].rearrange("p (t k) -> p t k", k=K), soff[:, :, :], float(UNSENT), None,
                                  ALU.add).then_inc(s["slots_ready"], 1)
                dve.tensor_copy(expt[:, bass.ds(b * TB * K, TB * K)].rearrange("p (t k) -> p t k", k=K), topf[:, :, :])
                dve.tensor_scalar(sent[:, bass.ds(b * TB * K, TB * K)].rearrange("p (t k) -> p t k", k=K),
                                  soff[:, :, :], float(UNSENT), None, ALU.add).then_inc(s["w_ready"], 1)

            def norm_ffn(b, g, h):
                dve.wait_ge(s["xnf_free"], g + 1)
                norm(b, 2 * g + 1, xnf[h])

            dve.wait_ge(s["w_in"], 16 * 13)
            with dve.Fori(0, B // 2) as i:
                for h in range(2):
                    b = 2 * i + h
                    dve.wait_ge(s[f"x_in{h}"], 16 * i + 16)
                    norm(b, 2 * b, xna)
                    dve.wait_ge(s["einv_ready"], b + 1)
                    dve.scalar_tensor_tensor(out=qT[:, :], in0=bank[4][:, :], scalar=cols[:, 0:1], in1=einv[:, :],
                                             op0=ALU.add, op1=ALU.mult).then_inc(s["qT_ready"], 1)
                    bias = a_kvb[:, :].unsqueeze(1).to_broadcast([P, 2, 2 * D])
                    dve.tensor_tensor(tok[:, 0:2, :], bank[7][:, :].rearrange("p (t n) -> p t n", t=2), bias, ALU.add)
                    dve.tensor_tensor(tok[:, 2:4, :], bank[3][:, :].rearrange("p (t n) -> p t n", t=2), bias,
                                      ALU.add).then_inc(s["tok_ready"], 1)
                    for c in range(TB):
                        if c:
                            dve.wait_ge(s["state_done"], b * (TB - 1) + c)
                            dve.tensor_tensor(stm[c % 2][:, :], bank[2][:, 0:D], block8[:, :], ALU.mult).then_inc(s["stm_ready"], 1)
                        for g in range(NG):
                            dve.wait_ge(s["sc_done"], (b * TB + c) * NG + g + 1)
                            dve.tensor_tensor(pT[c % 2][:, g, :, :], bank[4 + g][:, :].rearrange("p (j t) -> p j t", j=GH),
                                              causal[:, :].unsqueeze(1).to_broadcast([P, GH, P]),
                                              ALU.mult).then_inc(s["pT_ready"], 1)
                    dve.wait_ge(s["bias_added"], b + 1)
                    dve.wait_ge(s["o_done"], b + 1)
                    xb = xs[:, tiles_of(b), :]
                    dve.tensor_tensor(xb, xb, bank[3][:, :].rearrange("p (t d) -> p t d", t=TB), ALU.add).then_inc(s["x1_ready"], 1)
                    dve.wait_ge(s["x1_ready"], b + 1)
                    norm_ffn(b, b, h)
                    route(b, b, h)

            def tables(layer):
                n = [layer * 17]

                def link(ins):
                    n[0] += 1
                    ins.then_inc(s["tb"], 1)
                    dve.wait_ge(s["tb"], n[0])

                def wide(t):
                    return t[:, :].unsqueeze(1).to_broadcast([P, 2, E])
                tc = tilecol[:, :].unsqueeze(2).to_broadcast([P, 2, E])
                dve.wait_ge(s["counts_done"], layer + 1)
                link(dve.tensor_scalar(cnt[:, :, :], bank[1][:, 0:K * E].rearrange("p (k e) -> p k e", k=K),
                                       float(CAP), None, ALU.min))
                dve.tensor_tensor(tailf[:, :], ebase[:, :], cnt[:, 1, :], ALU.add)
                link(dve.tensor_tensor(ntok[:, :], cnt[:, 0, :], cnt[:, 1, :], ALU.add))
                link(dve.tensor_tensor(over[:, :, :], ntok[:, :].unsqueeze(2).to_broadcast([P, E, LNMAX]),
                                       mstep[:, :].unsqueeze(1).to_broadcast([P, E, LNMAX]), ALU.is_gt))
                link(dve.tensor_reduce(ntile[:, :], over[:, :, :], AX.X, ALU.add))
                link(dve.tensor_tensor_scan(tend[:, :], ones[:, 0:E], ntile[:, :], 0.0, ALU.mult, ALU.add))
                link(dve.tensor_tensor(tstart[:, :], tend[:, :], ntile[:, :], ALU.subtract))
                dve.tensor_tensor(past[:, :, :], tc, wide(tend), ALU.is_ge)
                dve.tensor_tensor(reached[:, :, :], tc, wide(tstart), ALU.is_ge)
                link(dve.scalar_tensor_tensor(out=rowof[:, :], in0=tstart[:, :], scalar=float(-P), in1=ebase[:, :],
                                              op0=ALU.mult, op1=ALU.add))
                dve.tensor_tensor(here[:, :, :], reached[:, :, :], past[:, :, :], ALU.subtract)
                dve.tensor_reduce(texp[:, :], past[:, :, :], AX.X, ALU.add)
                link(dve.tensor_tensor(rowof[:, :], rowof[:, :], cnt[:, 0, :], ALU.subtract))
                dve.tensor_reduce(hsum[:, :], here[:, :, :], AX.X, ALU.add)
                dve.tensor_scalar(texpc[:, :], texp[:, :], float(E - 1), None, ALU.min)
                dve.tensor_scalar(tlin[:, :], tilecol[:, :], float(P), float(-DUMMY), ALU.mult, ALU.add)
                link(dve.tensor_tensor(toff[:, :, :], here[:, :, :], wide(rowof), ALU.mult))
                dve.tensor_reduce(toffs[:, :], toff[:, :, :], AX.X, ALU.add)
                link(dve.tensor_tensor(tlin2[:, :], tlin[:, :], hsum[:, :], ALU.mult))
                link(dve.scalar_tensor_tensor(out=trow[:, :], in0=tlin2[:, :], scalar=float(DUMMY), in1=toffs[:, :],
                                              op0=ALU.add, op1=ALU.add))
                dve.tensor_copy(tails[0:1, :], tailf[0:1, :]).then_inc(s["tables"], 1)
                dve.wait_ge(s["table_done"], layer + 1)
                dve.tensor_copy(table[0:1, :], bank[1][0:1, 0:2 * TILES]).then_inc(s["tables"], 1)
                dve.memset(ohsum[:, :], 0.0)
                dve.wait_ge(s["w_ready"], B * (layer + 1))
                link(dve.tensor_tensor(whose[:, :, :], expt[:, :].unsqueeze(2).to_broadcast([P, NT * K, E]),
                                       eiota[:, :].unsqueeze(1).to_broadcast([P, NT * K, E]), ALU.is_equal))
                link(dve.tensor_tensor(whose[:, :, :], whose[:, :, :], rowof[:, :].unsqueeze(1).to_broadcast([P, NT * K, E]),
                                       ALU.mult))
                dve.tensor_scalar(kept[:, :], sent[:, :], float(DUMMY), None, ALU.is_lt)
                link(dve.tensor_reduce(shift[:, :], whose[:, :, :], AX.X, ALU.add))
                link(dve.scalar_tensor_tensor(out=shift[:, :], in0=sent[:, :], scalar=float(-ZROW), in1=shift[:, :],
                                              op0=ALU.add, op1=ALU.subtract))
                link(dve.tensor_tensor(shift[:, :], shift[:, :], kept[:, :], ALU.mult))
                link(dve.tensor_scalar(slots[:, :], shift[:, :], float(ZROW), None, ALU.add))

            def experts(layer):
                base = layer * GROUPS

                def hidden(g, h):
                    dve.wait_ge(s["silu_done"], g + 1 + base)
                    for q in range(2):
                        up = bank[3 + 2 * h + q][:, :].rearrange("p (j n) -> p j n", j=2)[:, :, D:2 * D]
                        last = dve.tensor_tensor(hid[h][:, 2 * q:2 * q + 2, :], sg[h][:, 2 * q:2 * q + 2, :], up, ALU.mult)
                    last.then_inc(s["hid_done"], 1)

                def y_copy(g, h, i):
                    dve.wait_ge(s["y_done"], g + 1 + base)
                    dve.wait_ge(s[f"y_out{h}"], AHEAD + (i + layer * (GROUPS // 2)) * 16)
                    dve.tensor_copy(ye[h][:, :, :].rearrange("p j d -> p (j d)"), bank[7][:, :]).then_inc(s["y_ready"], 1)

                hidden(0, 0)
                hidden(1, 1)
                with dve.Fori(1, GROUPS // 2) as i:
                    for h in range(2):
                        hidden(2 * i + h, h)
                        y_copy(2 * i + h - 2, h, i - 1)
                y_copy(GROUPS - 2, 0, GROUPS // 2 - 1)
                y_copy(GROUPS - 1, 1, GROUPS // 2 - 1)

            def indices(b, h):
                dve.tensor_copy(slg[h][:, :], slots[:, bass.ds(b * TB * K, TB * K)]).then_inc(s["slg_ready"], 1)

            def combine(b, h, g):
                dve.wait_ge(s["fetched"], g + 1)
                for k in range(K):
                    if k:
                        dve.wait_ge(s["comb0"], g + 1)
                    for j in range(TB):
                        xb = xs[:, b * TB + j, :]
                        last = dve.scalar_tensor_tensor(out=xb, in0=yg[h][:, K * j + k, :],
                                                        scalar=wts[:, bass.ds((b * TB + j) * K + k, 1)], in1=xb,
                                                        op0=ALU.mult, op1=ALU.add)
                    last.then_inc(s["comb0"] if k == 0 else s["combined"], 1)
                dve.wait_ge(s["combined"], g + 1)

            tables(0)
            experts(0)

            dve.wait_ge(s["w_ready"], B)
            dve.wait_ge(s["w_in2"], 16 * 13)
            indices(0, 0)
            dve.sem_inc(s["bmax_done"], 2)

            def attention_b(b, i, h, last_batch):
                g = b + B
                if not last_batch:
                    indices(b + 1, 1 - h)
                combine(b, h, b)
                norm(b, 2 * g, xna)
                dve.wait_ge(s["bproj_done"], b + 1)
                bias = b_qvb[:, :].unsqueeze(1).to_broadcast([P, 2, 2 * D])
                for q in range(2):
                    last = dve.tensor_tensor(tok[:, 2 * q:2 * q + 2, :], bank[4 + q][:, :].rearrange("p (t n) -> p t n", t=2),
                                             bias, ALU.add)
                last.then_inc(s["btok_ready"], 1)
                sv = smax[:, :, :].rearrange("p t (g j) -> p t g j", j=GH)
                for n in range(TB * GH * 2):
                    t, j, gp = n // (2 * GH), n // 2 % GH, n % 2
                    dve.wait_ge(s["bsc_done"], b * (TB * GH * 2) + n + 1)
                    r = 2 + 2 * (n % 3)
                    for q in range(2):
                        last = dve.tensor_reduce(sv[:, t, 2 * gp + q, j:j + 1], bank[r + q][:, :], AX.X, ALU.max)
                    last.then_inc(s["bmax_done"], 1)
                dve.wait_ge(s["mT_done"], b + 1)
                dve.tensor_scalar(mT[:, :], bank[0][0:H, :], SCALE, None, ALU.mult).then_inc(s["mTs_done"], 1)
                dve.wait_ge(s["mTs_done"], b + 1)
                settle(dve)
                dve.max(m8[:, :], mT[:, :]).then_inc(s["m8_done"], 1)
                dve.wait_ge(s["m8_done"], b + 1)
                settle(dve)
                dve.max_index(m8i[:, :], m8[:, :], mT[:, :]).then_inc(s["m8i_done"], 1)
                dve.wait_ge(s["m8i_done"], b + 1)
                dve.tensor_copy(m8f[:, 0:TOPU], m8i[:, 0:TOPU]).then_inc(s["m8f_done"], 1)
                dve.wait_ge(s["m8f_done"], b + 1)
                dve.tensor_tensor(idg[:, :, :], headrow[:, :, :], m8f[:, :].unsqueeze(1).to_broadcast([H, H, SLOTU]),
                                  ALU.mult).then_inc(s["idg_done"], 1)
                dve.wait_ge(s["idx_done"], b + 1)
                dve.tensor_copy(idc[:, :], bank[1][:, P:P + 1]).then_inc(s["idc_done"], 1)
                dve.tensor_tensor(selT[:, :, :], bank[1][:, 0:P].unsqueeze(1).to_broadcast([P, TB, P]),
                                  tokcol[:, :].unsqueeze(2).to_broadcast([P, TB, P]), ALU.is_equal)
                dve.wait_ge(s["idc_done"], b + 1)
                dve.tensor_scalar(sel[:, :], tokrow[:, :], idc[:, 0:1], None, ALU.is_equal).then_inc(s["sel_done"], 1)
                dve.wait_ge(s["qsel_done"], b + 1)
                dve.tensor_tensor(qsel[:, :], bank[0][:, 0:P], block8[:, :], ALU.mult).then_inc(s["qsel_ready"], 1)
                dve.wait_ge(s["att_done"], b + 1)
                dve.tensor_reduce(amax[:, :], bank[1][:, :], AX.X, ALU.max).then_inc(s["amax_done"], 1)
                dve.wait_ge(s["amax_done"], b + 1)
                dve.tensor_scalar(aneg[:, :], amax[:, :], -SCALE, None, ALU.mult).then_inc(s["aneg_done"], 1)
                dve.wait_ge(s["aexp_done"], b + 1)
                dve.reciprocal(ainv[:, :], asum[:, :]).then_inc(s["ainv_done"], 1)
                dve.wait_ge(s["cx_done"], b + 1)
                dve.tensor_tensor(cxm[:, :], bank[1][:, 0:P], block8[:, :], ALU.mult).then_inc(s["cx_ready"], 1)
                dve.wait_ge(s["cw_done"], b + 1)
                dve.wait_ge(s["ainv_done"], b + 1)
                dve.tensor_scalar(cwo[:, :], bank[0][:, 0:D], ainv[:, 0:1], None, ALU.mult).then_inc(s["cw_ready"], 1)
                dve.wait_ge(s["bias_added"], g + 1)
                dve.wait_ge(s["bo_done"], b + 1)
                xb = xs[:, tiles_of(b), :]
                dve.tensor_tensor(xb, xb, bank[1][:, :].rearrange("p (t d) -> p t d", t=TB), ALU.add).then_inc(s["x1_ready"], 1)
                dve.wait_ge(s["x1_ready"], g + 1)
                norm_ffn(b, g, h)
                route(b, g, h)

            with dve.Fori(0, B // 2 - 1) as i:
                for h in range(2):
                    attention_b(2 * i + h, i, h, False)
            attention_b(B - 2, B // 2 - 1, 0, False)
            attention_b(B - 1, B // 2 - 1, 1, True)
            tables(1)
            experts(1)
            dve.wait_ge(s["w_ready"], 2 * B)
            indices(0, 0)
            with dve.Fori(0, B // 2 - 1) as i:
                for h in range(2):
                    indices(2 * i + h + 1, 1 - h)
                    combine(2 * i + h, h, 2 * i + h + B)
            indices(B - 1, 1)
            combine(B - 2, 0, 2 * B - 2)
            combine(B - 1, 1, 2 * B - 1)

        @block.tensor
        def _(pe):
            def turn(n, src):
                pe.wait_ge(s["xn_ready"], n + 1)
                for j in range(TB):
                    last = pe.transpose(bank[0][:, j * P:(j + 1) * P], src[:, j, :], ident[:, :])
                last.then_inc(s["tp_done"], 1)
                pe.wait_ge(s["xT_ready"], n + 1)

            def route(g, h):
                turn(2 * g + 1, xnf[h])
                for j in range(TB):
                    last = pe.matmul(bank[2][:, j * E:(j + 1) * E], xfT[:, j * P:(j + 1) * P], rt_w[:, :], start=True, stop=True)
                last.then_inc(s["logits_done"], 1)
                pe.wait_ge(s["oneh_done"], g + 1)
                KE = K * E
                rk = bank[2][:, P:2 * P]
                pe.matmul(rk.rearrange("p (t n) -> p t n", n=KE), onesb[:, :],
                          ohsum[:, :].unsqueeze(1).to_broadcast([P, TB, KE]), start=True, stop=False)
                for j in range(TB - 1):
                    pe.matmul(bank[2][:, P + (j + 1) * KE:2 * P].rearrange("p (t n) -> p t n", n=KE), onesb[:, :],
                              oneh[:, j, :, :].rearrange("p k e -> p (k e)").unsqueeze(1).to_broadcast([P, TB - 1 - j, KE]),
                              start=False, stop=False)
                pe.matmul(rk, before[:, :], oneh[:, :, :, :].rearrange("p t k e -> p (t k e)"), start=False,
                          stop=True).then_inc(s["rank_done"], 1)

            pe.wait_ge(s["consts3"], 1)
            pe.wait_ge(s["wnr"], 1)
            pe.wait_ge(s["w_in"], 16 * 13)
            with pe.Fori(0, B // 2) as i:
                for h in range(2):
                    b = 2 * i + h
                    turn(2 * b, xna)
                    pe.matmul(bank[5][:, :], a_wnr[:, :], xnT[:, :], start=True, stop=True)
                    pe.matmul(bank[4][:, :], a_wq[:, :], xnT[:, :], start=True, stop=True)
                    pe.matmul(bank[6][:, :], a_wk[:, :], xnT[:, :], start=True, stop=True)
                    for j in range(TB):
                        last = pe.matmul(bank[(7, 3)[j // 2]][:, j % 2 * 2 * D:(j % 2 + 1) * 2 * D], xnT[:, j * P:(j + 1) * P],
                                         a_wkv[:, :], start=True, stop=True)
                    last.then_inc(s["proj_done"], 1)
                    pe.wait_ge(s["kT_ready"], b + 1)
                    pe.wait_ge(s["qm_ready"], b + 1)
                    pe.wait_ge(s["tok_ready"], b + 1)

                    def scores(c):
                        for g in range(NG):
                            rows = slice(32 * g, 32 * g + 32)
                            if c:
                                pe.wait_ge(s["pT_ready"], (b * TB + c - 1) * NG + g + 1)
                            pe.matmul(bank[4 + g][:, :].rearrange("p (j t) -> p j t", j=GH), kT[rows, c * P:(c + 1) * P],
                                      qm[rows, :, c * P:(c + 1) * P], start=True, stop=True).then_inc(s["sc_done"], 1)

                    scores(0)
                    for c in range(TB):
                        ct = bank[1][:, c * P:(c + 1) * P]
                        if c + 1 < TB:
                            if c:
                                pe.wait_ge(s["stm_ready"], b * (TB - 1) + c)
                            pe.matmul(bank[2][:, 0:D], tok[:, c, 0:D], tok[:, c, D:2 * D], start=(c == 0), stop=True,
                                      skip_group_check=True).then_inc(s["state_done"], 1)
                            scores(c + 1)
                        if c:
                            pe.wait_ge(s["stm_ready"], b * (TB - 1) + c)
                            pe.matmul(ct, stm[c % 2][:, :], qT[:, c * P:(c + 1) * P], start=True, stop=False, skip_group_check=True)
                        pe.wait_ge(s["pT_ready"], (b * TB + c) * NG + NG)
                        pe.wait_ge(s["vm_ready"], b + 1)
                        for j in range(GH):
                            for g in range(NG):
                                last = pe.matmul(bank[1][32 * g:32 * g + 32, c * P:(c + 1) * P],
                                                 vm[:, c, j * P + 32 * g:j * P + 32 * g + 32], pT[c % 2][:, g, j, :],
                                                 start=(c == 0 and j == 0), stop=(j == GH - 1), skip_group_check=True)
                    last.then_inc(s["ctx_done"], 1)
                    pe.wait_ge(s["ctxT_ready"], b + 1)
                    for j in range(TB):
                        last = pe.matmul(bank[3][:, j * D:(j + 1) * D], ctxT[:, j * P:(j + 1) * P], a_wo[:, :], start=True, stop=True)
                    last.then_inc(s["o_done"], 1)
                    route(b, h)

            def tables(layer):
                pe.wait_ge(s["ohsum_done"], B * (layer + 1))
                pe.matmul(bank[1][:, 0:K * E], onesb[:, :], ohsum[:, :], start=True, stop=True).then_inc(s["counts_done"], 1)
                pe.wait_ge(s["tb"], 17 * layer + 11)
                for n, src in enumerate((trow, texpc)):
                    for c, width in ((0, P), (1, TILES - P)):
                        at = n * TILES + c * P
                        last = pe.matmul(bank[1][0:1, at:at + width], src[:, c:c + 1], ident[:, 0:width], start=True, stop=True)
                last.then_inc(s["table_done"], 1)

            def experts(layer):
                base = layer * GROUPS
                pe.wait_ge(s["tables"], 2 * (layer + 1))
                pe.wait_ge(s["w_in2"], 16 * 13)

                def turn_x(g, h, i):
                    pe.wait_ge(s[f"xe_in{h}"], (i + 1 + layer * (GROUPS // 2)) * 16 * GT)
                    for j in range(GT):
                        last = pe.transpose(bank[0][:, j * P:(j + 1) * P], xe[h][:, j, :], ident[:, :])
                    last.then_inc(s["xe_tp"], 1)

                def expert_of(g, j):
                    return pe.value_load(table[0:1, bass.ds(g * GT + j + TILES, 1)], min_val=0, max_val=E - 1)

                def gate_up(g, h):
                    pe.wait_ge(s["xeT_ready"], g + 1 + base)
                    for j in range(GT):
                        last = pe.matmul(bank[3 + 2 * h + j // 2][:, j % 2 * 2 * D:(j % 2 + 1) * 2 * D], xeT[h][:, j, :],
                                         gu_w[:, bass.ds(expert_of(g, j), 1), :].rearrange("p a n -> p (a n)"), start=True, stop=True)
                    last.then_inc(s["gu_done"], 1)

                def turn_h(g, h):
                    pe.wait_ge(s["hid_done"], g + 1 + base)
                    pe.wait_ge(s["hidT_ready"], g + base + 1)
                    for j in range(GT):
                        last = pe.transpose(bank[1][:, j * P:(j + 1) * P], hid[h][:, j, :], ident[:, :])
                    last.then_inc(s["hid_tp"], 1)

                def down(g, h):
                    pe.wait_ge(s["hidT_ready"], g + 2 + base)
                    pe.wait_ge(s["y_ready"], g + base + 1)
                    for j in range(GT):
                        last = pe.matmul(bank[7][:, j * D:(j + 1) * D], hidT[h][:, j, :],
                                         dn_w[:, bass.ds(expert_of(g, j), 1), :].rearrange("p a n -> p (a n)"), start=True, stop=True)
                    last.then_inc(s["y_done"], 1)

                turn_x(0, 0, 0)
                gate_up(0, 0)
                turn_x(1, 1, 0)
                gate_up(1, 1)
                turn_x(2, 0, 1)
                turn_h(0, 0)
                with pe.Fori(1, GROUPS // 2 - 1) as i:
                    for h in range(2):
                        gate_up(2 * i + h, h)
                        turn_x(2 * i + h + 1, 1 - h, i + h)
                        turn_h(2 * i + h - 1, 1 - h)
                        down(2 * i + h - 2, h)
                G = GROUPS
                gate_up(G - 2, 0)
                turn_x(G - 1, 1, G // 2 - 1)
                turn_h(G - 3, 1)
                down(G - 4, 0)
                gate_up(G - 1, 1)
                turn_h(G - 2, 0)
                down(G - 3, 1)
                turn_h(G - 1, 1)
                down(G - 2, 0)
                down(G - 1, 1)

            tables(0)
            experts(0)

            pe.wait_ge(s["bmax_done"], 2)
            with pe.Fori(0, B // 2) as i:
                for h in range(2):
                    b = 2 * i + h
                    turn(2 * (b + B), xna)
                    pe.matmul(bank[2][:, :], b_wq[:, :], xnT[:, :], start=True, stop=True)
                    pe.matmul(bank[3][:, :], b_wk[:, :], xnT[:, :], start=True, stop=True)
                    for j in range(TB):
                        last = pe.matmul(bank[4 + j // 2][:, j % 2 * 2 * D:(j % 2 + 1) * 2 * D], xnT[:, j * P:(j + 1) * P],
                                         b_wqv[:, :], start=True, stop=True)
                    last.then_inc(s["bproj_done"], 1)
                    pe.wait_ge(s["bqm_ready"], b + 1)
                    pe.wait_ge(s["btok_ready"], b + 1)
                    NP = TB * GH * 2
                    for n in range(NP):
                        t, j, gp = n // (2 * GH), n // 2 % GH, n % 2
                        if n >= 3:
                            pe.wait_ge(s["bmax_done"], b * NP + n - 2 + 2)
                        for q in range(2):
                            g = 2 * gp + q
                            rows = slice(32 * g, 32 * g + 32)
                            last = pe.matmul(bank[2 + 2 * (n % 3) + q][:, :], qm[rows, j, t * P:(t + 1) * P], kT[rows, :],
                                             start=True, stop=True)
                        last.then_inc(s["bsc_done"], 1)
                    pe.wait_ge(s["bmax_done"], b * NP + NP + 2)
                    for t in range(TB):
                        last = pe.transpose(bank[0][0:H, t * P:(t + 1) * P], smax[:, t, :], ident[:, :])
                    last.then_inc(s["mT_done"], 1)
                    pe.wait_ge(s["idg_done"], b + 1)
                    idr = idg[:, :, :].rearrange("h a u -> h (a u)")
                    pe.matmul(bank[1][:, 0:P], ones[0:H, :], idr, start=True, stop=True)
                    pe.matmul(bank[1][:, P:P + 1], idr, ones[0:H, 0:1], start=True, stop=True).then_inc(s["idx_done"], 1)
                    pe.wait_ge(s["sel_done"], b + 1)
                    for t in range(TB):
                        last = pe.matmul(bank[0][:, 0:P], tok[:, t, 0:D], selT[:, t, :], start=(t == 0), stop=(t == TB - 1))
                    last.then_inc(s["qsel_done"], 1)
                    pe.wait_ge(s["qsel_ready"], b + 1)
                    pe.matmul(bank[1][:, :], qsel[:, :], kT[:, :], start=True, stop=True).then_inc(s["att_done"], 1)
                    pe.wait_ge(s["aexp_done"], b + 1)
                    for t in range(TB):
                        last = pe.transpose(bank[0][:, t * P:(t + 1) * P], aexp[:, t * P:(t + 1) * P], ident[:, :])
                    last.then_inc(s["aeT_done"], 1)
                    pe.wait_ge(s["aeT_ready"], b + 1)
                    for t in range(TB):
                        last = pe.matmul(bank[1][:, 0:P], tok[:, t, D:2 * D], aexpT[:, t * P:(t + 1) * P], start=(t == 0), stop=(t == TB - 1))
                    last.then_inc(s["cx_done"], 1)
                    pe.wait_ge(s["cx_ready"], b + 1)
                    pe.matmul(bank[0][:, 0:D], cxm[:, :], b_wo[:, :], start=True, stop=True).then_inc(s["cw_done"], 1)
                    pe.wait_ge(s["cw_ready"], b + 1)
                    for t in range(TB):
                        last = pe.matmul(bank[1][:, t * D:(t + 1) * D], sel[:, t * P:(t + 1) * P], cwo[:, :], start=True, stop=True)
                    last.then_inc(s["bo_done"], 1)
                    route(b + B, h)
            tables(1)
            experts(1)


_NAMES = {"x": "L0_attn_a_x", "a_Wqk": "L0_attn_a_Wqk", "a_bqk": "L0_attn_a_bqk", "a_Wv": "L0_attn_a_Wv", "a_bv": "L0_attn_a_bv",
          "a_Wn": "L0_attn_a_Wn", "a_Wo": "L0_attn_a_Wo", "a_bo": "L0_attn_a_bo",
          "b_bq": "L0_attn_b_bq", "b_bk": "L0_attn_b_bk", "b_bv": "L0_attn_b_bv", "b_bo": "L0_attn_b_bo",
          "f_router": "L0_ffn_router_w", "f_gate": "L0_ffn_gate_w", "f_up": "L0_ffn_up_w", "f_down": "L0_ffn_down_w"}
_TURNED = {"b_wqT": "L0_attn_b_wq", "b_wkT": "L0_attn_b_wk", "b_wvT": "L0_attn_b_wv", "b_woT": "L0_attn_b_wo"}


def kernel(**inputs):
    import numpy as np
    import concourse.bacc as bacc
    from concourse.bass_utils import run_bass_kernel_spmd

    arrays = {n: np.ascontiguousarray(inputs[src]) for n, src in _NAMES.items()}
    for n, src in _TURNED.items():
        arrays[n] = np.ascontiguousarray(np.asarray(inputs[src]).T)
    arrays["a_bnr"] = np.repeat(np.asarray(inputs["L0_attn_a_bn"]), DH)
    nc = bacc.Bacc("TRN2", target_bir_lowering=False, num_devices=1)
    w = {n: nc.dram_tensor("in_" + n, a.shape, mybir.dt.from_np(a.dtype), kind="ExternalInput").ap() for n, a in arrays.items()}
    out = nc.dram_tensor("out", (B, SEQ, D), F32, kind="ExternalOutput").ap()
    build(nc, w, out)
    r = run_bass_kernel_spmd(nc, [{"in_" + n: a for n, a in arrays.items()}], core_ids=[0])
    return r.results[0]["out"]
```

```python
from contextlib import ExitStack

import concourse.bass as bass
from concourse import mybir

F32 = mybir.dt.float32
BF16 = mybir.dt.bfloat16
I32 = mybir.dt.int32
U32 = mybir.dt.uint32
ALU = mybir.AluOpType
ACT = mybir.ActivationFunctionType
AX = mybir.AxisListType

P = 128
D = 128
H = 16
DH = D // H
GH = 4
NG = H // GH
E = 16
K = 2
B = 16
SEQ = 512
TB = SEQ // P
T = B * SEQ
NT = T // P
CAP = -(-T * K * 5 // (E * 4))
UT = 2
UR = UT * P
SPAN = K * CAP + UR
UNITS = 80
GU = 2
GT = GU * UT
GROUPS = UNITS // GU
NX = 4
assert UNITS >= T * K // UR + E - 1 and GROUPS % NX == 0
DUMMY = E * SPAN
UNSENT = DUMMY + UR
ZROW = UNITS * UR
TOPU = 6
PRODUCTS = ((0, 0), (0, 1), (0, 2), (1, 0), (1, 1), (1, 2), (2, 0), (2, 1))
STACK = DH * len(PRODUCTS)
PAIRS = TB * H // 2
SLOTU = 8
EPS = 1e-5
SCALE = float(DH) ** -0.5
LNMAX = -(-K * CAP // UR)


def build(nc, w, out):
    ctx = ExitStack()
    with ctx:
        def sb(name, shape, dt=F32):
            return ctx.enter_context(nc.sbuf_tensor(name, shape, dt))

        def pb(name):
            return ctx.enter_context(nc.psum_tensor(name, [P, 512], F32))

        def sem(name):
            return ctx.enter_context(nc.semaphore(name))

        disp = nc.dram_tensor("disp", [DUMMY + UR, D], F32).ap()
        ybuf = nc.dram_tensor("ybuf", [ZROW + P, D], F32).ap()
        qparts = [nc.dram_tensor(f"qparts{h}", [3, P, SEQ], BF16).ap() for h in range(2)]
        kparts = [nc.dram_tensor(f"kparts{h}", [3, P, SEQ], BF16).ap() for h in range(2)]

        xs = sb("xs", [P, NT, D])
        sent = sb("sent", [P, NT * K])
        expt = sb("expt", [P, NT * K])
        slots = sb("slots", [P, NT * K], I32)
        wts = sb("wts", [P, NT * K])
        gu_w = sb("gu_w", [P, E, 2 * D])
        dn_w = sb("dn_w", [P, E, D])
        rt_w = sb("rt_w", [P, E])
        a_wq = sb("a_wq", [P, D])
        a_wk = sb("a_wk", [P, D])
        a_wkv = sb("a_wkv", [P, 2 * D])
        a_wn = sb("a_wn", [P, E])
        a_wnr = sb("a_wnr", [P, D])
        a_wo = sb("a_wo", [P, D])
        b_wq = sb("b_wq", [P, D])
        b_wk = sb("b_wk", [P, D])
        b_wqv = sb("b_wqv", [P, 2 * D])
        b_wo = sb("b_wo", [P, D])
        cols = sb("cols", [P, 6])
        a_kvb = sb("a_kvb", [P, 2 * D])
        b_qvb = sb("b_qvb", [P, 2 * D])
        a_bo = sb("a_bo", [P, D])
        b_bo = sb("b_bo", [P, D])

        ident = sb("ident", [P, P])
        ones = sb("ones", [P, P])
        zeros = sb("zeros", [P, UT * D])
        onesb = sb("onesb", [P, P], BF16)
        before = sb("before", [P, P], BF16)
        causal = sb("causal", [P, P])
        block8 = sb("block8", [P, P])
        headpos = sb("headpos", [P, H, DH])
        headof = sb("headof", [P, H])
        inhead = sb("inhead", [P, GH])
        headrow = sb("headrow", [H, H, SLOTU])
        eiota = sb("eiota", [P, E])
        tokcol = sb("tokcol", [P, TB])
        tokrow = sb("tokrow", [P, SEQ])
        unitcol = sb("unitcol", [P, 1])
        mstep = sb("mstep", [P, LNMAX])
        ebase = sb("ebase", [P, E])
        ksign = sb("ksign", [P, TB, K])
        kbase = sb("kbase", [P, TB, K])

        st = sb("st", [P, TB, 6])
        mv = sb("mv", [P, TB, 2])
        rstd = sb("rstd", [P, TB])
        lnv = sb("lnv", [P, TB])
        lnh = sb("lnh", [P, TB])
        lny = [sb(f"lny{h}", [P, TB]) for h in range(2)]
        lnt = sb("lnt", [P, TB])
        lnu = sb("lnu", [P, TB])
        xna = sb("xna", [P, TB, D])
        xnT = sb("xnT", [P, SEQ])
        xnf = [sb(f"xnf{h}", [P, TB, D]) for h in range(2)]
        xfT = sb("xfT", [P, SEQ])
        lmax = sb("lmax", [P, TB])
        lsub = sb("lsub", [P, TB, E])
        lexp = sb("lexp", [P, TB, E])
        lsum = sb("lsum", [P, TB])
        linv = sb("linv", [P, TB])
        top8 = sb("top8", [P, TB, 8])
        top8i = sb("top8i", [P, TB, 8], U32)
        topf = sb("topf", [P, TB, K])
        topw = sb("topw", [P, TB, K])
        oneh = sb("oneh", [P, TB, K, E], BF16)
        ohnew = sb("ohnew", [P, K * E])
        ohsum = sb("ohsum", [P, K * E], BF16)
        rkoh = sb("rkoh", [P, TB * K, E])
        rank = sb("rank", [P, TB, K])
        keep = sb("keep", [P, TB, K])
        sbase = sb("sbase", [P, TB, K])
        soff = sb("soff", [P, TB, K])
        sval = sb("sval", [P, TB, K])
        sgo = sb("sgo", [P, TB, K])
        sli = [sb(f"sli{h}", [P, TB * K], I32) for h in range(2)]
        slg = [sb(f"slg{h}", [P, TB * K], I32) for h in range(2)]
        yg = [sb(f"yg{h}", [P, TB * K, D]) for h in range(2)]

        cnt = sb("cnt", [P, K, E])
        ntok = sb("ntok", [P, E])
        over = sb("over", [P, E, LNMAX])
        ntile = sb("ntile", [P, E])
        tend = sb("tend", [P, E])
        tstart = sb("tstart", [P, E])
        rowof = sb("rowof", [P, E])
        past = sb("past", [P, E])
        reached = sb("reached", [P, E])
        here = sb("here", [P, E])
        hsum = sb("hsum", [P, 1])
        texp = sb("texp", [P, 1])
        texpc = sb("texpc", [P, 1])
        toff = sb("toff", [P, E])
        toffs = sb("toffs", [P, 1])
        tlin = sb("tlin", [P, 1])
        tlin2 = sb("tlin2", [P, 1])
        trow = sb("trow", [P, 1])
        
        shift = sb("shift", [P, NT * K])
        kept = sb("kept", [P, NT * K])
        tailf = sb("tailf", [P, E])
        table = sb("table", [1, 2 * UNITS], I32)
        tails = sb("tails", [1, E], I32)
        part = [sb(f"part{x}", [P, 3, SEQ], BF16) for x in "qk"]
        restk = sb("restk", [P, SEQ])
        stackq = [sb(f"stackq{h}", [P, H, SEQ], BF16) for h in range(2)]
        stackk = [sb(f"stackk{h}", [P, H, SEQ], BF16) for h in range(2)]

        def carve(t, width, shapes):
            flat = t[:, :, :].rearrange("p h t -> p (h t)").bitcast(F32)
            at, views = 0, []
            for n, shape in enumerate(shapes):
                size = 1
                for x in shape:
                    size *= x
                v = flat[:, at:at + size]
                if len(shape) == 2:
                    v = v.rearrange("p (a b) -> p a b", a=shape[0])
                if len(shape) == 3:
                    v = v.rearrange("p (a b c) -> p a b c", a=shape[0], b=shape[1])
                views.append(v)
                at += size
            assert at <= width
            return views
        pT = carve(stackk[0], H * SEQ // 2, [(NG, GH, P)] * 2)
        whose, = carve(stackk[0], H * SEQ // 2, [(NT * K, E)])
        qm, = carve(stackq[0], H * SEQ // 2, [(GH, SEQ)])
        xe = carve(stackq[1], H * SEQ // 2, [(GT, D)] * NX)
        xeT = carve(stackq[1], H * SEQ // 2, [(NX * GT, D)] + [(GT, D)] * 2)[1:]
        sg = carve(stackq[1], H * SEQ // 2, [((NX + 2) * GT, D)] + [(GT, D)] * 2)[1:]
        hid, hidT, ye = (carve(stackk[1], H * SEQ // 2, [(max(1, 2 * n * GT), D)] + [(GT, D)] * 2)[1:] if n else
                         carve(stackk[1], H * SEQ // 2, [(GT, D)] * 2) for n in range(3))
        einv = sb("einv", [P, SEQ])
        qT = sb("qT", [P, SEQ])
        kTs = [sb(f"kT{h}", [P, SEQ]) for h in range(2)]
        kT = kTs[0]
        selT = sb("selT", [P, TB, P])
        sel = sb("sel", [P, SEQ])
        aexp = sb("aexp", [P, SEQ])
        aexpT = sb("aexpT", [P, SEQ])
        toks = [sb(f"tok{h}", [P, TB, 2 * D]) for h in range(2)]
        tok = toks[0]
        VSTEP = D + DH
        vm, = carve(stackq[1], H * SEQ // 2, [(TB, GH * VSTEP)])
        stm = [sb(f"stm{h}", [P, D]) for h in range(2)]
        ctxT = sb("ctxT", [P, SEQ])
        smax = [sb(f"smax{h}", [P, TB, H]) for h in range(2)]
        mT = sb("mT", [H, SEQ])
        m8 = sb("m8", [H, SLOTU])
        m8i = sb("m8i", [H, SLOTU], U32)
        m8f = sb("m8f", [H, SLOTU])
        idg = sb("idg", [H, H, SLOTU])
        idc = sb("idc", [P, 1])
        qsel = sb("qsel", [P, P])
        amax = sb("amax", [P, 1])
        aneg = sb("aneg", [P, 1])
        asum = sb("asum", [P, 1])
        ainv = sb("ainv", [P, 1])
        cxm = sb("cxm", [P, P])
        cwo = sb("cwo", [P, D])

        pair = [ctx.enter_context(nc.psum_tensor(f"pair{i}", [P, 2, 512], F32)) for i in range(2)]
        bank = [pb(f"bank{i}") for i in range(4)] + [pair[i // 2][:, i % 2, :] for i in range(4)]

        names = ("w_in w_in2 consts0 consts1 consts2 consts3 ms0 ms1 wnr x_in0 x_in1 bias_added " + " ".join(f"{k}_{n}" for k in ("att", "ffn") for n in "stats moments rs xn_ready tp_done xT_ready".split()) + " "
                 ""
                 "x1_ready logits_done lmax_done lsub_done lexp_done lsum_done linv_done top_done topi_done topf_done oneh_done "
                 "rank_done rkoh_done rk_done ohnew_done ohsum_done keep_done sbase_done soff_done sval_done sgo_done slots_ready "
                 "w_ready sent0 sent1 counts_done tb table_done tables tails_in zeroed stored_all "
                 "xe_in0 xe_in1 xe_tp xeT_ready gu_done silu_done hid_done hid_tp hidT_ready y_done y_ready xe_in2 xe_in3 y_out0 y_out1 "
                 "slg_ready got0 got1 comb0 combined "
                 "zeroed_k zeroed_q proj_done einv_ready qT_ready kT_ready qm_ready tok_ready vm_ready sc_done pT_ready state_done stm_ready ctx_done ctxT_ready o_done "
                 "bproj_done tokproj_done btok_ready first_parts second_parts rest_ready third_parts parts_out0 parts_out1 stack_in0 stack_in1 bsc_done bmax_done mT_done mTs_done m8_done m8i_done m8f_done idg_done "
                 "idx_done idc_done sel_done qsel_done qsel_ready att_done amax_done aneg_done aexp_done aeT_done aeT_ready cx_done cx_ready "
                 "cw_done ainv_done cw_ready bo_done x_out settled xnf_free fetched")
        s = {n: sem(n) for n in names.split()}

        block = ctx.enter_context(nc.Block())

        def tiles_of(b):
            return bass.ds(b * TB, TB)

        x_b = w["x"].rearrange("b (t p) d -> b p t d", p=P)
        out_b = out.rearrange("b (t p) d -> b p t d", p=P)
        WLOADS = 20

        def settle(eng):
            eng.sem_inc(s["settled"], 1)

        AHEAD = 16

        def each_batch(eng, body):
            body(0, 0, 0, last=False)
            with eng.Fori(0, B // 2 - 2) as i:
                body(2 * i + 1, i, 1)
                body(2 * i + 2, i + 1, 0)
            body(B - 3, B // 2 - 2, 1)
            body(B - 2, B // 2 - 1, 0, fetch=False)
            body(B - 1, B // 2 - 1, 1, next=False, fetch=False)

        @block.sync
        def _(sp):
            for h in range(2):
                sp.sem_inc(s[f"y_out{h}"], AHEAD)
            for dst, src in ((a_wq[:, :], w["a_Wqk"][:, 0:D]), (a_wk[:, :], w["a_Wqk"][:, D:2 * D]),
                             (a_wkv[:, 0:D], w["a_Wqk"][:, D:2 * D]), (a_wkv[:, D:2 * D], w["a_Wv"]),
                             (a_wn[:, :], w["a_Wn"]), (a_wo[:, :], w["a_Wo"]),
                             (cols[:, 0:1], w["a_bqk"][0:D].rearrange("(p a) -> p a", a=1)),
                             (cols[:, 1:2], w["a_bqk"][D:2 * D].rearrange("(p a) -> p a", a=1)),
                             (cols[:, 5:6], w["a_bnr"].rearrange("(p a) -> p a", a=1)),
                             (a_kvb[:, 0:D], w["a_bqk"][D:2 * D].rearrange("(a n) -> a n", a=1).to_broadcast([P, D])),
                             (a_kvb[:, D:2 * D], w["a_bv"].rearrange("(a n) -> a n", a=1).to_broadcast([P, D])),
                             (a_bo[:, :], w["a_bo"].rearrange("(a n) -> a n", a=1).to_broadcast([P, D])),
                             (rt_w[:, :], w["f_router"])):
                sp.dma_start(dst, src).then_inc(s["w_in"], 16)
            for h in range(2):
                sp.dma_start(xs[:, tiles_of(h), :], x_b[h]).then_inc(s[f"x_in{h}"], 16)
            with sp.Fori(1, B // 2) as i:
                for h in range(2):
                    sp.wait_ge(s[f"x_in{h}"], i * 16)
                    sp.dma_start(xs[:, tiles_of(2 * i + h), :], x_b[2 * i + h]).then_inc(s[f"x_in{h}"], 16)
            for dst, src in ((gu_w[:, :, 0:D], w["f_gate"].rearrange("e d h -> d e h")),
                             (gu_w[:, :, D:2 * D], w["f_up"].rearrange("e d h -> d e h")),
                             (dn_w[:, :, :], w["f_down"].rearrange("e d h -> d e h")),
                             (b_wq[:, :], w["b_wqT"]), (b_wk[:, :], w["b_wkT"]),
                             (b_wqv[:, 0:D], w["b_wqT"]), (b_wqv[:, D:2 * D], w["b_wvT"]), (b_wo[:, :], w["b_woT"]),
                             (cols[:, 3:4], w["b_bq"].rearrange("(p a) -> p a", a=1)),
                             (cols[:, 4:5], w["b_bk"].rearrange("(p a) -> p a", a=1)),
                             (b_qvb[:, 0:D], w["b_bq"].rearrange("(a n) -> a n", a=1).to_broadcast([P, D])),
                             (b_qvb[:, D:2 * D], w["b_bv"].rearrange("(a n) -> a n", a=1).to_broadcast([P, D])),
                             (b_bo[:, :], w["b_bo"].rearrange("(a n) -> a n", a=1).to_broadcast([P, D]))):
                sp.dma_start(dst, src).then_inc(s["w_in2"], 16)
            sp.wait_ge(s["consts1"], 1)
            sp.dma_start(disp[DUMMY:DUMMY + UR, :].rearrange("(p a) d -> p (a d)", a=UT), zeros[:, :]).then_inc(s["zeroed"], 16)
            sp.dma_start(ybuf[ZROW:ZROW + P, :], zeros[:, 0:D]).then_inc(s["zeroed"], 16)

            def experts(layer):
                sp.wait_ge(s["tables"], 2 * (layer + 1))
                for e in range(E):
                    row = sp.value_load(tails[0:1, e:e + 1], min_val=0, max_val=DUMMY - UR)
                    sp.dma_start(disp[bass.ds(row, UR), :].rearrange("(p a) d -> p (a d)", a=UT),
                                 zeros[:, :]).then_inc(s["zeroed"], 16)
                sp.wait_ge(s["zeroed"], 16 * (2 + E * (layer + 1)))
                for h in range(2):
                    sp.wait_ge(s[f"sent{h}"], 16 * TB * K * (B // 2) * (layer + 1))

                def load(g, r):
                    rows = [sp.value_load(table[0:1, bass.ds(g * GU + u, 1)], min_val=0, max_val=DUMMY) for u in range(GU)]
                    for u in range(GU):
                        sp.dma_start(xe[r][:, UT * u:UT * (u + 1), :], disp[bass.ds(rows[u], UR), :].rearrange(
                            "(p a) d -> p a d", a=UT)).then_inc(s[f"xe_in{r}"], 16)

                def reload(g, r):
                    sp.wait_ge(s["xe_tp"], g + 1 + layer * GROUPS)
                    load(g + NX, r)

                def store(g, h):
                    sp.wait_ge(s["y_ready"], g + 2 + layer * GROUPS)
                    sp.dma_start(ybuf[bass.ds(g * (GT * P), GT * P), :].rearrange("(u p a) d -> p u (a d)", p=P, a=UT),
                                 ye[h][:, :, :].rearrange("p (u a) d -> p u (a d)", a=UT)).then_inc(s[f"y_out{h}"], 16)

                for r in range(NX):
                    load(r, r)
                reload(0, 0)
                reload(1, 1)
                for r in (2, 3):
                    reload(r, r)
                    store(r - 2, r % 2)
                with sp.Fori(1, GROUPS // NX - 1) as i:
                    for r in range(NX):
                        reload(NX * i + r, r)
                        store(NX * i + r - 2, r % 2)
                for g in range(GROUPS - NX - 2, GROUPS):
                    store(g, g % 2)
                for h in range(2):
                    sp.wait_ge(s[f"y_out{h}"], AHEAD + 16 * (GROUPS // 2) * (layer + 1))
                sp.sem_inc(s["stored_all"], 1)

            experts(0)
            with sp.Fori(0, B // 2) as i:
                for h in range(2):
                    sp.wait_ge(s["third_parts"], 2 * i + h + 1)
                    for dst, src in ((qparts[h], part[0]), (kparts[h], part[1])):
                        sp.dma_start(dst.rearrange("c p t -> p c t"), src[:, :, :]).then_inc(s[f"parts_out{h}"], 16)
                    sp.wait_ge(s[f"parts_out{h}"], (i + 1) * 32)
                    for n, (cq, ck) in enumerate(PRODUCTS):
                        rows = slice(n * DH, (n + 1) * DH)
                        for stack, parts, c in ((stackq, qparts, cq), (stackk, kparts, ck)):
                            sp.dma_start(stack[h][rows, :, :], parts[h][c].rearrange("(d h) t -> d h t", h=H)).then_inc(
                                s[f"stack_in{h}"], 16)
            experts(1)
            with sp.Fori(0, B) as i:
                sp.wait_ge(s["combined"], i + 1 + B)
                sp.dma_start(out_b[i], xs[:, tiles_of(i), :]).then_inc(s["x_out"], 16)
            sp.wait_ge(s["x_out"], 16 * B)

        @block.gpsimd
        def _(pool):
            pool.sem_inc(s["xnf_free"], 2)
            pool.memset(ident[:, :], 0.0)
            pool.memset(ones[:, :], 1.0)
            pool.memset(onesb[:, :], 1.0)
            pool.memset(zeros[:, :], 0.0).then_inc(s["consts1"], 1)
            pool.memset(block8[:, :], 1.0)
            pool.memset(causal[:, :], 1.0)
            pool.memset(before[:, :], 1.0)
            pool.memset(headrow[:, :, :], 0.0)
            pool.memset(headpos[:, :, :], 0.0)
            pool.memset(ohsum[:, :], 0.0)
            pool.memset(vm[:, :, :], 0.0)
            pool.memset(m8f[:, :], -1.0)
            for k in range(K):
                pool.memset(ksign[:, :, k], 2.0 * k - 1.0)
                pool.memset(kbase[:, :, k], float(CAP - 1 + k)).then_inc(s["ms0"], 1)
            pool.wait_ge(s["ms0"], K)
            pool.affine_select(out=ident[:, :], in_=ident[:, :], compare_op=ALU.not_equal, fill=1.0, base=0,
                               pattern=[[-1, P]], channel_multiplier=1)
            pool.affine_select(out=causal[:, :], in_=causal[:, :], compare_op=ALU.is_ge, fill=0.0, base=0,
                               pattern=[[1, P]], channel_multiplier=-1)
            pool.affine_select(out=before[:, :], in_=before[:, :], compare_op=ALU.is_ge, fill=0.0, base=-1,
                               pattern=[[1, P]], channel_multiplier=-1)
            pool.affine_select(out=headrow[:, :, :], in_=headrow[:, :, :], compare_op=ALU.not_equal, fill=1.0, base=0,
                               pattern=[[-1, H], [0, SLOTU]], channel_multiplier=1)
            pool.affine_select(out=headpos[:, :, :], in_=headpos[:, :, :], compare_op=ALU.not_equal, fill=1.0, base=0,
                               pattern=[[-1, H], [-H, DH]], channel_multiplier=1)
            bv = block8[:, :].rearrange("p (h d) -> p h d", d=DH)
            pool.affine_select(out=bv, in_=bv, compare_op=ALU.is_ge, fill=0.0, base=0,
                               pattern=[[-DH, H], [0, DH]], channel_multiplier=1).then_inc(s["ms1"], 1)
            pool.wait_ge(s["ms1"], 1)
            pool.affine_select(out=bv, in_=bv, compare_op=ALU.is_ge, fill=0.0, base=DH - 1,
                               pattern=[[DH, H], [0, DH]], channel_multiplier=-1)

            def iota(t, base, pattern, cm):
                return pool.iota(t, base=base, pattern=pattern, channel_multiplier=cm,
                                 allow_small_or_imprecise_dtypes=True)
            iota(eiota[:, :], 0, [[1, E]], 0)
            iota(tokcol[:, :], 0, [[P, TB]], 1)
            iota(tokrow[:, :], 0, [[1, SEQ]], 0)
            iota(unitcol[:, :], 0, [[1, 1]], 1)
            iota(mstep[:, :], 0, [[UR, LNMAX]], 0)
            iota(ebase[:, :], CAP, [[SPAN, E]], 0).then_inc(s["consts2"], 1)

            def send(g, i, h):
                pool.wait_ge(s["slots_ready"], g + 1)
                settle(pool)
                for j in range(TB):
                    for k in range(K):
                        pool.indirect_dma_start(
                            out=disp, out_offset=bass.IndirectOffsetOnAxis(ap=sli[h][:, K * j + k:K * j + k + 1], axis=0),
                            in_=xnf[h][:, j, :], in_offset=None, bounds_check=DUMMY - 1, oob_is_err=False,
                        ).then_inc(s[f"sent{h}"], 16)
                pool.wait_ge(s[f"sent{h}"], (i + 1) * 16 * TB * K)
                pool.sem_inc(s["xnf_free"], 1)

            def fetch(g, i, h):
                pool.wait_ge(s["slg_ready"], g + 1)
                settle(pool)
                for j in range(TB * K):
                    pool.indirect_dma_start(
                        out=yg[h][:, j, :], out_offset=None, in_=ybuf,
                        in_offset=bass.IndirectOffsetOnAxis(ap=slg[h][:, j:j + 1], axis=0),
                    ).then_inc(s[f"got{h}"], 16)
                pool.wait_ge(s[f"got{h}"], (i + 1) * 16 * TB * K)
                pool.sem_inc(s["fetched"], 1)

            def add_bias(b, g, row):
                pool.wait_ge(s["att_xn_ready"], g + 1)
                settle(pool)
                xb = xs[:, tiles_of(b), :]
                pool.tensor_tensor(xb, xb, row[:, :].unsqueeze(1).to_broadcast([P, TB, D]), ALU.add).then_inc(s["bias_added"], 1)

            pool.wait_ge(s["w_in"], 16 * 13)
            with pool.Fori(0, B // 2) as i:
                for h in range(2):
                    b = 2 * i + h
                    add_bias(b, b, a_bo)
                    pool.wait_ge(s["tok_ready"], b + 1)
                    settle(pool)
                    for j in range(TB):
                        dst = vm[:, j, :].rearrange("p (j x) -> p j x", x=VSTEP)[:, :, 0:D].rearrange(
                            "p j (g y) -> p j g y", y=GH * DH)[:, :, :, 0:DH]
                        src = tok[:, j, D:2 * D].rearrange("p (g j d) -> p j g d", g=NG, j=GH)
                        last = pool.tensor_copy(dst, src)
                    last.then_inc(s["vm_ready"], 1)
                    send(b, i, h)
            pool.wait_ge(s["w_in2"], 16 * 13)
            pool.wait_ge(s["stored_all"], 1)
            fetch(0, 0, 0)
            pool.memset(stackk[1][STACK:P, :, :], 0.0)
            pool.memset(stackq[1][STACK:P, :, :], 0.0).then_inc(s["zeroed_q"], 1)
            fetch(1, 0, 1)

            def rests(n, k):
                pool.wait_ge(s["first_parts"], n + 1)
                settle(pool)
                pool.tensor_tensor(qT[:, :], qT[:, :], part[0][:, 0, :], ALU.subtract)
                pool.tensor_tensor(restk[:, :], kTs[k][:, :], part[1][:, 0, :], ALU.subtract).then_inc(s["rest_ready"], 1)
                pool.wait_ge(s["second_parts"], n + 1)
                settle(pool)
                pool.tensor_tensor(part[0][:, 2, :], qT[:, :], part[0][:, 1, :], ALU.subtract)
                pool.tensor_tensor(part[1][:, 2, :], restk[:, :], part[1][:, 1, :], ALU.subtract).then_inc(s["third_parts"], 1)

            def body(b, u, h, last=True, next=True, fetch_=True):
                if last:
                    add_bias(b - 1, b - 1 + B, b_bo)
                if fetch_:
                    fetch(b + 2, u + 1, h)
                if next:
                    rests(b + 1, 1 - h)
                if last:
                    send(b - 1 + B, u + h - 1 + B // 2, 1 - h)

            rests(0, 0)
            each_batch(pool, lambda b, u, h, last=True, next=True, fetch=True: body(b, u, h, last, next, fetch))
            add_bias(B - 1, 2 * B - 1, b_bo)
            send(2 * B - 1, B - 1, 1)
            pool.wait_ge(s["stored_all"], 2)
            with pool.Fori(0, B // 2) as i:
                for h in range(2):
                    b = 2 * i + h
                    fetch(b + B, i + B // 2, h)

        @block.scalar
        def _(act):
            act.sem_inc(s["hidT_ready"], 1)
            act.wait_ge(s["w_in"], 16 * 13)
            act.activation(a_wnr[:, :].rearrange("p (h d) -> p h d", d=DH),
                           a_wn[:, :].unsqueeze(2).to_broadcast([P, H, DH]), ACT.Copy).then_inc(s["wnr"], 1)
            act.activation(cols[:, 2:3], cols[:, 5:6], ACT.Copy, scale=-1.0).then_inc(s["wnr"], 1)
            act.wait_ge(s["wnr"], 2)

            def turned(n, kind, dst, src=bank[0]):
                act.wait_ge(s[kind + "_tp_done"], n + 1)
                act.activation(dst[:, :], src[:, :], ACT.Copy).then_inc(s[kind + "_xT_ready"], 1)

            def route_exp(g):
                act.wait_ge(s["lsub_done"], g + 1)
                act.activation(lexp[:, :, :], lsub[:, :, :], ACT.Exp).then_inc(s["lexp_done"], 1)

            act.wait_ge(s["consts3"], 1)
            with act.Fori(0, B) as b:
                turned(b, "att", xnT)
                act.wait_ge(s["proj_done"], b + 1)
                act.activation(einv[:, :], bank[5][:, :], ACT.Exp, bias=cols[:, 2:3], scale=-1.0).then_inc(s["einv_ready"], 1)
                act.activation(kT[:, :], bank[6][:, :], ACT.Identity, bias=cols[:, 1:2]).then_inc(s["kT_ready"], 1)
                act.wait_ge(s["qT_ready"], b + 1)
                for j in range(GH):
                    last = act.activation(qm[:, j, :], qT[:, :], ACT.Copy, scale=inhead[:, j:j + 1])
                last.then_inc(s["qm_ready"], 1)
                act.wait_ge(s["ctx_done"], b + 1)
                act.activation(ctxT[:, :], bank[1][:, :], ACT.Copy).then_inc(s["ctxT_ready"], 1)
                turned(b, "ffn", xfT)
                route_exp(b)

            def experts(layer):
                base = layer * GROUPS

                def xT(g, h):
                    act.wait_ge(s["xe_tp"], g + 1 + base)
                    act.activation(xeT[h][:, :, :].rearrange("p j d -> p (j d)"), bank[0][:, :], ACT.Copy).then_inc(s["xeT_ready"], 1)

                def silu(g, h):
                    act.wait_ge(s["gu_done"], g + 1 + base)
                    for q in range(2):
                        src = bank[3 + 2 * h + q][:, :].rearrange("p (j n) -> p j n", j=2)[:, :, 0:D]
                        last = act.activation(sg[h][:, 2 * q:2 * q + 2, :], src, ACT.Silu)
                    last.then_inc(s["silu_done"], 1)

                def hT(g, h):
                    act.wait_ge(s["hid_tp"], g + 1 + base)
                    act.activation(hidT[h][:, :, :].rearrange("p j d -> p (j d)"), bank[1][:, :], ACT.Copy).then_inc(s["hidT_ready"], 1)

                xT(0, 0)
                silu(0, 0)
                xT(1, 1)
                silu(1, 1)
                xT(2, 0)
                hT(0, 0)
                with act.Fori(1, GROUPS // 2 - 1) as i:
                    for h in range(2):
                        silu(2 * i + h, h)
                        xT(2 * i + h + 1, 1 - h)
                        hT(2 * i + h - 1, 1 - h)
                silu(GROUPS - 2, 0)
                xT(GROUPS - 1, 1)
                hT(GROUPS - 3, 1)
                silu(GROUPS - 1, 1)
                hT(GROUPS - 2, 0)
                hT(GROUPS - 1, 1)

            experts(0)
            act.wait_ge(s["w_in2"], 16 * 13)
            def first_parts(n, k):
                act.wait_ge(s["bproj_done"], n + 1)
                act.activation(qT[:, :], bank[2][:, :], ACT.Identity, bias=cols[:, 3:4])
                act.activation(part[0][:, 0, :], bank[2][:, :], ACT.Identity, bias=cols[:, 3:4])
                act.activation(kTs[k][:, :], bank[3][:, :], ACT.Identity, bias=cols[:, 4:5])
                act.activation(part[1][:, 0, :], bank[3][:, :], ACT.Identity, bias=cols[:, 4:5]).then_inc(s["first_parts"], 1)

            def second_parts(n):
                act.wait_ge(s["rest_ready"], n + 1)
                act.activation(part[0][:, 1, :], qT[:, :], ACT.Copy)
                act.activation(part[1][:, 1, :], restk[:, :], ACT.Copy).then_inc(s["second_parts"], 1)

            def selected_exp(b):
                act.wait_ge(s["aneg_done"], b + 1)
                act.activation(aexp[:, :], bank[1][:, :], ACT.Exp, bias=aneg[:, 0:1], scale=SCALE,
                               accum_out=asum[:, 0:1]).then_inc(s["aexp_done"], 1)

            def finish(b):
                act.wait_ge(s["aeT_done"], b + 1)
                act.activation(aexpT[:, :], bank[0][:, :], ACT.Copy).then_inc(s["aeT_ready"], 1)
                turned(b + B, "ffn", xfT)
                route_exp(b + B)

            def body(b, u, h, last=True, next=True, fetch=True):
                if next:
                    turned(b + 1 + B, "att", xnT, bank[2])
                    first_parts(b + 1, 1 - h)
                if last:
                    selected_exp(b - 1)
                if next:
                    second_parts(b + 1)
                if last:
                    finish(b - 1)

            turned(B, "att", xnT, bank[2])
            first_parts(0, 0)
            second_parts(0)
            each_batch(act, body)
            selected_exp(B - 1)
            finish(B - 1)
            experts(1)

        @block.vector
        def _(dve):
            dve.sem_inc(s["y_ready"], 1)
            dve.wait_ge(s["consts2"], 1)
            dve.tensor_reduce(headof[:, :], headpos[:, :, :], AX.X, ALU.add)
            dve.tensor_reduce(inhead[:, :], block8[:, :].rearrange("p (g j d) -> p j g d", g=NG, j=GH)[:, :, :, 0],
                              AX.X, ALU.add).then_inc(s["consts3"], 1)

            def norm(b, n, dst, kind):
                rs, stats, moments = s[kind + "_rs"], s[kind + "_stats"], s[kind + "_moments"]
                settle(dve)
                for j in range(TB):
                    last = dve.bn_stats(st[:, j, :], xs[:, b * TB + j, :])
                last.then_inc(stats, 1)
                dve.wait_ge(stats, n + 1)
                settle(dve)
                for j in range(TB):
                    last = dve.bn_aggr(mv[:, j, :], st[:, j, :])
                last.then_inc(moments, 1)
                dve.wait_ge(moments, n + 1)
                dve.tensor_scalar(lnv[:, :], mv[:, :, 1], EPS, None, ALU.add).then_inc(rs, 1)
                dve.tensor_scalar(lnh[:, :], mv[:, :, 1], EPS, -0.5, ALU.add, ALU.mult)
                dve.wait_ge(rs, n * 11 + 1)
                dve.tensor_scalar(lny[0][:, :].bitcast(I32), lnv[:, :].bitcast(I32), -0.5, float(0x5f3759df),
                                  ALU.mult, ALU.add).then_inc(rs, 1)
                for r in range(3):
                    y, z = lny[r % 2], (lny[1 - r % 2] if r < 2 else rstd)
                    dve.wait_ge(rs, n * 11 + 2 + 3 * r)
                    dve.tensor_tensor(lnt[:, :], y[:, :], y[:, :], ALU.mult).then_inc(rs, 1)
                    dve.wait_ge(rs, n * 11 + 3 + 3 * r)
                    dve.tensor_tensor(lnu[:, :], lnt[:, :], lnh[:, :], ALU.mult).then_inc(rs, 1)
                    dve.wait_ge(rs, n * 11 + 4 + 3 * r)
                    dve.scalar_tensor_tensor(out=z[:, :], in0=lnu[:, :], scalar=1.5, in1=y[:, :],
                                             op0=ALU.add, op1=ALU.mult).then_inc(rs, 1)
                dve.wait_ge(rs, n * 11 + 11)
                for j in range(TB):
                    last = dve.tensor_scalar(dst[:, j, :], xs[:, b * TB + j, :], mv[:, j, 0:1], rstd[:, j:j + 1],
                                             ALU.subtract, ALU.mult)
                last.then_inc(s[kind + "_xn_ready"], 1)

            def route_max(g, at):
                lg = at[:, 0:TB * E].rearrange("p (t e) -> p t e", e=E)
                dve.wait_ge(s["logits_done"], g + 1)
                dve.tensor_reduce(lmax[:, :], lg, AX.X, ALU.max).then_inc(s["lmax_done"], 1)
                dve.wait_ge(s["lmax_done"], g + 1)
                dve.tensor_tensor(lsub[:, :, :], lg, lmax[:, :].unsqueeze(2).to_broadcast([P, TB, E]),
                                  ALU.subtract).then_inc(s["lsub_done"], 1)

            def route_top(g):
                dve.wait_ge(s["lexp_done"], g + 1)
                settle(dve)
                for j in range(TB):
                    last = dve.max(top8[:, j, :], lexp[:, j, :])
                last.then_inc(s["top_done"], 1)
                dve.tensor_reduce(lsum[:, :], lexp[:, :, :], AX.X, ALU.add).then_inc(s["lsum_done"], 1)
                dve.wait_ge(s["top_done"], g + 1)
                settle(dve)
                for j in range(TB):
                    last = dve.max_index(top8i[:, j, :], top8[:, j, :], lexp[:, j, :])
                last.then_inc(s["topi_done"], 1)
                dve.wait_ge(s["lsum_done"], g + 1)
                dve.reciprocal(linv[:, :], lsum[:, :]).then_inc(s["linv_done"], 1)
                dve.wait_ge(s["topi_done"], g + 1)
                dve.tensor_copy(topf[:, :, :], top8i[:, :, 0:K]).then_inc(s["topf_done"], 1)
                dve.wait_ge(s["linv_done"], g + 1)
                dve.tensor_tensor(topw[:, :, :], top8[:, :, 0:K], linv[:, :].unsqueeze(2).to_broadcast([P, TB, K]), ALU.mult)
                dve.wait_ge(s["topf_done"], g + 1)
                for k in range(K):
                    last = dve.tensor_tensor(oneh[:, :, k, :], eiota[:, :].unsqueeze(1).to_broadcast([P, TB, E]),
                                             topf[:, :, k:k + 1].to_broadcast([P, TB, E]), ALU.is_equal)
                last.then_inc(s["oneh_done"], 1)
                dve.wait_ge(s["oneh_done"], g + 1)
                dve.tensor_reduce(ohnew[:, :], oneh[:, :, :, :].rearrange("p t k e -> p (k e) t"), AX.X,
                                  ALU.add).then_inc(s["ohnew_done"], 1)
                dve.tensor_scalar(sbase[:, :, :], topf[:, :, :], float(SPAN), None, ALU.mult).then_inc(s["sbase_done"], 1)

            def route_rows(b, g, h, at):
                dve.wait_ge(s["rank_done"], g + 1)
                dve.tensor_tensor(rkoh[:, :, :], at[:, P:2 * P].rearrange("p (t e) -> p t e", e=E),
                                  oneh[:, :, :, :].rearrange("p t k e -> p (t k) e"), ALU.mult).then_inc(s["rkoh_done"], 1)
                dve.wait_ge(s["ohnew_done"], g + 1)
                dve.tensor_tensor(ohsum[:, :], ohsum[:, :], ohnew[:, :], ALU.add).then_inc(s["ohsum_done"], 1)
                dve.wait_ge(s["rkoh_done"], g + 1)
                dve.tensor_reduce(rank[:, :, :].rearrange("p t k -> p (t k)"), rkoh[:, :, :], AX.X, ALU.add).then_inc(s["rk_done"], 1)
                dve.wait_ge(s["rk_done"], g + 1)
                dve.tensor_scalar(keep[:, :, :], rank[:, :, :], float(CAP), None, ALU.is_lt)
                dve.tensor_tensor(soff[:, :, :], rank[:, :, :], ksign[:, :, :], ALU.mult).then_inc(s["soff_done"], 1)
                dve.wait_ge(s["sbase_done"], g + 1)
                dve.wait_ge(s["soff_done"], g + 1)
                dve.scalar_tensor_tensor(out=sval[:, :, :], in0=sbase[:, :, :], scalar=float(-UNSENT), in1=soff[:, :, :],
                                         op0=ALU.add, op1=ALU.add).then_inc(s["sval_done"], 1)
                dve.tensor_tensor(wts[:, bass.ds(b * TB * K, TB * K)].rearrange("p (t k) -> p t k", k=K),
                                  topw[:, :, :], keep[:, :, :], ALU.mult)
                dve.wait_ge(s["sval_done"], g + 1)
                dve.tensor_tensor(sgo[:, :, :], sval[:, :, :], kbase[:, :, :], ALU.add).then_inc(s["sgo_done"], 1)
                dve.wait_ge(s["sgo_done"], g + 1)
                dve.tensor_tensor(soff[:, :, :], sgo[:, :, :], keep[:, :, :], ALU.mult).then_inc(s["keep_done"], 1)
                dve.wait_ge(s["keep_done"], g + 1)
                dve.tensor_scalar(sli[h][:, :].rearrange("p (t k) -> p t k", k=K), soff[:, :, :], float(UNSENT), None,
                                  ALU.add).then_inc(s["slots_ready"], 1)
                dve.tensor_copy(expt[:, bass.ds(b * TB * K, TB * K)].rearrange("p (t k) -> p t k", k=K), topf[:, :, :])
                dve.tensor_scalar(sent[:, bass.ds(b * TB * K, TB * K)].rearrange("p (t k) -> p t k", k=K),
                                  soff[:, :, :], float(UNSENT), None, ALU.add).then_inc(s["w_ready"], 1)

            def norm_ffn(b, g, h):
                dve.wait_ge(s["xnf_free"], g + 1)
                norm(b, g, xnf[h], "ffn")

            dve.wait_ge(s["w_in"], 16 * 13)
            with dve.Fori(0, B // 2) as i:
                for h in range(2):
                    b = 2 * i + h
                    dve.wait_ge(s[f"x_in{h}"], 16 * i + 16)
                    norm(b, b, xna, "att")
                    dve.wait_ge(s["einv_ready"], b + 1)
                    dve.scalar_tensor_tensor(out=qT[:, :], in0=bank[4][:, :], scalar=cols[:, 0:1], in1=einv[:, :],
                                             op0=ALU.add, op1=ALU.mult).then_inc(s["qT_ready"], 1)
                    bias = a_kvb[:, :].unsqueeze(1).to_broadcast([P, 2, 2 * D])
                    dve.tensor_tensor(tok[:, 0:2, :], bank[7][:, :].rearrange("p (t n) -> p t n", t=2), bias, ALU.add)
                    dve.tensor_tensor(tok[:, 2:4, :], bank[3][:, :].rearrange("p (t n) -> p t n", t=2), bias,
                                      ALU.add).then_inc(s["tok_ready"], 1)
                    for c in range(TB):
                        if c:
                            dve.wait_ge(s["state_done"], b * (TB - 1) + c)
                            dve.tensor_tensor(stm[c % 2][:, :], bank[2][:, 0:D], block8[:, :], ALU.mult).then_inc(s["stm_ready"], 1)
                        for g in range(NG):
                            dve.wait_ge(s["sc_done"], (b * TB + c) * NG + g + 1)
                            dve.tensor_tensor(pT[c % 2][:, g, :, :], bank[4 + g][:, :].rearrange("p (j t) -> p j t", j=GH),
                                              causal[:, :].unsqueeze(1).to_broadcast([P, GH, P]),
                                              ALU.mult).then_inc(s["pT_ready"], 1)
                    dve.wait_ge(s["bias_added"], b + 1)
                    dve.wait_ge(s["o_done"], b + 1)
                    xb = xs[:, tiles_of(b), :]
                    dve.tensor_tensor(xb, xb, bank[3][:, :].rearrange("p (t d) -> p t d", t=TB), ALU.add).then_inc(s["x1_ready"], 1)
                    dve.wait_ge(s["x1_ready"], b + 1)
                    norm_ffn(b, b, h)
                    route_max(b, bank[2])
                    route_top(b)
                    route_rows(b, b, h, bank[2])

            def tables(layer):
                n = [layer * 17]

                def link(ins):
                    n[0] += 1
                    ins.then_inc(s["tb"], 1)
                    dve.wait_ge(s["tb"], n[0])

                def wide(t):
                    return t[:, :]
                tc = unitcol[:, 0:1].to_broadcast([P, E])
                dve.wait_ge(s["counts_done"], layer + 1)
                link(dve.tensor_scalar(cnt[:, :, :], bank[1][:, 0:K * E].rearrange("p (k e) -> p k e", k=K),
                                       float(CAP), None, ALU.min))
                dve.tensor_tensor(tailf[:, :], ebase[:, :], cnt[:, 1, :], ALU.add)
                link(dve.tensor_tensor(ntok[:, :], cnt[:, 0, :], cnt[:, 1, :], ALU.add))
                link(dve.tensor_tensor(over[:, :, :], ntok[:, :].unsqueeze(2).to_broadcast([P, E, LNMAX]),
                                       mstep[:, :].unsqueeze(1).to_broadcast([P, E, LNMAX]), ALU.is_gt))
                link(dve.tensor_reduce(ntile[:, :], over[:, :, :], AX.X, ALU.add))
                link(dve.tensor_tensor_scan(tend[:, :], ones[:, 0:E], ntile[:, :], 0.0, ALU.mult, ALU.add))
                link(dve.tensor_tensor(tstart[:, :], tend[:, :], ntile[:, :], ALU.subtract))
                dve.tensor_tensor(past[:, :], tc, wide(tend), ALU.is_ge)
                dve.tensor_tensor(reached[:, :], tc, wide(tstart), ALU.is_ge)
                link(dve.scalar_tensor_tensor(out=rowof[:, :], in0=tstart[:, :], scalar=float(-UR), in1=ebase[:, :],
                                              op0=ALU.mult, op1=ALU.add))
                dve.tensor_tensor(here[:, :], reached[:, :], past[:, :], ALU.subtract)
                dve.tensor_reduce(texp[:, :], past[:, :], AX.X, ALU.add)
                link(dve.tensor_tensor(rowof[:, :], rowof[:, :], cnt[:, 0, :], ALU.subtract))
                dve.tensor_reduce(hsum[:, :], here[:, :], AX.X, ALU.add)
                dve.tensor_scalar(texpc[:, :], texp[:, :], float(E - 1), None, ALU.min)
                dve.tensor_scalar(tlin[:, :], unitcol[:, :], float(UR), float(-DUMMY), ALU.mult, ALU.add)
                link(dve.tensor_tensor(toff[:, :], here[:, :], wide(rowof), ALU.mult))
                dve.tensor_reduce(toffs[:, :], toff[:, :], AX.X, ALU.add)
                link(dve.tensor_tensor(tlin2[:, :], tlin[:, :], hsum[:, :], ALU.mult))
                link(dve.scalar_tensor_tensor(out=trow[:, :], in0=tlin2[:, :], scalar=float(DUMMY), in1=toffs[:, :],
                                              op0=ALU.add, op1=ALU.add))
                dve.tensor_copy(tails[0:1, :], tailf[0:1, :]).then_inc(s["tables"], 1)
                dve.wait_ge(s["table_done"], layer + 1)
                dve.tensor_copy(table[0:1, :], bank[1][0:1, 0:2 * UNITS]).then_inc(s["tables"], 1)
                dve.memset(ohsum[:, :], 0.0)
                dve.wait_ge(s["w_ready"], B * (layer + 1))
                link(dve.tensor_tensor(whose[:, :, :], expt[:, :].unsqueeze(2).to_broadcast([P, NT * K, E]),
                                       eiota[:, :].unsqueeze(1).to_broadcast([P, NT * K, E]), ALU.is_equal))
                link(dve.tensor_tensor(whose[:, :, :], whose[:, :, :], rowof[:, :].unsqueeze(1).to_broadcast([P, NT * K, E]),
                                       ALU.mult))
                dve.tensor_scalar(kept[:, :], sent[:, :], float(DUMMY), None, ALU.is_lt)
                link(dve.tensor_reduce(shift[:, :], whose[:, :, :], AX.X, ALU.add))
                link(dve.scalar_tensor_tensor(out=shift[:, :], in0=sent[:, :], scalar=float(-ZROW), in1=shift[:, :],
                                              op0=ALU.add, op1=ALU.subtract))
                link(dve.tensor_tensor(shift[:, :], shift[:, :], kept[:, :], ALU.mult))
                if layer == 0:
                    dve.memset(stackk[0][STACK:P, :, :], 0.0)
                    dve.memset(stackq[0][STACK:P, :, :], 0.0).then_inc(s["zeroed_k"], 1)
                link(dve.tensor_scalar(slots[:, :], shift[:, :], float(ZROW), None, ALU.add))

            def experts(layer):
                base = layer * GROUPS

                def hidden(g, h):
                    dve.wait_ge(s["silu_done"], g + 1 + base)
                    for q in range(2):
                        up = bank[3 + 2 * h + q][:, :].rearrange("p (j n) -> p j n", j=2)[:, :, D:2 * D]
                        last = dve.tensor_tensor(hid[h][:, 2 * q:2 * q + 2, :], sg[h][:, 2 * q:2 * q + 2, :], up, ALU.mult)
                    last.then_inc(s["hid_done"], 1)

                def y_copy(g, h, i):
                    dve.wait_ge(s["y_done"], g + 1 + base)
                    dve.wait_ge(s[f"y_out{h}"], AHEAD + (i + layer * (GROUPS // 2)) * 16)
                    dve.tensor_copy(ye[h][:, :, :].rearrange("p j d -> p (j d)"), bank[7][:, :]).then_inc(s["y_ready"], 1)

                hidden(0, 0)
                hidden(1, 1)
                with dve.Fori(1, GROUPS // 2) as i:
                    for h in range(2):
                        hidden(2 * i + h, h)
                        y_copy(2 * i + h - 2, h, i - 1)
                y_copy(GROUPS - 2, 0, GROUPS // 2 - 1)
                y_copy(GROUPS - 1, 1, GROUPS // 2 - 1)

            def indices(b, h):
                dve.tensor_copy(slg[h][:, :], slots[:, bass.ds(b * TB * K, TB * K)]).then_inc(s["slg_ready"], 1)

            def add_choice(b, h, k, done):
                for j in range(TB):
                    xb = xs[:, b * TB + j, :]
                    last = dve.scalar_tensor_tensor(out=xb, in0=yg[h][:, K * j + k, :],
                                                    scalar=wts[:, bass.ds((b * TB + j) * K + k, 1)], in1=xb,
                                                    op0=ALU.mult, op1=ALU.add)
                last.then_inc(done, 1)

            def add_first(b, h, g):
                dve.wait_ge(s["fetched"], g + 1)
                add_choice(b, h, 0, s["comb0"])

            def add_second(b, h, g):
                dve.wait_ge(s["comb0"], g + 1)
                add_choice(b, h, 1, s["combined"])

            tables(0)
            experts(0)

            dve.wait_ge(s["w_ready"], B)
            dve.wait_ge(s["w_in2"], 16 * 13)
            indices(0, 0)

            def normed(b, h):
                dve.wait_ge(s["combined"], b + 1)
                norm(b, b + B, xna, "att")

            def q_and_v(b, h):
                dve.wait_ge(s["tokproj_done"], b + 1)
                bias = b_qvb[:, :].unsqueeze(1).to_broadcast([P, 2, 2 * D])
                for q in range(2):
                    last = dve.tensor_tensor(toks[h][:, 2 * q:2 * q + 2, :], bank[2 + q][:, :].rearrange("p (t n) -> p t n", t=2),
                                             bias, ALU.add)
                last.then_inc(s["btok_ready"], 1)

            def largest(b, h, n):
                dve.wait_ge(s["bsc_done"], b * PAIRS + n + 1)
                t, m = n // (H // 2), n % (H // 2)
                dve.tensor_reduce(smax[h][:, t, 2 * m:2 * m + 2], pair[n % 2][:, :, :], AX.X, ALU.max).then_inc(s["bmax_done"], 1)

            def top_queries(b):
                dve.wait_ge(s["mT_done"], b + 1)
                dve.tensor_scalar(mT[:, :], bank[0][0:H, :], SCALE, None, ALU.mult).then_inc(s["mTs_done"], 1)
                dve.wait_ge(s["mTs_done"], b + 1)
                settle(dve)
                dve.max(m8[:, :], mT[:, :]).then_inc(s["m8_done"], 1)
                dve.wait_ge(s["m8_done"], b + 1)
                settle(dve)
                dve.max_index(m8i[:, :], m8[:, :], mT[:, :]).then_inc(s["m8i_done"], 1)
                dve.wait_ge(s["m8i_done"], b + 1)
                dve.tensor_copy(m8f[:, 0:TOPU], m8i[:, 0:TOPU]).then_inc(s["m8f_done"], 1)
                dve.wait_ge(s["m8f_done"], b + 1)
                dve.tensor_tensor(idg[:, :, :], headrow[:, :, :], m8f[:, :].unsqueeze(1).to_broadcast([H, H, SLOTU]),
                                  ALU.mult).then_inc(s["idg_done"], 1)

            def selections(b):
                dve.wait_ge(s["idx_done"], b + 1)
                dve.tensor_copy(idc[:, :], bank[1][:, P:P + 1]).then_inc(s["idc_done"], 1)
                dve.tensor_tensor(selT[:, :, :], bank[1][:, 0:P].unsqueeze(1).to_broadcast([P, TB, P]),
                                  tokcol[:, :].unsqueeze(2).to_broadcast([P, TB, P]), ALU.is_equal)
                dve.wait_ge(s["idc_done"], b + 1)
                dve.tensor_scalar(sel[:, :], tokrow[:, :], idc[:, 0:1], None, ALU.is_equal).then_inc(s["sel_done"], 1)

            def selected_q(b):
                dve.wait_ge(s["qsel_done"], b + 1)
                dve.tensor_tensor(qsel[:, :].rearrange("p (h u) -> p h u", h=H), bank[0][:, 0:P].rearrange("p (h u) -> p h u", h=H),
                                  headof[:, :].unsqueeze(2).to_broadcast([P, H, SLOTU]), ALU.mult).then_inc(s["qsel_ready"], 1)

            def selected_max(b):
                dve.wait_ge(s["att_done"], b + 1)
                dve.tensor_reduce(amax[:, :], bank[1][:, :], AX.X, ALU.max).then_inc(s["amax_done"], 1)
                dve.wait_ge(s["amax_done"], b + 1)
                dve.tensor_scalar(aneg[:, :], amax[:, :], -SCALE, None, ALU.mult).then_inc(s["aneg_done"], 1)

            def context(b):
                dve.wait_ge(s["aexp_done"], b + 1)
                dve.reciprocal(ainv[:, :], asum[:, :]).then_inc(s["ainv_done"], 1)
                dve.wait_ge(s["cx_done"], b + 1)
                dve.tensor_tensor(cxm[:, :], bank[1][:, 0:P], block8[:, :], ALU.mult).then_inc(s["cx_ready"], 1)

            def context_out(b):
                dve.wait_ge(s["cw_done"], b + 1)
                dve.wait_ge(s["ainv_done"], b + 1)
                dve.tensor_scalar(cwo[:, :], bank[0][:, 0:D], ainv[:, 0:1], None, ALU.mult).then_inc(s["cw_ready"], 1)

            def residual(b):
                dve.wait_ge(s["bias_added"], b + B + 1)
                dve.wait_ge(s["bo_done"], b + 1)
                xb = xs[:, tiles_of(b), :]
                dve.tensor_tensor(xb, xb, bank[1][:, :].rearrange("p (t d) -> p t d", t=TB), ALU.add).then_inc(s["x1_ready"], 1)
                dve.wait_ge(s["x1_ready"], b + B + 1)

            def body(b, u, h, last=True, next=True, fetch=True):
                for n in range(PAIRS):
                    largest(b, h, n)
                    if fetch and n == 0:
                        indices(b + 2, h)
                    if last and n == 1:
                        top_queries(b - 1)
                    if next and n == 2:
                        add_first(b + 1, 1 - h, b + 1)
                    if next and n == 3:
                        add_second(b + 1, 1 - h, b + 1)
                    if last and n == 4:
                        selections(b - 1)
                    if next and n == 5:
                        normed(b + 1, 1 - h)
                    if last and n == 7:
                        selected_q(b - 1)
                    if last and n == 10:
                        selected_max(b - 1)
                    if last and n == 15:
                        context(b - 1)
                    if last and n == 17:
                        context_out(b - 1)
                    if next and n == 18:
                        q_and_v(b + 1, 1 - h)
                    if last and n == 19:
                        residual(b - 1)
                        norm_ffn(b - 1, b - 1 + B, 1 - h)
                    if last and n == 23:
                        route_max(b - 1 + B, bank[1])
                    if last and n == 25:
                        route_top(b - 1 + B)
                    if last and n == 28:
                        route_rows(b - 1, b - 1 + B, 1 - h, bank[1])

            indices(1, 1)
            add_first(0, 0, 0)
            add_second(0, 0, 0)
            normed(0, 0)
            q_and_v(0, 0)
            each_batch(dve, body)
            b = B - 1
            top_queries(b)
            selections(b)
            selected_q(b)
            selected_max(b)
            context(b)
            context_out(b)
            residual(b)
            norm_ffn(b, b + B, 1)
            route_max(b + B, bank[1])
            route_top(b + B)
            route_rows(b, b + B, 1, bank[1])
            tables(1)
            experts(1)
            dve.wait_ge(s["w_ready"], 2 * B)
            indices(0, 0)
            with dve.Fori(0, B // 2 - 1) as i:
                for h in range(2):
                    indices(2 * i + h + 1, 1 - h)
                    add_first(2 * i + h, h, 2 * i + h + B)
                    add_second(2 * i + h, h, 2 * i + h + B)
            indices(B - 1, 1)
            for h in range(2):
                add_first(B - 2 + h, h, 2 * B - 2 + h)
                add_second(B - 2 + h, h, 2 * B - 2 + h)

        @block.tensor
        def _(pe):
            def turn(n, kind, src, dst=bank[0]):
                pe.wait_ge(s[kind + "_xn_ready"], n + 1)
                for j in range(TB):
                    last = pe.transpose(dst[:, j * P:(j + 1) * P], src[:, j, :], ident[:, :])
                last.then_inc(s[kind + "_tp_done"], 1)

            def logits(g, lg):
                pe.wait_ge(s["ffn_xT_ready"], g + 1)
                for j in range(TB):
                    last = pe.matmul(lg[:, j * E:(j + 1) * E], xfT[:, j * P:(j + 1) * P], rt_w[:, :], start=True, stop=True)
                last.then_inc(s["logits_done"], 1)

            def ranks(g, lg):
                pe.wait_ge(s["oneh_done"], g + 1)
                KE = K * E
                rk = lg[:, P:2 * P]
                pe.matmul(rk.rearrange("p (t n) -> p t n", n=KE), onesb[:, :],
                          ohsum[:, :].unsqueeze(1).to_broadcast([P, TB, KE]), start=True, stop=False)
                for j in range(TB - 1):
                    pe.matmul(lg[:, P + (j + 1) * KE:2 * P].rearrange("p (t n) -> p t n", n=KE), onesb[:, :],
                              oneh[:, j, :, :].rearrange("p k e -> p (k e)").unsqueeze(1).to_broadcast([P, TB - 1 - j, KE]),
                              start=False, stop=False)
                pe.matmul(rk, before[:, :], oneh[:, :, :, :].rearrange("p t k e -> p (t k e)"), start=False,
                          stop=True).then_inc(s["rank_done"], 1)

            pe.wait_ge(s["consts3"], 1)
            pe.wait_ge(s["wnr"], 1)
            pe.wait_ge(s["w_in"], 16 * 13)
            with pe.Fori(0, B // 2) as i:
                for h in range(2):
                    b = 2 * i + h
                    turn(b, "att", xna)
                    pe.wait_ge(s["att_xT_ready"], b + 1)
                    pe.matmul(bank[5][:, :], a_wnr[:, :], xnT[:, :], start=True, stop=True)
                    pe.matmul(bank[4][:, :], a_wq[:, :], xnT[:, :], start=True, stop=True)
                    pe.matmul(bank[6][:, :], a_wk[:, :], xnT[:, :], start=True, stop=True)
                    for j in range(TB):
                        last = pe.matmul(bank[(7, 3)[j // 2]][:, j % 2 * 2 * D:(j % 2 + 1) * 2 * D], xnT[:, j * P:(j + 1) * P],
                                         a_wkv[:, :], start=True, stop=True)
                    last.then_inc(s["proj_done"], 1)
                    pe.wait_ge(s["kT_ready"], b + 1)
                    pe.wait_ge(s["qm_ready"], b + 1)
                    pe.wait_ge(s["tok_ready"], b + 1)

                    def scores(c):
                        for g in range(NG):
                            rows = slice(32 * g, 32 * g + 32)
                            if c:
                                pe.wait_ge(s["pT_ready"], (b * TB + c - 1) * NG + g + 1)
                            pe.matmul(bank[4 + g][:, :].rearrange("p (j t) -> p j t", j=GH), kT[rows, c * P:(c + 1) * P],
                                      qm[rows, :, c * P:(c + 1) * P], start=True, stop=True).then_inc(s["sc_done"], 1)

                    scores(0)
                    for c in range(TB):
                        ct = bank[1][:, c * P:(c + 1) * P]
                        if c + 1 < TB:
                            if c:
                                pe.wait_ge(s["stm_ready"], b * (TB - 1) + c)
                            pe.matmul(bank[2][:, 0:D], tok[:, c, 0:D], tok[:, c, D:2 * D], start=(c == 0), stop=True,
                                      skip_group_check=True).then_inc(s["state_done"], 1)
                            scores(c + 1)
                        if c:
                            pe.wait_ge(s["stm_ready"], b * (TB - 1) + c)
                            pe.matmul(ct, stm[c % 2][:, :], qT[:, c * P:(c + 1) * P], start=True, stop=False, skip_group_check=True)
                        pe.wait_ge(s["pT_ready"], (b * TB + c) * NG + NG)
                        pe.wait_ge(s["vm_ready"], b + 1)
                        for j in range(GH):
                            for g in range(NG):
                                last = pe.matmul(bank[1][32 * g:32 * g + 32, c * P:(c + 1) * P],
                                                 vm[:, c, j * P + 32 * g:j * P + 32 * g + 32], pT[c % 2][:, g, j, :],
                                                 start=(c == 0 and j == 0), stop=(j == GH - 1), skip_group_check=True)
                    last.then_inc(s["ctx_done"], 1)
                    pe.wait_ge(s["ctxT_ready"], b + 1)
                    for j in range(TB):
                        last = pe.matmul(bank[3][:, j * D:(j + 1) * D], ctxT[:, j * P:(j + 1) * P], a_wo[:, :], start=True, stop=True)
                    last.then_inc(s["o_done"], 1)
                    turn(b, "ffn", xnf[h])
                    logits(b, bank[2])
                    ranks(b, bank[2])

            def tables(layer):
                pe.wait_ge(s["ohsum_done"], B * (layer + 1))
                pe.matmul(bank[1][:, 0:K * E], onesb[:, :], ohsum[:, :], start=True, stop=True).then_inc(s["counts_done"], 1)
                pe.wait_ge(s["tb"], 17 * layer + 11)
                for n, src in enumerate((trow, texpc)):
                    last = pe.matmul(bank[1][0:1, n * UNITS:(n + 1) * UNITS], src[:, 0:1], ident[:, 0:UNITS], start=True, stop=True)
                last.then_inc(s["table_done"], 1)

            def experts(layer):
                base = layer * GROUPS
                pe.wait_ge(s["tables"], 2 * (layer + 1))
                pe.wait_ge(s["w_in2"], 16 * 13)

                def turn_x(g, r, i):
                    pe.wait_ge(s[f"xe_in{r}"], (i + 1 + layer * (GROUPS // NX)) * 16 * GU)
                    for j in range(GT):
                        last = pe.transpose(bank[0][:, j * P:(j + 1) * P], xe[r][:, j, :], ident[:, :])
                    last.then_inc(s["xe_tp"], 1)

                def experts_of(g):
                    return [pe.value_load(table[0:1, bass.ds(g * GU + u + UNITS, 1)], min_val=0, max_val=E - 1) for u in range(GU)]

                def gate_up(g, h, ex):
                    pe.wait_ge(s["xeT_ready"], g + 1 + base)
                    for j in range(GT):
                        last = pe.matmul(bank[3 + 2 * h + j // 2][:, j % 2 * 2 * D:(j % 2 + 1) * 2 * D], xeT[h][:, j, :],
                                         gu_w[:, bass.ds(ex[j // UT], 1), :].rearrange("p a n -> p (a n)"), start=True, stop=True)
                    last.then_inc(s["gu_done"], 1)

                def turn_h(g, h):
                    pe.wait_ge(s["hid_done"], g + 1 + base)
                    pe.wait_ge(s["hidT_ready"], g + base + 1)
                    for j in range(GT):
                        last = pe.transpose(bank[1][:, j * P:(j + 1) * P], hid[h][:, j, :], ident[:, :])
                    last.then_inc(s["hid_tp"], 1)

                def down(g, h, ex):
                    pe.wait_ge(s["hidT_ready"], g + 2 + base)
                    pe.wait_ge(s["y_ready"], g + base + 1)
                    for j in range(GT):
                        last = pe.matmul(bank[7][:, j * D:(j + 1) * D], hidT[h][:, j, :],
                                         dn_w[:, bass.ds(ex[j // UT], 1), :].rearrange("p a n -> p (a n)"), start=True, stop=True)
                    last.then_inc(s["y_done"], 1)

                def stage(g, r, i, edge=None):
                    h = r % 2
                    ex = experts_of(g)
                    if edge is None or edge >= 2:
                        done = experts_of(g - 2)
                    gate_up(g, h, ex)
                    if edge is None or edge < GROUPS - 1:
                        turn_x(g + 1, (r + 1) % NX, i + (r + 1) // NX)
                    if edge is None or edge >= 1:
                        turn_h(g - 1, 1 - h)
                    if edge is None or edge >= 2:
                        down(g - 2, h, done)

                turn_x(0, 0, 0)
                for g in range(NX):
                    stage(g, g, 0, g)
                with pe.Fori(1, GROUPS // NX - 1) as i:
                    for r in range(NX):
                        stage(NX * i + r, r, i)
                for g in range(GROUPS - NX, GROUPS):
                    stage(g, g % NX, GROUPS // NX - 1, g)
                down(GROUPS - 2, 0, experts_of(GROUPS - 2))
                turn_h(GROUPS - 1, 1)
                down(GROUPS - 1, 1, experts_of(GROUPS - 1))

            tables(0)
            experts(0)

            def project(n):
                pe.wait_ge(s["att_xT_ready"], n + B + 1)
                pe.matmul(bank[2][:, :], b_wq[:, :], xnT[:, :], start=True, stop=True)
                pe.matmul(bank[3][:, :], b_wk[:, :], xnT[:, :], start=True, stop=True).then_inc(s["bproj_done"], 1)

            def project_tokens(n):
                pe.wait_ge(s["first_parts"], n + 1)
                for j in range(TB):
                    last = pe.matmul(bank[2 + j // 2][:, j % 2 * 2 * D:(j % 2 + 1) * 2 * D], xnT[:, j * P:(j + 1) * P],
                                     b_wqv[:, :], start=True, stop=True)
                last.then_inc(s["tokproj_done"], 1)

            def scores(b, h, n, first):
                t, m = n // (H // 2), n % (H // 2)
                if not (first and n < 2):
                    pe.wait_ge(s["bmax_done"], b * PAIRS + n - 1)
                for q in range(2):
                    last = pe.matmul(pair[n % 2][:, q, :], stackq[h][:, 2 * m + q, t * P:(t + 1) * P], stackk[h][:, 2 * m + q, :],
                                     start=True, stop=True)
                last.then_inc(s["bsc_done"], 1)

            def turn_largest(b, h):
                pe.wait_ge(s["bmax_done"], b * PAIRS + PAIRS)
                for t in range(TB):
                    last = pe.transpose(bank[0][0:H, t * P:(t + 1) * P], smax[h][:, t, :], ident[:, :])
                last.then_inc(s["mT_done"], 1)

            def spread_indices(b):
                pe.wait_ge(s["idg_done"], b + 1)
                idr = idg[:, :, :].rearrange("h a u -> h (a u)")
                pe.matmul(bank[1][:, 0:P], ones[0:H, :], idr, start=True, stop=True)
                pe.matmul(bank[1][:, P:P + 1], idr, ones[0:H, 0:1], start=True, stop=True).then_inc(s["idx_done"], 1)

            def select_q(b, h):
                pe.wait_ge(s["sel_done"], b + 1)
                pe.wait_ge(s["btok_ready"], b + 1)
                for t in range(TB):
                    last = pe.matmul(bank[0][:, 0:P], toks[h][:, t, 0:D], selT[:, t, :], start=(t == 0), stop=(t == TB - 1))
                last.then_inc(s["qsel_done"], 1)

            def selected_scores(b, h):
                pe.wait_ge(s["qsel_ready"], b + 1)
                pe.matmul(bank[1][:, :], qsel[:, :], kTs[h][:, :], start=True, stop=True).then_inc(s["att_done"], 1)

            def turn_exp(b):
                pe.wait_ge(s["aexp_done"], b + 1)
                for t in range(TB):
                    last = pe.transpose(bank[0][:, t * P:(t + 1) * P], aexp[:, t * P:(t + 1) * P], ident[:, :])
                last.then_inc(s["aeT_done"], 1)

            def context(b, h):
                pe.wait_ge(s["aeT_ready"], b + 1)
                for t in range(TB):
                    last = pe.matmul(bank[1][:, 0:P], toks[h][:, t, D:2 * D], aexpT[:, t * P:(t + 1) * P], start=(t == 0), stop=(t == TB - 1))
                last.then_inc(s["cx_done"], 1)

            def context_out(b):
                pe.wait_ge(s["cx_ready"], b + 1)
                pe.matmul(bank[0][:, 0:D], cxm[:, :], b_wo[:, :], start=True, stop=True).then_inc(s["cw_done"], 1)

            def scatter_context(b):
                pe.wait_ge(s["cw_ready"], b + 1)
                for t in range(TB):
                    last = pe.matmul(bank[1][:, t * D:(t + 1) * D], sel[:, t * P:(t + 1) * P], cwo[:, :], start=True, stop=True)
                last.then_inc(s["bo_done"], 1)

            def body(b, u, h, last=True, next=True, fetch=True):
                pe.wait_ge(s[f"stack_in{h}"], (u + 1) * 32 * len(PRODUCTS))
                for n in range(PAIRS):
                    scores(b, h, n, not last)
                    if last and n == 0:
                        turn_largest(b - 1, 1 - h)
                    if last and n == 3:
                        spread_indices(b - 1)
                    if last and n == 6:
                        select_q(b - 1, 1 - h)
                    if next and n == 7:
                        turn(b + 1 + B, "att", xna, bank[2])
                    if last and n == 8:
                        selected_scores(b - 1, 1 - h)
                    if next and n == 9:
                        project(b + 1)
                    if last and n == 12:
                        turn_exp(b - 1)
                    if last and n == 14:
                        context(b - 1, 1 - h)
                    if last and n == 16:
                        context_out(b - 1)
                    if next and n == 16:
                        project_tokens(b + 1)
                    if last and n == 18:
                        scatter_context(b - 1)
                    if last and n == 21:
                        turn(b - 1 + B, "ffn", xnf[1 - h])
                    if last and n == 22:
                        logits(b - 1 + B, bank[1])
                    if last and n == 27:
                        ranks(b - 1 + B, bank[1])

            pe.wait_ge(s["zeroed_k"], 1)
            pe.wait_ge(s["zeroed_q"], 1)
            turn(B, "att", xna, bank[2])
            project(0)
            project_tokens(0)
            each_batch(pe, body)
            b = B - 1
            turn_largest(b, 1)
            spread_indices(b)
            select_q(b, 1)
            selected_scores(b, 1)
            turn_exp(b)
            context(b, 1)
            context_out(b)
            scatter_context(b)
            turn(b + B, "ffn", xnf[1])
            logits(b + B, bank[1])
            ranks(b + B, bank[1])
            tables(1)
            experts(1)


_NAMES = {"x": "L0_attn_a_x", "a_Wqk": "L0_attn_a_Wqk", "a_bqk": "L0_attn_a_bqk", "a_Wv": "L0_attn_a_Wv", "a_bv": "L0_attn_a_bv",
          "a_Wn": "L0_attn_a_Wn", "a_Wo": "L0_attn_a_Wo", "a_bo": "L0_attn_a_bo",
          "b_bv": "L0_attn_b_bv", "b_bo": "L0_attn_b_bo",
          "f_router": "L0_ffn_router_w", "f_gate": "L0_ffn_gate_w", "f_up": "L0_ffn_up_w", "f_down": "L0_ffn_down_w"}
_SPREAD = {"b_wqT": "L0_attn_b_wq", "b_wkT": "L0_attn_b_wk", "b_bq": "L0_attn_b_bq", "b_bk": "L0_attn_b_bk"}
_TURNED = {"b_wvT": "L0_attn_b_wv", "b_woT": "L0_attn_b_wo"}


def kernel(**inputs):
    import numpy as np
    import concourse.bacc as bacc
    from concourse.bass_utils import run_bass_kernel_spmd

    arrays = {n: np.ascontiguousarray(inputs[src]) for n, src in _NAMES.items()}
    for n, src in _TURNED.items():
        arrays[n] = np.ascontiguousarray(np.asarray(inputs[src]).T)
    for n, src in _SPREAD.items():
        a = np.asarray(inputs[src])
        a = np.moveaxis(a.reshape((H, DH) + a.shape[1:]), 0, 1).reshape(a.shape)
        arrays[n] = np.ascontiguousarray(a.T)
    arrays["a_bnr"] = np.repeat(np.asarray(inputs["L0_attn_a_bn"]), DH)
    nc = bacc.Bacc("TRN2", target_bir_lowering=False, num_devices=1)
    w = {n: nc.dram_tensor("in_" + n, a.shape, mybir.dt.from_np(a.dtype), kind="ExternalInput").ap() for n, a in arrays.items()}
    out = nc.dram_tensor("out", (B, SEQ, D), F32, kind="ExternalOutput").ap()
    build(nc, w, out)
    r = run_bass_kernel_spmd(nc, [{"in_" + n: a for n, a in arrays.items()}], core_ids=[0])
    return r.results[0]["out"]
```

```python
from contextlib import ExitStack

import concourse.bass as bass
from concourse import mybir

F32 = mybir.dt.float32
BF16 = mybir.dt.bfloat16
I32 = mybir.dt.int32
U32 = mybir.dt.uint32
ALU = mybir.AluOpType
ACT = mybir.ActivationFunctionType
AX = mybir.AxisListType

P = 128
D = 128
H = 16
DH = D // H
GH = 4
NG = H // GH
E = 16
K = 2
B = 16
SEQ = 512
TB = SEQ // P
T = B * SEQ
NT = T // P
CAP = -(-T * K * 5 // (E * 4))
UT = 2
UR = UT * P
SPAN = K * CAP + UR
UNITS = 80
GU = 2
GT = GU * UT
GROUPS = UNITS // GU
NX = 4
assert UNITS >= T * K // UR + E - 1 and GROUPS % NX == 0
DUMMY = E * SPAN
UNSENT = DUMMY + UR
ZROW = UNITS * UR
TOPU = 6
PARTS = 3
STACK = DH * PARTS * PARTS // 32 * 32
STACK_DMAS = PARTS * (PARTS + 1)
UA = TB * NG
LAG = 3
RING = 3
PAIRS = TB * H // 2
SLOTU = 8
EPS = 1e-5
SCALE = float(DH) ** -0.5
CALLS = B + 3
LNMAX = -(-K * CAP // UR)


def build(nc, w, out):
    ctx = ExitStack()
    with ctx:
        def sb(name, shape, dt=F32):
            return ctx.enter_context(nc.sbuf_tensor(name, shape, dt))

        def pb(name):
            return ctx.enter_context(nc.psum_tensor(name, [P, 512], F32))

        def sem(name):
            return ctx.enter_context(nc.semaphore(name))

        disp = nc.dram_tensor("disp", [DUMMY + UR, D], F32).ap()
        ybuf = nc.dram_tensor("ybuf", [ZROW + P, D], F32).ap()
        qparts = [nc.dram_tensor(f"qparts{h}", [3, P, SEQ], BF16).ap() for h in range(2)]
        kparts = [nc.dram_tensor(f"kparts{h}", [3, P, SEQ], BF16).ap() for h in range(2)]

        xs = sb("xs", [P, NT, D])
        sent = sb("sent", [P, NT * K])
        expt = sb("expt", [P, NT * K])
        slots = sb("slots", [P, NT * K], I32)
        wts = sb("wts", [P, NT * K])
        gu_w = sb("gu_w", [P, E, 2 * D])
        dn_w = sb("dn_w", [P, E, D])
        rt_w = sb("rt_w", [P, E])
        a_wq = sb("a_wq", [P, D])
        a_wk = sb("a_wk", [P, D])
        a_wkv = sb("a_wkv", [P, 2 * D])
        a_wn = sb("a_wn", [P, E])
        a_wnr = sb("a_wnr", [P, D])
        a_wo = sb("a_wo", [P, D])
        b_wq = sb("b_wq", [P, D])
        b_wk = sb("b_wk", [P, D])
        b_wqv = sb("b_wqv", [P, 2 * D])
        b_wo = sb("b_wo", [P, D])
        cols = sb("cols", [P, 6])
        a_kvb = sb("a_kvb", [P, 2 * D])
        b_qvb = sb("b_qvb", [P, 2 * D])
        a_bo = sb("a_bo", [P, D])
        b_bo = sb("b_bo", [P, D])

        ident = sb("ident", [P, P])
        ones = sb("ones", [P, P])
        zeros = sb("zeros", [P, UT * D])
        onesb = sb("onesb", [P, P], BF16)
        before = sb("before", [P, P], BF16)
        causal = sb("causal", [P, P])
        block8 = sb("block8", [P, P])
        headpos = sb("headpos", [P, H, DH])
        headof = sb("headof", [P, H])
        headrow = sb("headrow", [H, H, SLOTU])
        eiota = sb("eiota", [P, E])
        tokcol = sb("tokcol", [P, TB])
        tokrow = sb("tokrow", [P, SEQ])
        unitcol = sb("unitcol", [P, 1])
        mstep = sb("mstep", [P, LNMAX])
        ebase = sb("ebase", [P, E])
        ksign = sb("ksign", [P, TB, K])
        kbase = sb("kbase", [P, TB, K])

        st = sb("st", [P, 2 * TB, 6])
        mv = sb("mv", [P, 2 * TB, 2])
        rstd = sb("rstd", [P, 2 * TB])
        nmr = sb("nmr", [P, 2 * TB])
        lnv = sb("lnv", [P, 2 * TB])
        lnh = sb("lnh", [P, 2 * TB])
        lny = [sb(f"lny{h}", [P, 2 * TB]) for h in range(2)]
        lnt = sb("lnt", [P, 2 * TB])
        lnu = sb("lnu", [P, 2 * TB])
        xna = sb("xna", [P, TB, D])
        xnT = sb("xnT", [P, SEQ])
        xnf = [sb(f"xnf{h}", [P, TB, D]) for h in range(2)]
        xfT = sb("xfT", [P, SEQ])
        lmax = sb("lmax", [P, TB])
        lsub = sb("lsub", [P, TB, E])
        lexp = sb("lexp", [P, TB, E])
        lsum = sb("lsum", [P, TB])
        linv = sb("linv", [P, TB])
        top8 = sb("top8", [P, TB, 8])
        top8i = sb("top8i", [P, TB, 8], U32)
        topf = sb("topf", [P, TB, K])
        topw = sb("topw", [P, TB, K])
        oneh = sb("oneh", [P, TB, K, E], BF16)
        ohnew = sb("ohnew", [P, K * E])
        ohsum = sb("ohsum", [P, K * E], BF16)
        rkoh = sb("rkoh", [P, TB * K, E])
        rank = sb("rank", [P, TB, K])
        keep = sb("keep", [P, TB, K])
        sbase = sb("sbase", [P, TB, K])
        soff = sb("soff", [P, TB, K])
        sval = sb("sval", [P, TB, K])
        sgo = sb("sgo", [P, TB, K])
        sli = [sb(f"sli{h}", [P, TB * K], I32) for h in range(2)]
        slg = [sb(f"slg{h}", [P, TB * K], I32) for h in range(2)]
        vmyg = sb("vmyg", [P, TB * GH * (D + DH)])
        vm = vmyg[:, :].rearrange("p (t x) -> p t x", t=TB)
        yg = [vmyg[:, h * TB * K * D:(h + 1) * TB * K * D].rearrange("p (j d) -> p j d", d=D) for h in range(2)]

        cnt = sb("cnt", [P, K, E])
        ntok = sb("ntok", [P, E])
        over = sb("over", [P, E, LNMAX])
        ntile = sb("ntile", [P, E])
        tend = sb("tend", [P, E])
        tstart = sb("tstart", [P, E])
        rowof = sb("rowof", [P, E])
        past = sb("past", [P, E])
        reached = sb("reached", [P, E])
        here = sb("here", [P, E])
        hsum = sb("hsum", [P, 1])
        texp = sb("texp", [P, 1])
        texpc = sb("texpc", [P, 1])
        toff = sb("toff", [P, E])
        toffs = sb("toffs", [P, 1])
        tlin = sb("tlin", [P, 1])
        tlin2 = sb("tlin2", [P, 1])
        trow = sb("trow", [P, 1])
        shift = sb("shift", [P, NT * K])
        kept = sb("kept", [P, NT * K])
        tailf = sb("tailf", [P, E])
        table = sb("table", [1, 2 * UNITS], I32)
        tails = sb("tails", [1, E], I32)
        part = [sb(f"part{x}", [P, 3, SEQ], BF16) for x in "qk"]
        restq = sb("restq", [P, SEQ])
        restk = sb("restk", [P, SEQ])
        stackq = [sb(f"stackq{h}", [P, H, SEQ], BF16) for h in range(2)]
        stackk = [sb(f"stackk{h}", [P, H, SEQ], BF16) for h in range(2)]

        def carve(t, width, shapes):
            flat = t[:, :, :].rearrange("p h t -> p (h t)").bitcast(F32)
            at, views = 0, []
            for n, shape in enumerate(shapes):
                size = 1
                for x in shape:
                    size *= x
                v = flat[:, at:at + size]
                if len(shape) == 2:
                    v = v.rearrange("p (a b) -> p a b", a=shape[0])
                if len(shape) == 3:
                    v = v.rearrange("p (a b c) -> p a b c", a=shape[0], b=shape[1])
                views.append(v)
                at += size
            assert at <= width
            return views
        whose, = carve(stackk[0], H * SEQ // 2, [(NT * K, E)])
        xe = carve(stackq[1], H * SEQ // 2, [(GT, D)] * NX)
        xeT = carve(stackq[1], H * SEQ // 2, [(NX * GT, D)] + [(GT, D)] * 2)[1:]
        sg = carve(stackq[1], H * SEQ // 2, [((NX + 2) * GT, D)] + [(GT, D)] * 2)[1:]
        hid, hidT, ye = (carve(stackk[1], H * SEQ // 2, [(max(1, 2 * n * GT), D)] + [(GT, D)] * 2)[1:] if n else
                         carve(stackk[1], H * SEQ // 2, [(GT, D)] * 2) for n in range(3))
        einv = sb("einv", [P, SEQ])
        qTs = [sb(f"qT{h}", [P, SEQ]) for h in range(2)]
        qT = qTs[0]
        kTs = [sb(f"kT{h}", [P, SEQ]) for h in range(2)]
        pT = [sb(f"pT{n}", [P, GH, P]) for n in range(4)]
        selT, sel, aexp, aexpT = pT[0], *(t[:, :, :].rearrange("p a b -> p (a b)") for t in pT[1:])
        toks = [sb(f"tok{h}", [P, TB, 2 * D]) for h in range(2)]
        VSTEP = D + DH
        stm = [sb(f"stm{h}", [P, D]) for h in range(2)]
        ctxT = sb("ctxT", [P, SEQ])
        smax = [sb(f"smax{h}", [P, TB, H]) for h in range(2)]
        mT = sb("mT", [H, SEQ])
        m8 = sb("m8", [H, SLOTU])
        m8i = sb("m8i", [H, SLOTU], U32)
        m8f = sb("m8f", [H, SLOTU])
        idg = sb("idg", [H, H, SLOTU])
        idc = sb("idc", [P, 1])
        qsel = sb("qsel", [P, P])
        amax = sb("amax", [P, 1])
        aneg = sb("aneg", [P, 1])
        asum = sb("asum", [P, 1])
        ainv = sb("ainv", [P, 1])
        cxm = sb("cxm", [P, P])
        cwo = sb("cwo", [P, D])

        pair = [ctx.enter_context(nc.psum_tensor(f"pair{i}", [P, 2, 512], F32)) for i in range(RING)]
        bank = [pb(f"bank{i}") for i in range(2)] + [pair[i // 2][:, i % 2, :] for i in range(2 * RING)]

        names = ("w_in w_in2 stacks_zero vm_zero consts1 consts2 consts3 ms0 ms1 wnr x_in0 x_in1 bias_added " + " ".join(f"{k}_{n}" for k in ("att", "ffn") for n in "xn_ready tp_done xT_ready".split()) + " stats moments rs rstd_ready "
                 ""
                 "x1_ready logits_done lmax_done lsub_done lexp_done lsum_done linv_done top_done topi_done topf_done oneh_done "
                 "rank_done rkoh_done rk_done ohnew_done ohsum_done keep_done sbase_done soff_done sval_done sgo_done slots_ready "
                 "w_ready sent0 sent1 counts_done tb table_done tables zeroed stored_all "
                 "xe_in0 xe_in1 xe_tp xeT_ready gu_done silu_done hid_done hid_tp hidT_ready y_done y_ready xe_in2 xe_in3 y_out0 y_out1 "
                 "slg_ready got0 got1 comb0 combined "
                 "zeroed_k zeroed_q n_done q_done k_done kv_done einv_ready qT_ready kT_ready tok_ready vm_ready pv_done sc_done pT_ready state_done stm_ready ctxT_ready o_done "
                 "bproj_done tokproj_done btok_ready first_parts second_parts q_parts selrow_done rest_ready third_parts parts_out0 parts_out1 stack_in0 stack_in1 bsc_done bmax_done mT_done mTs_done m8_done m8i_done m8f_done idg_done "
                 "idx_done idc_done sel_done qsel_done qsel_ready att_done amax_done aneg_done aexp_done aeT_done aeT_ready cx_done cx_ready "
                 "cw_done ainv_done cw_ready bo_done x_out settled xnf_free fetched")
        s = {n: sem(n) for n in names.split()}

        block = ctx.enter_context(nc.Block())

        def tiles_of(b):
            return bass.ds(b * TB, TB)

        x_b = w["x"].rearrange("b (t p) d -> b p t d", p=P)
        out_b = out.rearrange("b (t p) d -> b p t d", p=P)
        WLOADS = 20

        def settle(eng):
            eng.sem_inc(s["settled"], 1)

        AHEAD = 16

        def each_batch(eng, body):
            body(0, 0, 0, last=False)
            with eng.Fori(0, B // 2 - 2) as i:
                body(2 * i + 1, i, 1)
                body(2 * i + 2, i + 1, 0)
            body(B - 3, B // 2 - 2, 1)
            body(B - 2, B // 2 - 1, 0, fetch=False)
            body(B - 1, B // 2 - 1, 1, next=False, fetch=False)

        def clear_tails(eng, layer, experts):
            eng.wait_ge(s["tables"], 2 * layer + 1)
            for e in experts:
                row = eng.value_load(tails[0:1, e:e + 1], min_val=0, max_val=DUMMY - UR)
                eng.dma_start(disp[bass.ds(row, UR), :].rearrange("(p a) d -> p (a d)", a=UT),
                              zeros[:, :]).then_inc(s["zeroed"], 16)

        @block.sync
        def _(sp):
            for h in range(2):
                sp.sem_inc(s[f"y_out{h}"], AHEAD)
            for dst, src in ((a_wq[:, :], w["a_Wqk"][:, 0:D]), (a_wk[:, :], w["a_Wqk"][:, D:2 * D]),
                             (a_wkv[:, 0:D], w["a_Wqk"][:, D:2 * D]), (a_wkv[:, D:2 * D], w["a_Wv"]),
                             (a_wn[:, :], w["a_Wn"]), (a_wo[:, :], w["a_Wo"]),
                             (cols[:, 0:1], w["a_bqk"][0:D].rearrange("(p a) -> p a", a=1)),
                             (cols[:, 1:2], w["a_bqk"][D:2 * D].rearrange("(p a) -> p a", a=1)),
                             (cols[:, 5:6], w["a_bnr"].rearrange("(p a) -> p a", a=1)),
                             (a_kvb[:, 0:D], w["a_bqk"][D:2 * D].rearrange("(a n) -> a n", a=1).to_broadcast([P, D])),
                             (a_kvb[:, D:2 * D], w["a_bv"].rearrange("(a n) -> a n", a=1).to_broadcast([P, D])),
                             (a_bo[:, :], w["a_bo"].rearrange("(a n) -> a n", a=1).to_broadcast([P, D])),
                             (rt_w[:, :], w["f_router"])):
                sp.dma_start(dst, src).then_inc(s["w_in"], 16)
            for h in range(2):
                sp.dma_start(xs[:, tiles_of(h), :], x_b[h]).then_inc(s[f"x_in{h}"], 16)

            def stacks(n, i, h):
                sp.wait_ge(s["third_parts"], n + 1)
                for dst, src in ((qparts[h], part[0]), (kparts[h], part[1])):
                    sp.dma_start(dst.rearrange("c p t -> p c t"), src[:, :, :]).then_inc(s[f"parts_out{h}"], 16)
                sp.wait_ge(s[f"parts_out{h}"], (i + 1) * 32)
                for c in range(PARTS):
                    for m in range(PARTS * c, PARTS * (c + 1)):
                        sp.dma_start(stackq[h][m * DH:(m + 1) * DH, :, :], qparts[h][c].rearrange("(d h) t -> d h t", h=H)).then_inc(
                            s[f"stack_in{h}"], 16)
                    sp.dma_start(stackk[h][PARTS * c * DH:PARTS * (c + 1) * DH, :, :],
                                 kparts[h].rearrange("c (d h) t -> (c d) h t", h=H)).then_inc(s[f"stack_in{h}"], 16)

            def x_ahead(i, h):
                sp.wait_ge(s[f"x_in{h}"], (i + 1) * 16)
                sp.dma_start(xs[:, tiles_of(2 * i + 2 + h), :], x_b[2 * i + 2 + h]).then_inc(s[f"x_in{h}"], 16)

            for h in range(2):
                stacks(h, 0, h)
                x_ahead(0, h)
            for dst, src in ((gu_w[:, :, 0:D], w["f_gate"].rearrange("e d h -> d e h")),
                             (gu_w[:, :, D:2 * D], w["f_up"].rearrange("e d h -> d e h")),
                             (dn_w[:, :, :], w["f_down"].rearrange("e d h -> d e h")),
                             (b_wq[:, :], w["b_wqT"]), (b_wk[:, :], w["b_wkT"]),
                             (b_wqv[:, 0:D], w["b_wqT"]), (b_wqv[:, D:2 * D], w["b_wvT"]), (b_wo[:, :], w["b_woT"]),
                             (cols[:, 3:4], w["b_bq"].rearrange("(p a) -> p a", a=1)),
                             (cols[:, 4:5], w["b_bk"].rearrange("(p a) -> p a", a=1)),
                             (b_qvb[:, 0:D], w["b_bq"].rearrange("(a n) -> a n", a=1).to_broadcast([P, D])),
                             (b_qvb[:, D:2 * D], w["b_bv"].rearrange("(a n) -> a n", a=1).to_broadcast([P, D])),
                             (b_bo[:, :], w["b_bo"].rearrange("(a n) -> a n", a=1).to_broadcast([P, D]))):
                sp.dma_start(dst, src).then_inc(s["w_in2"], 16)
            with sp.Fori(1, B // 2 - 1) as i:
                for h in range(2):
                    stacks(2 * i + h, i, h)
                    x_ahead(i, h)
            for h in range(2):
                stacks(B - 2 + h, B // 2 - 1, h)
            sp.wait_ge(s["consts1"], 1)
            sp.dma_start(disp[DUMMY:DUMMY + UR, :].rearrange("(p a) d -> p (a d)", a=UT), zeros[:, :]).then_inc(s["zeroed"], 16)
            sp.dma_start(ybuf[ZROW:ZROW + P, :], zeros[:, 0:D]).then_inc(s["zeroed"], 16)

            def experts(layer):
                clear_tails(sp, layer, range(E // 2))
                sp.wait_ge(s["tables"], 2 * (layer + 1))
                sp.wait_ge(s["zeroed"], 16 * (2 + E * (layer + 1)))
                for h in range(2):
                    sp.wait_ge(s[f"sent{h}"], 16 * TB * K * (B // 2) * (layer + 1))

                def load(g, r):
                    rows = nc.values_load_multi_w_load_instructions(
                        table[0:1, bass.ds(g * GU, GU)], engines=[mybir.EngineType.SP], min_val=0, max_val=DUMMY)[1]
                    for u in range(GU):
                        sp.dma_start(xe[r][:, UT * u:UT * (u + 1), :], disp[bass.ds(rows[u], UR), :].rearrange(
                            "(p a) d -> p a d", a=UT)).then_inc(s[f"xe_in{r}"], 16)

                def reload(g, r):
                    sp.wait_ge(s["xe_tp"], g + 1 + layer * GROUPS)
                    load(g + NX, r)

                def store(g, h):
                    sp.wait_ge(s["y_ready"], g + 2 + layer * GROUPS)
                    sp.dma_start(ybuf[bass.ds(g * (GT * P), GT * P), :].rearrange("(u p a) d -> p u (a d)", p=P, a=UT),
                                 ye[h][:, :, :].rearrange("p (u a) d -> p u (a d)", a=UT)).then_inc(s[f"y_out{h}"], 16)

                for r in range(NX):
                    load(r, r)
                reload(0, 0)
                reload(1, 1)
                for r in (2, 3):
                    reload(r, r)
                    store(r - 2, r % 2)
                with sp.Fori(1, GROUPS // NX - 1) as i:
                    for r in range(NX):
                        reload(NX * i + r, r)
                        store(NX * i + r - 2, r % 2)
                for g in range(GROUPS - NX - 2, GROUPS):
                    store(g, g % 2)
                for h in range(2):
                    sp.wait_ge(s[f"y_out{h}"], AHEAD + 16 * (GROUPS // 2) * (layer + 1))
                sp.sem_inc(s["stored_all"], 1)

            experts(0)
            with sp.Fori(0, B // 2) as i:
                for h in range(2):
                    stacks(B + 2 * i + h, i + B // 2, h)
            experts(1)
            with sp.Fori(0, B) as i:
                sp.wait_ge(s["combined"], i + 1 + B)
                sp.dma_start(out_b[i], xs[:, tiles_of(i), :]).then_inc(s["x_out"], 16)
            sp.wait_ge(s["x_out"], 16 * B)

        @block.gpsimd
        def _(pool):
            pool.sem_inc(s["xnf_free"], 2)
            pool.memset(ident[:, :], 0.0)
            pool.memset(ones[:, :], 1.0)
            pool.memset(onesb[:, :], 1.0)
            pool.memset(zeros[:, :], 0.0).then_inc(s["consts1"], 1)
            pool.memset(block8[:, :], 1.0)
            pool.memset(causal[:, :], 1.0)
            pool.memset(before[:, :], 1.0)
            pool.memset(headrow[:, :, :], 0.0)
            pool.memset(headpos[:, :, :], 0.0)
            pool.memset(ohsum[:, :], 0.0)
            pool.memset(vmyg[:, :], 0.0).then_inc(s["vm_zero"], 1)
            pool.memset(m8f[:, :], -1.0)
            for k in range(K):
                pool.memset(ksign[:, :, k], 2.0 * k - 1.0)
                pool.memset(kbase[:, :, k], float(CAP - 1 + k)).then_inc(s["ms0"], 1)
            pool.wait_ge(s["ms0"], K)
            pool.affine_select(out=ident[:, :], in_=ident[:, :], compare_op=ALU.not_equal, fill=1.0, base=0,
                               pattern=[[-1, P]], channel_multiplier=1)
            pool.affine_select(out=causal[:, :], in_=causal[:, :], compare_op=ALU.is_ge, fill=0.0, base=0,
                               pattern=[[1, P]], channel_multiplier=-1)
            pool.affine_select(out=before[:, :], in_=before[:, :], compare_op=ALU.is_ge, fill=0.0, base=-1,
                               pattern=[[1, P]], channel_multiplier=-1)
            pool.affine_select(out=headrow[:, :, :], in_=headrow[:, :, :], compare_op=ALU.not_equal, fill=1.0, base=0,
                               pattern=[[-1, H], [0, SLOTU]], channel_multiplier=1)
            pool.affine_select(out=headpos[:, :, :], in_=headpos[:, :, :], compare_op=ALU.not_equal, fill=1.0, base=0,
                               pattern=[[-1, H], [-H, DH]], channel_multiplier=1)
            bv = block8[:, :].rearrange("p (h d) -> p h d", d=DH)
            pool.affine_select(out=bv, in_=bv, compare_op=ALU.is_ge, fill=0.0, base=0,
                               pattern=[[-DH, H], [0, DH]], channel_multiplier=1).then_inc(s["ms1"], 1)
            pool.wait_ge(s["ms1"], 1)
            pool.affine_select(out=bv, in_=bv, compare_op=ALU.is_ge, fill=0.0, base=DH - 1,
                               pattern=[[DH, H], [0, DH]], channel_multiplier=-1)

            def iota(t, base, pattern, cm):
                return pool.iota(t, base=base, pattern=pattern, channel_multiplier=cm,
                                 allow_small_or_imprecise_dtypes=True)
            iota(eiota[:, :], 0, [[1, E]], 0)
            iota(tokcol[:, :], 0, [[P, TB]], 1)
            iota(tokrow[:, :], 0, [[1, SEQ]], 0)
            iota(unitcol[:, :], 0, [[1, 1]], 1)
            iota(mstep[:, :], 0, [[UR, LNMAX]], 0)
            iota(ebase[:, :], CAP, [[SPAN, E]], 0).then_inc(s["consts2"], 1)

            def send(g, i, h):
                pool.wait_ge(s["slots_ready"], g + 1)
                settle(pool)
                for j in range(TB):
                    for k in range(K):
                        pool.indirect_dma_start(
                            out=disp, out_offset=bass.IndirectOffsetOnAxis(ap=sli[h][:, K * j + k:K * j + k + 1], axis=0),
                            in_=xnf[h][:, j, :], in_offset=None, bounds_check=DUMMY - 1, oob_is_err=False,
                        ).then_inc(s[f"sent{h}"], 16)
                pool.wait_ge(s[f"sent{h}"], (i + 1) * 16 * TB * K)
                pool.sem_inc(s["xnf_free"], 1)

            def fetch(g, h):
                pool.wait_ge(s["slg_ready"], g + 1)
                settle(pool)
                for j in range(TB * K):
                    pool.indirect_dma_start(
                        out=yg[h][:, j, :], out_offset=None, in_=ybuf,
                        in_offset=bass.IndirectOffsetOnAxis(ap=slg[h][:, j:j + 1], axis=0),
                    ).then_inc(s[f"got{h}"], 16)

            def fetched(i, h):
                pool.wait_ge(s[f"got{h}"], (i + 1) * 16 * TB * K)
                pool.sem_inc(s["fetched"], 1)

            def add_bias(b, g, row):
                pool.wait_ge(s["att_xn_ready"], g + 1)
                settle(pool)
                xb = xs[:, tiles_of(b), :]
                pool.tensor_tensor(xb, xb, row[:, :].unsqueeze(1).to_broadcast([P, TB, D]), ALU.add).then_inc(s["bias_added"], 1)

            pool.wait_ge(s["w_in"], 16 * 13)

            def rests(n, k, q):
                pool.wait_ge(s["first_parts"], n + 1)
                settle(pool)
                pool.tensor_tensor(restq[:, :], qTs[q][:, :], part[0][:, 0, :], ALU.subtract)
                pool.tensor_tensor(restk[:, :], kTs[k][:, :], part[1][:, 0, :], ALU.subtract).then_inc(s["rest_ready"], 1)
                pool.wait_ge(s["second_parts"], n + 1)
                settle(pool)
                pool.tensor_tensor(part[0][:, 2, :], restq[:, :], part[0][:, 1, :], ALU.subtract)
                pool.tensor_tensor(part[1][:, 2, :], restk[:, :], part[1][:, 1, :], ALU.subtract).then_inc(s["third_parts"], 1)

            def masked_v(b, h, c, first=False):
                pool.wait_ge(s["tok_ready"], 2 * b + 2)
                if not first:
                    pool.wait_ge(s["pv_done"], (b - 1) * UA + GH * (c + 1))
                settle(pool)
                dst = vm[:, c, :].rearrange("p (j x) -> p j x", x=VSTEP)[:, :, 0:D].rearrange(
                    "p j (g y) -> p j g y", y=GH * DH)[:, :, :, 0:DH]
                src = toks[h][:, c, D:2 * D].rearrange("p (g j d) -> p j g d", g=NG, j=GH)
                pool.tensor_copy(dst, src).then_inc(s["vm_ready"], 1)

            def attention_a(b, u, h, last=True, next=True, fetch=True):
                if next:
                    rests(b + 1, 0, 1 - h)
                    for c in range(TB - 1):
                        masked_v(b + 1, 1 - h, c)
                add_bias(b, b, a_bo)
                if last:
                    send(b - 1, u + h - 1, 1 - h)
                if next:
                    masked_v(b + 1, 1 - h, TB - 1)

            rests(0, 0, 0)
            pool.wait_ge(s["vm_zero"], 1)
            for c in range(TB):
                masked_v(0, 0, c, True)
            each_batch(pool, attention_a)
            send(B - 1, B // 2 - 1, 1)
            pool.wait_ge(s["w_in2"], 16 * 13)
            pool.wait_ge(s["stored_all"], 1)
            fetch(0, 0)
            fetched(0, 0)
            fetch(1, 1)
            pool.memset(stackk[1][STACK:P, :, :], 0.0)
            pool.memset(stackq[1][STACK:P, :, :], 0.0).then_inc(s["zeroed_q"], 1)
            fetched(0, 1)

            def selected_rows(b):
                pool.wait_ge(s["idc_done"], b + 1)
                settle(pool)
                pool.tensor_scalar(sel[:, :], tokrow[:, :], idc[:, 0:1], None, ALU.is_equal).then_inc(s["selrow_done"], 1)

            def body(b, u, h, last=True, next=True, fetch_=True):
                if fetch_:
                    fetch(b + 2, h)
                if last:
                    selected_rows(b - 1)
                if next:
                    rests(b + 1 + B, 1 - h, 0)
                if fetch_:
                    fetched(u + 1, h)
                add_bias(b, b + B, b_bo)
                if last:
                    send(b - 1 + B, u + h - 1 + B // 2, 1 - h)

            rests(B, 0, 0)
            each_batch(pool, lambda b, u, h, last=True, next=True, fetch=True: body(b, u, h, last, next, fetch))
            selected_rows(B - 1)
            send(2 * B - 1, B - 1, 1)
            pool.wait_ge(s["stored_all"], 2)
            fetch(B, 0)
            with pool.Fori(0, B // 2 - 1) as i:
                for h in range(2):
                    fetch(2 * i + h + 1 + B, 1 - h)
                    fetched(i + B // 2, h)
            fetch(2 * B - 1, 1)
            for h in range(2):
                fetched(B - 1, h)

        @block.scalar
        def _(act):
            act.sem_inc(s["hidT_ready"], 1)
            act.wait_ge(s["w_in"], 16 * 13)
            act.activation(a_wnr[:, :].rearrange("p (d h) -> p d h", h=H),
                           a_wn[:, :].unsqueeze(1).to_broadcast([P, DH, H]), ACT.Copy).then_inc(s["wnr"], 1)
            act.activation(cols[:, 2:3], cols[:, 5:6], ACT.Copy, scale=-1.0).then_inc(s["wnr"], 1)
            act.wait_ge(s["wnr"], 2)

            def turned(n, kind, dst, src=bank[0]):
                act.wait_ge(s[kind + "_tp_done"], n + 1)
                act.activation(dst[:, :], src[:, :], ACT.Copy).then_inc(s[kind + "_xT_ready"], 1)

            def apply_norm(b, n, dst, kind, q, call):
                act.wait_ge(s["rstd_ready"], call + 1)
                if kind == "ffn":
                    act.wait_ge(s["xnf_free"], n + 1)
                for j in range(TB):
                    at = q * TB + j
                    last = act.activation(dst[:, j, :], xs[:, b * TB + j, :], ACT.Identity, bias=nmr[:, at:at + 1],
                                          scale=rstd[:, at:at + 1])
                last.then_inc(s[kind + "_xn_ready"], 1)

            def route_exp(g):
                act.wait_ge(s["lsub_done"], g + 1)
                act.activation(lexp[:, :, :], lsub[:, :, :], ACT.Exp).then_inc(s["lexp_done"], 1)

            act.wait_ge(s["consts3"], 1)
            def second_parts(n):
                act.wait_ge(s["rest_ready"], n + 1)
                act.activation(part[0][:, 1, :], restq[:, :], ACT.Copy)
                act.activation(part[1][:, 1, :], restk[:, :], ACT.Copy).then_inc(s["second_parts"], 1)

            def front_a(b, h):
                turned(b, "att", xnT, bank[3])
                act.wait_ge(s["n_done"], b + 1)
                act.activation(einv[:, :], bank[3][:, :], ACT.Exp, bias=cols[:, 2:3], scale=-1.0).then_inc(s["einv_ready"], 1)
                act.wait_ge(s["k_done"], b + 1)
                act.activation(kTs[0][:, :], bank[3][:, :], ACT.Identity, bias=cols[:, 1:2])
                act.activation(part[1][:, 0, :], bank[3][:, :], ACT.Identity, bias=cols[:, 1:2]).then_inc(s["kT_ready"], 1)
                act.wait_ge(s["qT_ready"], b + 1)
                act.activation(part[0][:, 0, :], qTs[h][:, :], ACT.Copy).then_inc(s["first_parts"], 1)
                second_parts(b)

            def context_a(b):
                act.wait_ge(s["pv_done"], b * UA + UA)
                act.activation(ctxT[:, :], bank[1][:, :], ACT.Copy).then_inc(s["ctxT_ready"], 1)

            def attention_a(b, u, h, last=True, next=True, fetch=True):
                if next:
                    front_a(b + 1, 1 - h)
                if last:
                    apply_norm(b - 1, b - 1, xnf[1 - h], "ffn", 0, b + 2)
                if fetch:
                    apply_norm(b + 2, b + 2, xna, "att", int(last), b + 2)
                if last:
                    turned(b - 1, "ffn", xfT)
                    route_exp(b - 1)
                context_a(b)

            apply_norm(0, 0, xna, "att", 0, 0)
            front_a(0, 0)
            apply_norm(1, 1, xna, "att", 0, 1)
            each_batch(act, attention_a)
            apply_norm(B - 1, B - 1, xnf[1], "ffn", 0, B + 2)
            turned(B - 1, "ffn", xfT)
            route_exp(B - 1)

            def experts(layer):
                base = layer * GROUPS

                def xT(g, h):
                    act.wait_ge(s["xe_tp"], g + 1 + base)
                    act.activation(xeT[h][:, :, :].rearrange("p j d -> p (j d)"), bank[0][:, :], ACT.Copy).then_inc(s["xeT_ready"], 1)

                def silu(g, h):
                    act.wait_ge(s["gu_done"], g + 1 + base)
                    for q in range(2):
                        src = bank[3 + 2 * h + q][:, :].rearrange("p (j n) -> p j n", j=2)[:, :, 0:D]
                        last = act.activation(sg[h][:, 2 * q:2 * q + 2, :], src, ACT.Silu)
                    last.then_inc(s["silu_done"], 1)

                def hT(g, h):
                    act.wait_ge(s["hid_tp"], g + 1 + base)
                    act.activation(hidT[h][:, :, :].rearrange("p j d -> p (j d)"), bank[1][:, :], ACT.Copy).then_inc(s["hidT_ready"], 1)

                clear_tails(act, layer, range(E // 2, E))
                xT(0, 0)
                silu(0, 0)
                xT(1, 1)
                silu(1, 1)
                xT(2, 0)
                hT(0, 0)
                with act.Fori(1, GROUPS // 2 - 1) as i:
                    for h in range(2):
                        silu(2 * i + h, h)
                        xT(2 * i + h + 1, 1 - h)
                        hT(2 * i + h - 1, 1 - h)
                silu(GROUPS - 2, 0)
                xT(GROUPS - 1, 1)
                hT(GROUPS - 3, 1)
                silu(GROUPS - 1, 1)
                hT(GROUPS - 2, 0)
                hT(GROUPS - 1, 1)

            experts(0)
            act.wait_ge(s["w_in2"], 16 * 13)
            def first_parts(n, k):
                act.wait_ge(s["bproj_done"], 2 * n + 1)
                act.activation(qT[:, :], bank[0][:, :], ACT.Identity, bias=cols[:, 3:4])
                act.activation(part[0][:, 0, :], bank[0][:, :], ACT.Identity, bias=cols[:, 3:4]).then_inc(s["q_parts"], 1)
                act.wait_ge(s["bproj_done"], 2 * n + 2)
                act.activation(kTs[k][:, :], bank[0][:, :], ACT.Identity, bias=cols[:, 4:5])
                act.activation(part[1][:, 0, :], bank[0][:, :], ACT.Identity, bias=cols[:, 4:5]).then_inc(s["first_parts"], 1)

            def selected_exp(b):
                act.wait_ge(s["aneg_done"], b + 1)
                act.activation(aexp[:, :], bank[1][:, :], ACT.Exp, bias=aneg[:, 0:1], scale=SCALE,
                               accum_out=asum[:, 0:1]).then_inc(s["aexp_done"], 1)

            def largest(b):
                act.wait_ge(s["mT_done"], b + 1)
                act.activation(mT[:, :], bank[0][0:H, :], ACT.Copy, scale=SCALE).then_inc(s["mTs_done"], 1)

            def turned_exp(b):
                act.wait_ge(s["aeT_done"], b + 1)
                act.activation(aexpT[:, :], bank[1][:, :], ACT.Copy).then_inc(s["aeT_ready"], 1)

            def finish(b):
                turned(b + B, "ffn", xfT)
                route_exp(b + B)

            def body(b, u, h, last=True, next=True, fetch=True):
                if last:
                    largest(b - 1)
                if next:
                    turned(b + 1 + B, "att", xnT)
                    first_parts(b + 1, 1 - h)
                if last:
                    selected_exp(b - 1)
                    turned_exp(b - 1)
                if next:
                    second_parts(b + 1 + B)
                if last:
                    apply_norm(b - 1, b - 1 + B, xnf[1 - h], "ffn", 0, b + 2 + CALLS)
                if fetch:
                    apply_norm(b + 2, b + 2 + B, xna, "att", int(last), b + 2 + CALLS)
                if last:
                    finish(b - 1)

            apply_norm(0, B, xna, "att", 0, CALLS)
            turned(B, "att", xnT)
            first_parts(0, 0)
            second_parts(B)
            apply_norm(1, B + 1, xna, "att", 0, CALLS + 1)
            each_batch(act, body)
            largest(B - 1)
            selected_exp(B - 1)
            turned_exp(B - 1)
            apply_norm(B - 1, 2 * B - 1, xnf[1], "ffn", 0, B + 2 + CALLS)
            finish(B - 1)
            experts(1)

        @block.vector
        def _(dve):
            dve.sem_inc(s["y_ready"], 1)
            dve.sem_inc(s["rk_done"], 1)
            for t in (*stackq, *stackk):
                last = dve.memset(t[STACK:P, :, :], 0.0)
            last.then_inc(s["stacks_zero"], 1)
            dve.wait_ge(s["consts2"], 1)
            dve.tensor_reduce(headof[:, :], headpos[:, :, :], AX.X, ALU.add).then_inc(s["consts3"], 1)

            def row_stats(call, batches):
                settle(dve)
                for q, b in enumerate(batches):
                    for j in range(TB):
                        last = dve.bn_stats(st[:, q * TB + j, :], xs[:, b * TB + j, :])
                last.then_inc(s["stats"], 1)

            def row_moments(call, W):
                dve.wait_ge(s["stats"], call + 1)
                settle(dve)
                for j in range(W):
                    last = dve.bn_aggr(mv[:, j, :], st[:, j, :])
                last.then_inc(s["moments"], 1)
                dve.wait_ge(s["moments"], call + 1)
                dve.tensor_scalar(lnv[:, 0:W], mv[:, 0:W, 1], EPS, None, ALU.add).then_inc(s["rs"], 1)
                dve.tensor_scalar(lnh[:, 0:W], mv[:, 0:W, 1], EPS, -0.5, ALU.add, ALU.mult)
                dve.wait_ge(s["rs"], call * 11 + 1)
                dve.tensor_scalar(lny[0][:, 0:W].bitcast(I32), lnv[:, 0:W].bitcast(I32), -0.5, float(0x5f3759df),
                                  ALU.mult, ALU.add).then_inc(s["rs"], 1)

            def newton(call, W, steps):
                for r in steps:
                    y, z = lny[r % 2], (lny[1 - r % 2] if r < 2 else rstd)
                    dve.wait_ge(s["rs"], call * 11 + 2 + 3 * r)
                    dve.tensor_tensor(lnt[:, 0:W], y[:, 0:W], y[:, 0:W], ALU.mult).then_inc(s["rs"], 1)
                    dve.wait_ge(s["rs"], call * 11 + 3 + 3 * r)
                    dve.tensor_tensor(lnu[:, 0:W], lnt[:, 0:W], lnh[:, 0:W], ALU.mult).then_inc(s["rs"], 1)
                    dve.wait_ge(s["rs"], call * 11 + 4 + 3 * r)
                    dve.scalar_tensor_tensor(out=z[:, 0:W], in0=lnu[:, 0:W], scalar=1.5, in1=y[:, 0:W],
                                             op0=ALU.add, op1=ALU.mult).then_inc(s["rs"], 1)

            def row_shift(call, W):
                dve.wait_ge(s["rs"], call * 11 + 11)
                dve.scalar_tensor_tensor(out=nmr[:, 0:W], in0=mv[:, 0:W, 0], scalar=-1.0, in1=rstd[:, 0:W],
                                         op0=ALU.mult, op1=ALU.mult).then_inc(s["rstd_ready"], 1)

            def norm(call, *batches, parts=range(5)):
                W = len(batches) * TB
                if 0 in parts:
                    row_stats(call, batches)
                if 1 in parts:
                    row_moments(call, W)
                if 2 in parts:
                    newton(call, W, (0,))
                if 3 in parts:
                    newton(call, W, (1,))
                if 4 in parts:
                    newton(call, W, (2,))
                    row_shift(call, W)

            def route_max(g, at):
                lg = at[:, 0:TB * E].rearrange("p (t e) -> p t e", e=E)
                dve.wait_ge(s["logits_done"], g + 1)
                dve.tensor_reduce(lmax[:, :], lg, AX.X, ALU.max).then_inc(s["lmax_done"], 1)
                dve.wait_ge(s["lmax_done"], g + 1)
                dve.tensor_tensor(lsub[:, :, :], lg, lmax[:, :].unsqueeze(2).to_broadcast([P, TB, E]),
                                  ALU.subtract).then_inc(s["lsub_done"], 1)

            def route_top(g):
                dve.wait_ge(s["lexp_done"], g + 1)
                settle(dve)
                for j in range(TB):
                    last = dve.max(top8[:, j, :], lexp[:, j, :])
                last.then_inc(s["top_done"], 1)
                dve.tensor_reduce(lsum[:, :], lexp[:, :, :], AX.X, ALU.add).then_inc(s["lsum_done"], 1)
                dve.wait_ge(s["top_done"], g + 1)
                settle(dve)
                for j in range(TB):
                    last = dve.max_index(top8i[:, j, :], top8[:, j, :], lexp[:, j, :])
                last.then_inc(s["topi_done"], 1)
                dve.wait_ge(s["lsum_done"], g + 1)
                dve.reciprocal(linv[:, :], lsum[:, :]).then_inc(s["linv_done"], 1)
                dve.wait_ge(s["topi_done"], g + 1)
                dve.tensor_copy(topf[:, :, :], top8i[:, :, 0:K]).then_inc(s["topf_done"], 1)
                dve.wait_ge(s["linv_done"], g + 1)
                dve.tensor_tensor(topw[:, :, :], top8[:, :, 0:K], linv[:, :].unsqueeze(2).to_broadcast([P, TB, K]), ALU.mult)
                dve.wait_ge(s["topf_done"], g + 1)
                for k in range(K):
                    last = dve.tensor_tensor(oneh[:, :, k, :], eiota[:, :].unsqueeze(1).to_broadcast([P, TB, E]),
                                             topf[:, :, k:k + 1].to_broadcast([P, TB, E]), ALU.is_equal)
                last.then_inc(s["oneh_done"], 1)
                dve.wait_ge(s["oneh_done"], g + 1)
                dve.tensor_reduce(ohnew[:, :], oneh[:, :, :, :].rearrange("p t k e -> p (k e) t"), AX.X,
                                  ALU.add).then_inc(s["ohnew_done"], 1)
                dve.tensor_scalar(sbase[:, :, :], topf[:, :, :], float(SPAN), None, ALU.mult).then_inc(s["sbase_done"], 1)

            def route_rows(b, g, h, at):
                dve.wait_ge(s["rank_done"], g + 1)
                dve.tensor_tensor(rkoh[:, :, :], at[:, P:2 * P].rearrange("p (t e) -> p t e", e=E),
                                  oneh[:, :, :, :].rearrange("p t k e -> p (t k) e"), ALU.mult).then_inc(s["rkoh_done"], 1)
                dve.wait_ge(s["ohnew_done"], g + 1)
                dve.tensor_tensor(ohsum[:, :], ohsum[:, :], ohnew[:, :], ALU.add).then_inc(s["ohsum_done"], 1)
                dve.wait_ge(s["rkoh_done"], g + 1)
                dve.tensor_reduce(rank[:, :, :].rearrange("p t k -> p (t k)"), rkoh[:, :, :], AX.X, ALU.add).then_inc(s["rk_done"], 1)
                dve.wait_ge(s["rk_done"], g + 2)
                dve.tensor_scalar(keep[:, :, :], rank[:, :, :], float(CAP), None, ALU.is_lt)
                dve.tensor_tensor(soff[:, :, :], rank[:, :, :], ksign[:, :, :], ALU.mult).then_inc(s["soff_done"], 1)
                dve.wait_ge(s["sbase_done"], g + 1)
                dve.wait_ge(s["soff_done"], g + 1)
                dve.scalar_tensor_tensor(out=sval[:, :, :], in0=sbase[:, :, :], scalar=float(-UNSENT), in1=soff[:, :, :],
                                         op0=ALU.add, op1=ALU.add).then_inc(s["sval_done"], 1)
                dve.tensor_tensor(wts[:, bass.ds(b * TB * K, TB * K)].rearrange("p (t k) -> p t k", k=K),
                                  topw[:, :, :], keep[:, :, :], ALU.mult)
                dve.wait_ge(s["sval_done"], g + 1)
                dve.tensor_tensor(sgo[:, :, :], sval[:, :, :], kbase[:, :, :], ALU.add).then_inc(s["sgo_done"], 1)
                dve.wait_ge(s["sgo_done"], g + 1)
                dve.tensor_tensor(soff[:, :, :], sgo[:, :, :], keep[:, :, :], ALU.mult).then_inc(s["keep_done"], 1)
                dve.wait_ge(s["keep_done"], g + 1)
                dve.tensor_scalar(sli[h][:, :].rearrange("p (t k) -> p t k", k=K), soff[:, :, :], float(UNSENT), None,
                                  ALU.add).then_inc(s["slots_ready"], 1)
                dve.tensor_copy(expt[:, bass.ds(b * TB * K, TB * K)].rearrange("p (t k) -> p t k", k=K), topf[:, :, :])
                dve.tensor_scalar(sent[:, bass.ds(b * TB * K, TB * K)].rearrange("p (t k) -> p t k", k=K),
                                  soff[:, :, :], float(UNSENT), None, ALU.add).then_inc(s["w_ready"], 1)

            dve.wait_ge(s["w_in"], 16 * 13)

            def scaled_q(b, h):
                dve.wait_ge(s["einv_ready"], b + 1)
                dve.wait_ge(s["q_done"], b + 1)
                dve.scalar_tensor_tensor(out=qTs[h][:, :], in0=bank[0][:, :], scalar=cols[:, 0:1], in1=einv[:, :],
                                         op0=ALU.add, op1=ALU.mult).then_inc(s["qT_ready"], 1)

            def k_and_v(b, h, half):
                dve.wait_ge(s["kv_done"], 2 * b + half + 1)
                dve.tensor_tensor(toks[h][:, 2 * half:2 * half + 2, :], bank[3][:, :].rearrange("p (t n) -> p t n", t=2),
                                  a_kvb[:, :].unsqueeze(1).to_broadcast([P, 2, 2 * D]), ALU.add).then_inc(s["tok_ready"], 1)

            def masked_scores(b, n, first):
                if not (first and n < 4):
                    dve.wait_ge(s["pv_done"], b * UA + n - 3)
                dve.wait_ge(s["sc_done"], b * UA + n + 1)
                dve.tensor_tensor(pT[n % 4][:, :, :], bank[4 + n % 4].rearrange("p (j t) -> p j t", j=GH),
                                  causal[:, :].unsqueeze(1).to_broadcast([P, GH, P]), ALU.mult).then_inc(s["pT_ready"], 1)

            def masked_state(b, c):
                dve.wait_ge(s["state_done"], b * (TB - 1) + c + 1)
                dve.tensor_tensor(stm[c % 2][:, :].rearrange("p (h d) -> p h d", h=H),
                                  bank[2][:, 0:D].rearrange("p (h d) -> p h d", h=H),
                                  headof[:, :].unsqueeze(2).to_broadcast([P, H, DH]), ALU.mult).then_inc(s["stm_ready"], 1)

            def residual_a(b):
                dve.wait_ge(s["bias_added"], b + 1)
                dve.wait_ge(s["o_done"], b + 1)
                xb = xs[:, tiles_of(b), :]
                dve.tensor_tensor(xb, xb, bank[0][:, :].rearrange("p (t d) -> p t d", t=TB), ALU.add).then_inc(s["x1_ready"], 1)
                dve.wait_ge(s["x1_ready"], b + 1)

            def attention_a(b, u, h, last=True, next=True, fetch=True):
                for n in range(UA):
                    masked_scores(b, n, not last)
                    if n % NG == 2 and n // NG < TB - 1:
                        masked_state(b, n // NG)
                    if next and n == 2:
                        scaled_q(b + 1, 1 - h)
                    if last and n == 4:
                        residual_a(b - 1)
                    if fetch and n == 4:
                        dve.wait_ge(s[f"x_in{h}"], 16 * (u + 2))
                    if 4 <= n < 9:
                        norm(b + 2, *([b - 1] if last else []), *([b + 2] if fetch else []), parts=(n - 4,))
                    if next and n == 6:
                        k_and_v(b + 1, 1 - h, 0)
                    if next and n == 11:
                        k_and_v(b + 1, 1 - h, 1)
                    if last and n == 12:
                        route_max(b - 1, bank[0])
                    if last and n == 13:
                        route_top(b - 1)
                    if last and n == 15:
                        route_rows(b - 1, b - 1, 1 - h, bank[0])

            dve.wait_ge(s["x_in0"], 16)
            norm(0, 0)
            scaled_q(0, 0)
            for half in range(2):
                k_and_v(0, 0, half)
            dve.wait_ge(s["x_in1"], 16)
            norm(1, 1)
            each_batch(dve, attention_a)
            b = B - 1
            residual_a(b)
            norm(B + 2, b)
            route_max(b, bank[0])
            route_top(b)
            route_rows(b, b, 1, bank[0])

            def tables(layer):
                n = [layer * 17]

                def link(ins):
                    n[0] += 1
                    ins.then_inc(s["tb"], 1)
                    dve.wait_ge(s["tb"], n[0])

                def wide(t):
                    return t[:, :]
                tc = unitcol[:, 0:1].to_broadcast([P, E])
                dve.wait_ge(s["counts_done"], layer + 1)
                link(dve.tensor_scalar(cnt[:, :, :], bank[1][:, 0:K * E].rearrange("p (k e) -> p k e", k=K),
                                       float(CAP), None, ALU.min))
                dve.tensor_tensor(tailf[:, :], ebase[:, :], cnt[:, 1, :], ALU.add)
                link(dve.tensor_tensor(ntok[:, :], cnt[:, 0, :], cnt[:, 1, :], ALU.add))
                link(dve.tensor_tensor(over[:, :, :], ntok[:, :].unsqueeze(2).to_broadcast([P, E, LNMAX]),
                                       mstep[:, :].unsqueeze(1).to_broadcast([P, E, LNMAX]), ALU.is_gt))
                dve.tensor_copy(tails[0:1, :], tailf[0:1, :]).then_inc(s["tables"], 1)
                link(dve.tensor_reduce(ntile[:, :], over[:, :, :], AX.X, ALU.add))
                link(dve.tensor_tensor_scan(tend[:, :], ones[:, 0:E], ntile[:, :], 0.0, ALU.mult, ALU.add))
                link(dve.tensor_tensor(tstart[:, :], tend[:, :], ntile[:, :], ALU.subtract))
                dve.tensor_tensor(past[:, :], tc, wide(tend), ALU.is_ge)
                dve.tensor_tensor(reached[:, :], tc, wide(tstart), ALU.is_ge)
                link(dve.scalar_tensor_tensor(out=rowof[:, :], in0=tstart[:, :], scalar=float(-UR), in1=ebase[:, :],
                                              op0=ALU.mult, op1=ALU.add))
                dve.tensor_tensor(here[:, :], reached[:, :], past[:, :], ALU.subtract)
                dve.tensor_reduce(texp[:, :], past[:, :], AX.X, ALU.add)
                link(dve.tensor_tensor(rowof[:, :], rowof[:, :], cnt[:, 0, :], ALU.subtract))
                dve.tensor_reduce(hsum[:, :], here[:, :], AX.X, ALU.add)
                dve.tensor_scalar(texpc[:, :], texp[:, :], float(E - 1), None, ALU.min)
                dve.tensor_scalar(tlin[:, :], unitcol[:, :], float(UR), float(-DUMMY), ALU.mult, ALU.add)
                link(dve.tensor_tensor(toff[:, :], here[:, :], wide(rowof), ALU.mult))
                dve.tensor_reduce(toffs[:, :], toff[:, :], AX.X, ALU.add)
                link(dve.tensor_tensor(tlin2[:, :], tlin[:, :], hsum[:, :], ALU.mult))
                link(dve.scalar_tensor_tensor(out=trow[:, :], in0=tlin2[:, :], scalar=float(DUMMY), in1=toffs[:, :],
                                              op0=ALU.add, op1=ALU.add))
                dve.wait_ge(s["table_done"], layer + 1)
                dve.tensor_copy(table[0:1, :], bank[1][0:1, 0:2 * UNITS]).then_inc(s["tables"], 1)
                dve.memset(ohsum[:, :], 0.0)
                dve.wait_ge(s["w_ready"], B * (layer + 1))
                link(dve.tensor_tensor(whose[:, :, :], expt[:, :].unsqueeze(2).to_broadcast([P, NT * K, E]),
                                       eiota[:, :].unsqueeze(1).to_broadcast([P, NT * K, E]), ALU.is_equal))
                link(dve.tensor_tensor(whose[:, :, :], whose[:, :, :], rowof[:, :].unsqueeze(1).to_broadcast([P, NT * K, E]),
                                       ALU.mult))
                dve.tensor_scalar(kept[:, :], sent[:, :], float(DUMMY), None, ALU.is_lt)
                link(dve.tensor_reduce(shift[:, :], whose[:, :, :], AX.X, ALU.add))
                link(dve.scalar_tensor_tensor(out=shift[:, :], in0=sent[:, :], scalar=float(-ZROW), in1=shift[:, :],
                                              op0=ALU.add, op1=ALU.subtract))
                link(dve.tensor_tensor(shift[:, :], shift[:, :], kept[:, :], ALU.mult))
                if layer == 0:
                    dve.memset(stackk[0][STACK:P, :, :], 0.0).then_inc(s["zeroed_k"], 1)
                link(dve.tensor_scalar(slots[:, :], shift[:, :], float(ZROW), None, ALU.add))

            def experts(layer):
                base = layer * GROUPS

                def hidden(g, h):
                    dve.wait_ge(s["silu_done"], g + 1 + base)
                    for q in range(2):
                        up = bank[3 + 2 * h + q][:, :].rearrange("p (j n) -> p j n", j=2)[:, :, D:2 * D]
                        last = dve.tensor_tensor(hid[h][:, 2 * q:2 * q + 2, :], sg[h][:, 2 * q:2 * q + 2, :], up, ALU.mult)
                    last.then_inc(s["hid_done"], 1)

                def y_copy(g, h, i):
                    dve.wait_ge(s["y_done"], g + 1 + base)
                    dve.wait_ge(s[f"y_out{h}"], AHEAD + (i + layer * (GROUPS // 2)) * 16)
                    dve.tensor_copy(ye[h][:, :, :].rearrange("p j d -> p (j d)"), bank[7][:, :]).then_inc(s["y_ready"], 1)

                hidden(0, 0)
                hidden(1, 1)
                with dve.Fori(1, GROUPS // 2) as i:
                    for h in range(2):
                        hidden(2 * i + h, h)
                        y_copy(2 * i + h - 2, h, i - 1)
                y_copy(GROUPS - 2, 0, GROUPS // 2 - 1)
                y_copy(GROUPS - 1, 1, GROUPS // 2 - 1)

            def indices(b, h):
                dve.tensor_copy(slg[h][:, :], slots[:, bass.ds(b * TB * K, TB * K)]).then_inc(s["slg_ready"], 1)

            def add_choice(b, h, k, done):
                for j in range(TB):
                    xb = xs[:, b * TB + j, :]
                    last = dve.scalar_tensor_tensor(out=xb, in0=yg[h][:, K * j + k, :],
                                                    scalar=wts[:, bass.ds((b * TB + j) * K + k, 1)], in1=xb,
                                                    op0=ALU.mult, op1=ALU.add)
                last.then_inc(done, 1)

            def add_first(b, h, g):
                dve.wait_ge(s["fetched"], g + 1)
                add_choice(b, h, 0, s["comb0"])

            def add_second(b, h, g):
                dve.wait_ge(s["comb0"], g + 1)
                add_choice(b, h, 1, s["combined"])

            tables(0)
            experts(0)

            dve.wait_ge(s["w_ready"], B)
            dve.wait_ge(s["w_in2"], 16 * 13)
            indices(0, 0)

            def q_and_v(b, h, half):
                dve.wait_ge(s["tokproj_done"], 2 * b + half + 1)
                dve.tensor_tensor(toks[h][:, 2 * half:2 * half + 2, :], bank[0][:, :].rearrange("p (t n) -> p t n", t=2),
                                  b_qvb[:, :].unsqueeze(1).to_broadcast([P, 2, 2 * D]), ALU.add).then_inc(s["btok_ready"], 1)

            def largest(b, h, n):
                dve.wait_ge(s["bsc_done"], b * PAIRS + n + 1)
                t, m = n // (H // 2), n % (H // 2)
                dve.tensor_reduce(smax[h][:, t, 2 * m:2 * m + 2], pair[n % RING][:, :, :], AX.X, ALU.max).then_inc(s["bmax_done"], 1)

            def top_queries(b):
                dve.wait_ge(s["mTs_done"], b + 1)
                settle(dve)
                dve.max(m8[:, :], mT[:, :]).then_inc(s["m8_done"], 1)
                dve.wait_ge(s["m8_done"], b + 1)
                settle(dve)
                dve.max_index(m8i[:, :], m8[:, :], mT[:, :]).then_inc(s["m8i_done"], 1)
                dve.wait_ge(s["m8i_done"], b + 1)
                dve.tensor_copy(m8f[:, 0:TOPU], m8i[:, 0:TOPU]).then_inc(s["m8f_done"], 1)
                dve.wait_ge(s["m8f_done"], b + 1)
                dve.tensor_tensor(idg[:, :, :], headrow[:, :, :], m8f[:, :].unsqueeze(1).to_broadcast([H, H, SLOTU]),
                                  ALU.mult).then_inc(s["idg_done"], 1)

            def selections(b):
                dve.wait_ge(s["idx_done"], b + 1)
                dve.tensor_copy(idc[:, :], bank[1][:, P:P + 1]).then_inc(s["idc_done"], 1)
                dve.tensor_tensor(selT[:, :, :], bank[1][:, 0:P].unsqueeze(1).to_broadcast([P, TB, P]),
                                  tokcol[:, :].unsqueeze(2).to_broadcast([P, TB, P]), ALU.is_equal).then_inc(s["sel_done"], 1)

            def selected_q(b):
                dve.wait_ge(s["qsel_done"], b + 1)
                dve.tensor_tensor(qsel[:, :].rearrange("p (h u) -> p h u", h=H), bank[1][:, 0:P].rearrange("p (h u) -> p h u", h=H),
                                  headof[:, :].unsqueeze(2).to_broadcast([P, H, SLOTU]), ALU.mult).then_inc(s["qsel_ready"], 1)

            def selected_max(b):
                dve.wait_ge(s["att_done"], b + 1)
                dve.tensor_reduce(amax[:, :], bank[1][:, :], AX.X, ALU.max).then_inc(s["amax_done"], 1)
                dve.wait_ge(s["amax_done"], b + 1)
                dve.tensor_scalar(aneg[:, :], amax[:, :], -SCALE, None, ALU.mult).then_inc(s["aneg_done"], 1)

            def context(b):
                dve.wait_ge(s["aexp_done"], b + 1)
                dve.reciprocal(ainv[:, :], asum[:, :]).then_inc(s["ainv_done"], 1)
                dve.wait_ge(s["cx_done"], b + 1)
                dve.tensor_tensor(cxm[:, :], bank[1][:, 0:P], block8[:, :], ALU.mult).then_inc(s["cx_ready"], 1)

            def context_out(b):
                dve.wait_ge(s["cw_done"], b + 1)
                dve.wait_ge(s["ainv_done"], b + 1)
                dve.tensor_scalar(cwo[:, :], bank[1][:, 0:D], ainv[:, 0:1], None, ALU.mult).then_inc(s["cw_ready"], 1)

            def residual(b):
                dve.wait_ge(s["bias_added"], b + B + 1)
                dve.wait_ge(s["bo_done"], b + 1)
                xb = xs[:, tiles_of(b), :]
                dve.tensor_tensor(xb, xb, bank[1][:, :].rearrange("p (t d) -> p t d", t=TB), ALU.add).then_inc(s["x1_ready"], 1)
                dve.wait_ge(s["x1_ready"], b + B + 1)

            def body(b, u, h, last=True, next=True, fetch=True):
                for n in range(PAIRS):
                    largest(b, h, n)
                    if fetch and n == 0:
                        indices(b + 2, h)
                    if last and n == 2:
                        top_queries(b - 1)
                    if last and n == 4:
                        selections(b - 1)
                    if last and n == 7:
                        selected_q(b - 1)
                    if last and n == 10:
                        selected_max(b - 1)
                    if last and n == 14:
                        context(b - 1)
                    if next and n == 15:
                        q_and_v(b + 1, 1 - h, 0)
                    if last and n == 17:
                        context_out(b - 1)
                    if fetch and n == 18:
                        add_first(b + 2, h, b + 2)
                    if next and n == 18:
                        q_and_v(b + 1, 1 - h, 1)
                    if fetch and n == 19:
                        add_second(b + 2, h, b + 2)
                    if last and n == 20:
                        residual(b - 1)
                    if fetch and n == 20:
                        dve.wait_ge(s["combined"], b + 3)
                    if 20 <= n < 24:
                        norm(b + 2 + CALLS, *([b - 1] if last else []), *([b + 2] if fetch else []),
                             parts=((0,), (1,), (2,), (3, 4))[n - 20])
                    if last and n == 27:
                        route_max(b - 1 + B, bank[1])
                    if last and n == 28:
                        route_top(b - 1 + B)
                    if last and n == 31:
                        route_rows(b - 1, b - 1 + B, 1 - h, bank[1])

            indices(1, 1)
            add_first(0, 0, 0)
            add_second(0, 0, 0)
            dve.wait_ge(s["combined"], 1)
            norm(CALLS, 0)
            add_first(1, 1, 1)
            add_second(1, 1, 1)
            for half in range(2):
                q_and_v(0, 0, half)
            dve.wait_ge(s["combined"], 2)
            norm(CALLS + 1, 1)
            each_batch(dve, body)
            b = B - 1
            top_queries(b)
            selections(b)
            selected_q(b)
            selected_max(b)
            context(b)
            context_out(b)
            residual(b)
            norm(B + 2 + CALLS, b)
            route_max(b + B, bank[1])
            route_top(b + B)
            route_rows(b, b + B, 1, bank[1])
            tables(1)
            experts(1)
            dve.wait_ge(s["w_ready"], 2 * B)
            indices(0, 0)
            with dve.Fori(0, B // 2 - 1) as i:
                for h in range(2):
                    indices(2 * i + h + 1, 1 - h)
                    add_first(2 * i + h, h, 2 * i + h + B)
                    add_second(2 * i + h, h, 2 * i + h + B)
            indices(B - 1, 1)
            for h in range(2):
                add_first(B - 2 + h, h, 2 * B - 2 + h)
                add_second(B - 2 + h, h, 2 * B - 2 + h)

        @block.tensor
        def _(pe):
            def turn(n, kind, src, dst=bank[0]):
                pe.wait_ge(s[kind + "_xn_ready"], n + 1)
                for j in range(TB):
                    last = pe.transpose(dst[:, j * P:(j + 1) * P], src[:, j, :], ident[:, :])
                last.then_inc(s[kind + "_tp_done"], 1)

            def logits(g, lg):
                pe.wait_ge(s["ffn_xT_ready"], g + 1)
                for j in range(TB):
                    last = pe.matmul(lg[:, j * E:(j + 1) * E], xfT[:, j * P:(j + 1) * P], rt_w[:, :], start=True, stop=True)
                last.then_inc(s["logits_done"], 1)

            def ranks(g, lg):
                pe.wait_ge(s["oneh_done"], g + 1)
                KE = K * E
                rk = lg[:, P:2 * P]
                pe.matmul(rk.rearrange("p (t n) -> p t n", n=KE), onesb[:, :],
                          ohsum[:, :].unsqueeze(1).to_broadcast([P, TB, KE]), start=True, stop=False)
                for j in range(TB - 1):
                    pe.matmul(lg[:, P + (j + 1) * KE:2 * P].rearrange("p (t n) -> p t n", n=KE), onesb[:, :],
                              oneh[:, j, :, :].rearrange("p k e -> p (k e)").unsqueeze(1).to_broadcast([P, TB - 1 - j, KE]),
                              start=False, stop=False)
                pe.matmul(rk, before[:, :], oneh[:, :, :, :].rearrange("p t k e -> p (t k e)"), start=False,
                          stop=True).then_inc(s["rank_done"], 1)

            pe.wait_ge(s["consts3"], 1)
            pe.wait_ge(s["wnr"], 1)
            pe.wait_ge(s["w_in"], 16 * 13)
            pe.wait_ge(s["stacks_zero"], 1)

            def project_nq(b, first=False):
                pe.wait_ge(s["att_xT_ready"], b + 1)
                pe.matmul(bank[3][:, :], a_wnr[:, :], xnT[:, :], start=True, stop=True).then_inc(s["n_done"], 1)
                if not first:
                    pe.wait_ge(s["rk_done"], b - 1)
                pe.matmul(bank[0][:, :], a_wq[:, :], xnT[:, :], start=True, stop=True).then_inc(s["q_done"], 1)

            def project_k(b):
                pe.wait_ge(s["einv_ready"], b + 1)
                pe.matmul(bank[3][:, :], a_wk[:, :], xnT[:, :], start=True, stop=True).then_inc(s["k_done"], 1)

            def project_kv(b, half):
                if half:
                    pe.wait_ge(s["tok_ready"], 2 * b + 1)
                else:
                    pe.wait_ge(s["kT_ready"], b + 1)
                for j in range(2):
                    t = 2 * half + j
                    last = pe.matmul(bank[3][:, j * 2 * D:(j + 1) * 2 * D], xnT[:, t * P:(t + 1) * P], a_wkv[:, :],
                                     start=True, stop=True)
                last.then_inc(s["kv_done"], 1)

            def scores_a(b, h, n, first):
                c, g = n // NG, n % NG
                if not (first and n < 4):
                    pe.wait_ge(s["pT_ready"], b * UA + n - 3)
                for j in range(GH):
                    last = pe.matmul(bank[4 + n % 4][:, j * P:(j + 1) * P], stackk[h][:, GH * g + j, c * P:(c + 1) * P],
                                     stackq[h][:, GH * g + j, c * P:(c + 1) * P], start=True, stop=True)
                last.then_inc(s["sc_done"], 1)

            def state(b, h, c):
                if c:
                    pe.wait_ge(s["stm_ready"], b * (TB - 1) + c)
                else:
                    pe.wait_ge(s["tok_ready"], 2 * b + 2)
                pe.matmul(bank[2][:, 0:D], toks[h][:, c, 0:D], toks[h][:, c, D:2 * D], start=(c == 0), stop=True,
                          skip_group_check=True).then_inc(s["state_done"], 1)

            def values(b, h, n):
                c, g = n // NG, n % NG
                if g == 0 and c:
                    pe.wait_ge(s["stm_ready"], b * (TB - 1) + c)
                    pe.matmul(bank[1][:, c * P:(c + 1) * P], stm[(c - 1) % 2][:, :], qTs[h][:, c * P:(c + 1) * P],
                              start=True, stop=False, skip_group_check=True)
                pe.wait_ge(s["pT_ready"], b * UA + n + 1)
                pe.wait_ge(s["vm_ready"], b * TB + c + 1)
                for j in range(GH):
                    last = pe.matmul(bank[1][32 * g:32 * g + 32, c * P:(c + 1) * P],
                                     vm[:, c, j * P + 32 * g:j * P + 32 * g + 32], pT[n % 4][:, j, :],
                                     start=(c == 0 and j == 0), stop=(j == GH - 1), skip_group_check=True)
                last.then_inc(s["pv_done"], 1)

            def out_a(b):
                pe.wait_ge(s["ctxT_ready"], b + 1)
                pe.wait_ge(s["rk_done"], b + 1)
                for j in range(TB):
                    last = pe.matmul(bank[0][:, j * D:(j + 1) * D], ctxT[:, j * P:(j + 1) * P], a_wo[:, :], start=True, stop=True)
                last.then_inc(s["o_done"], 1)

            def attention_a(b, u, h, last=True, next=True, fetch=True):
                pe.wait_ge(s[f"stack_in{h}"], (u + 1) * 16 * STACK_DMAS)
                for n in range(UA):
                    scores_a(b, h, n, not last)
                    if next and n == 0:
                        turn(b + 1, "att", xna, bank[3])
                    if next and n == 1:
                        project_nq(b + 1, not last)
                    if next and n == 2:
                        project_k(b + 1)
                    if n == LAG and last:
                        pe.wait_ge(s["ctxT_ready"], b)
                    if n >= LAG:
                        values(b, h, n - LAG)
                    if n % NG == 1 and n // NG < TB - 1:
                        state(b, h, n // NG)
                    if last and n == 3:
                        if next:
                            pe.wait_ge(s["qT_ready"], b + 2)
                        out_a(b - 1)
                    if next and n == 5:
                        project_kv(b + 1, 0)
                    if next and n == 10:
                        project_kv(b + 1, 1)
                    if last and n == 11:
                        turn(b - 1, "ffn", xnf[1 - h])
                    if last and n == 12:
                        logits(b - 1, bank[0])
                for n in range(UA - LAG, UA):
                    values(b, h, n)
                    if last and n == UA - 2:
                        ranks(b - 1, bank[0])

            turn(0, "att", xna, bank[3])
            project_nq(0, True)
            project_k(0)
            for half in range(2):
                project_kv(0, half)
            each_batch(pe, attention_a)
            b = B - 1
            out_a(b)
            turn(b, "ffn", xnf[1])
            logits(b, bank[0])
            ranks(b, bank[0])

            def tables(layer):
                pe.wait_ge(s["ohsum_done"], B * (layer + 1))
                pe.matmul(bank[1][:, 0:K * E], onesb[:, :], ohsum[:, :], start=True, stop=True).then_inc(s["counts_done"], 1)
                pe.wait_ge(s["tb"], 17 * layer + 11)
                for n, src in enumerate((trow, texpc)):
                    last = pe.matmul(bank[1][0:1, n * UNITS:(n + 1) * UNITS], src[:, 0:1], ident[:, 0:UNITS], start=True, stop=True)
                last.then_inc(s["table_done"], 1)

            def experts(layer):
                base = layer * GROUPS
                pe.wait_ge(s["tables"], 2 * (layer + 1))
                pe.wait_ge(s["w_in2"], 16 * 13)

                def turn_x(g, r, i):
                    pe.wait_ge(s[f"xe_in{r}"], (i + 1 + layer * (GROUPS // NX)) * 16 * GU)
                    for j in range(GT):
                        last = pe.transpose(bank[0][:, j * P:(j + 1) * P], xe[r][:, j, :], ident[:, :])
                    last.then_inc(s["xe_tp"], 1)

                def experts_of(g):
                    return nc.values_load_multi_w_load_instructions(
                        table[0:1, bass.ds(g * GU + UNITS, GU)], engines=[mybir.EngineType.PE], min_val=0, max_val=E - 1)[1]

                def gate_up(g, h, ex):
                    pe.wait_ge(s["xeT_ready"], g + 1 + base)
                    for j in range(GT):
                        last = pe.matmul(bank[3 + 2 * h + j // 2][:, j % 2 * 2 * D:(j % 2 + 1) * 2 * D], xeT[h][:, j, :],
                                         gu_w[:, bass.ds(ex[j // UT], 1), :].rearrange("p a n -> p (a n)"), start=True, stop=True)
                    last.then_inc(s["gu_done"], 1)

                def turn_h(g, h):
                    pe.wait_ge(s["hid_done"], g + 1 + base)
                    pe.wait_ge(s["hidT_ready"], g + base + 1)
                    for j in range(GT):
                        last = pe.transpose(bank[1][:, j * P:(j + 1) * P], hid[h][:, j, :], ident[:, :])
                    last.then_inc(s["hid_tp"], 1)

                def down(g, h, ex):
                    pe.wait_ge(s["hidT_ready"], g + 2 + base)
                    pe.wait_ge(s["y_ready"], g + base + 1)
                    for j in range(GT):
                        last = pe.matmul(bank[7][:, j * D:(j + 1) * D], hidT[h][:, j, :],
                                         dn_w[:, bass.ds(ex[j // UT], 1), :].rearrange("p a n -> p (a n)"), start=True, stop=True)
                    last.then_inc(s["y_done"], 1)

                def stage(g, r, i, known, edge=None):
                    h = r % 2
                    ex = experts_of(g)
                    if edge is None or edge >= 2:
                        done = known[r - 2] if r >= 2 else experts_of(g - 2)
                    known.append(ex)
                    gate_up(g, h, ex)
                    if edge is None or edge < GROUPS - 1:
                        turn_x(g + 1, (r + 1) % NX, i + (r + 1) // NX)
                    if edge is None or edge >= 1:
                        turn_h(g - 1, 1 - h)
                    if edge is None or edge >= 2:
                        down(g - 2, h, done)

                turn_x(0, 0, 0)
                known = []
                for g in range(NX):
                    stage(g, g, 0, known, g)
                with pe.Fori(1, GROUPS // NX - 1) as i:
                    known = []
                    for r in range(NX):
                        stage(NX * i + r, r, i, known)
                known = []
                for g in range(GROUPS - NX, GROUPS):
                    stage(g, g % NX, GROUPS // NX - 1, known, g)
                down(GROUPS - 2, 0, experts_of(GROUPS - 2))
                turn_h(GROUPS - 1, 1)
                down(GROUPS - 1, 1, experts_of(GROUPS - 1))

            tables(0)
            experts(0)

            def project_q(n):
                pe.wait_ge(s["att_xT_ready"], n + B + 1)
                pe.matmul(bank[0][:, :], b_wq[:, :], xnT[:, :], start=True, stop=True).then_inc(s["bproj_done"], 1)

            def project_k(n):
                pe.wait_ge(s["q_parts"], n + 1)
                pe.matmul(bank[0][:, :], b_wk[:, :], xnT[:, :], start=True, stop=True).then_inc(s["bproj_done"], 1)

            def project_tokens(n, half):
                if half:
                    pe.wait_ge(s["btok_ready"], 2 * n + 1)
                else:
                    pe.wait_ge(s["first_parts"], n + B + 1)
                for j in range(2):
                    t = 2 * half + j
                    last = pe.matmul(bank[0][:, j * 2 * D:(j + 1) * 2 * D], xnT[:, t * P:(t + 1) * P], b_wqv[:, :],
                                     start=True, stop=True)
                last.then_inc(s["tokproj_done"], 1)

            def scores(b, h, n, first):
                t, m = n // (H // 2), n % (H // 2)
                if n >= RING:
                    pe.wait_ge(s["bmax_done"], b * PAIRS + n - RING + 1)
                elif not first:
                    pe.wait_ge(s["bmax_done"], b * PAIRS - (PAIRS - 1 - n) % RING)
                for q in range(2):
                    last = pe.matmul(pair[n % RING][:, q, :], stackq[h][:, 2 * m + q, t * P:(t + 1) * P],
                                     stackk[h][:, 2 * m + q, :], start=True, stop=True)
                last.then_inc(s["bsc_done"], 1)

            def turn_largest(b, h):
                pe.wait_ge(s["bmax_done"], b * PAIRS + PAIRS)
                for t in range(TB):
                    last = pe.transpose(bank[0][0:H, t * P:(t + 1) * P], smax[h][:, t, :], ident[:, :])
                last.then_inc(s["mT_done"], 1)

            def spread_indices(b):
                pe.wait_ge(s["idg_done"], b + 1)
                idr = idg[:, :, :].rearrange("h a u -> h (a u)")
                pe.matmul(bank[1][:, 0:P], ones[0:H, :], idr, start=True, stop=True)
                pe.matmul(bank[1][:, P:P + 1], idr, ones[0:H, 0:1], start=True, stop=True).then_inc(s["idx_done"], 1)

            def select_q(b, h):
                pe.wait_ge(s["sel_done"], b + 1)
                pe.wait_ge(s["btok_ready"], 2 * b + 2)
                for t in range(TB):
                    last = pe.matmul(bank[1][:, 0:P], toks[h][:, t, 0:D], selT[:, t, :], start=(t == 0), stop=(t == TB - 1))
                last.then_inc(s["qsel_done"], 1)

            def selected_scores(b, h):
                pe.wait_ge(s["qsel_ready"], b + 1)
                pe.matmul(bank[1][:, :], qsel[:, :], kTs[h][:, :], start=True, stop=True).then_inc(s["att_done"], 1)

            def turn_exp(b):
                pe.wait_ge(s["aexp_done"], b + 1)
                for t in range(TB):
                    last = pe.transpose(bank[1][:, t * P:(t + 1) * P], aexp[:, t * P:(t + 1) * P], ident[:, :])
                last.then_inc(s["aeT_done"], 1)

            def context(b, h):
                pe.wait_ge(s["aeT_ready"], b + 1)
                for t in range(TB):
                    last = pe.matmul(bank[1][:, 0:P], toks[h][:, t, D:2 * D], aexpT[:, t * P:(t + 1) * P], start=(t == 0), stop=(t == TB - 1))
                last.then_inc(s["cx_done"], 1)

            def context_out(b):
                pe.wait_ge(s["cx_ready"], b + 1)
                pe.matmul(bank[1][:, 0:D], cxm[:, :], b_wo[:, :], start=True, stop=True).then_inc(s["cw_done"], 1)

            def scatter_context(b):
                pe.wait_ge(s["selrow_done"], b + 1)
                pe.wait_ge(s["cw_ready"], b + 1)
                for t in range(TB):
                    last = pe.matmul(bank[1][:, t * D:(t + 1) * D], sel[:, t * P:(t + 1) * P], cwo[:, :], start=True, stop=True)
                last.then_inc(s["bo_done"], 1)

            def body(b, u, h, last=True, next=True, fetch=True):
                pe.wait_ge(s[f"stack_in{h}"], (u + 1 + B // 2) * 16 * STACK_DMAS)
                for n in range(PAIRS):
                    scores(b, h, n, not last)
                    if last and n == 1:
                        turn_largest(b - 1, 1 - h)
                    if last and n == 4:
                        spread_indices(b - 1)
                    if next and n == 5:
                        if last:
                            pe.wait_ge(s["mTs_done"], b)
                        turn(b + 1 + B, "att", xna)
                    if last and n == 7:
                        select_q(b - 1, 1 - h)
                    if next and n == 8:
                        project_q(b + 1)
                    if last and n == 9:
                        selected_scores(b - 1, 1 - h)
                    if next and n == 10:
                        project_k(b + 1)
                    if last and n == 13:
                        turn_exp(b - 1)
                    if last and n == 14:
                        context(b - 1, 1 - h)
                    if next and n == 15:
                        project_tokens(b + 1, 0)
                    if last and n == 17:
                        context_out(b - 1)
                    if next and n == 18:
                        project_tokens(b + 1, 1)
                    if last and n == 20:
                        scatter_context(b - 1)
                    if last and n == 26:
                        turn(b - 1 + B, "ffn", xnf[1 - h])
                    if last and n == 27:
                        logits(b - 1 + B, bank[1])
                    if last and n == 31:
                        ranks(b - 1 + B, bank[1])

            pe.wait_ge(s["zeroed_k"], 1)
            pe.wait_ge(s["zeroed_q"], 1)
            turn(B, "att", xna)
            project_q(0)
            project_k(0)
            for half in range(2):
                project_tokens(0, half)
            each_batch(pe, body)
            b = B - 1
            turn_largest(b, 1)
            spread_indices(b)
            select_q(b, 1)
            selected_scores(b, 1)
            turn_exp(b)
            context(b, 1)
            context_out(b)
            scatter_context(b)
            turn(b + B, "ffn", xnf[1])
            logits(b + B, bank[1])
            ranks(b + B, bank[1])
            tables(1)
            experts(1)


_NAMES = {"x": "L0_attn_a_x", "a_Wv": "L0_attn_a_Wv", "a_bv": "L0_attn_a_bv",
          "a_Wn": "L0_attn_a_Wn", "a_Wo": "L0_attn_a_Wo", "a_bo": "L0_attn_a_bo",
          "b_bv": "L0_attn_b_bv", "b_bo": "L0_attn_b_bo",
          "f_router": "L0_ffn_router_w", "f_gate": "L0_ffn_gate_w", "f_up": "L0_ffn_up_w", "f_down": "L0_ffn_down_w"}
_SPREAD = {"b_wqT": "L0_attn_b_wq", "b_wkT": "L0_attn_b_wk", "b_bq": "L0_attn_b_bq", "b_bk": "L0_attn_b_bk"}
_TURNED = {"b_wvT": "L0_attn_b_wv", "b_woT": "L0_attn_b_wo"}


def kernel(**inputs):
    import numpy as np
    import concourse.bacc as bacc
    from concourse.bass_utils import run_bass_kernel_spmd

    arrays = {n: np.ascontiguousarray(inputs[src]) for n, src in _NAMES.items()}
    for n, src in _TURNED.items():
        arrays[n] = np.ascontiguousarray(np.asarray(inputs[src]).T)
    for n, src in _SPREAD.items():
        a = np.asarray(inputs[src])
        a = np.moveaxis(a.reshape((H, DH) + a.shape[1:]), 0, 1).reshape(a.shape)
        arrays[n] = np.ascontiguousarray(a.T)
    for n, src in (("a_Wqk", "L0_attn_a_Wqk"), ("a_bqk", "L0_attn_a_bqk")):
        a = np.asarray(inputs[src])
        arrays[n] = np.ascontiguousarray(np.moveaxis(a.reshape(a.shape[:-1] + (2, H, DH)), -1, -2).reshape(a.shape))
    arrays["a_bnr"] = np.tile(np.asarray(inputs["L0_attn_a_bn"]), DH)
    nc = bacc.Bacc("TRN2", target_bir_lowering=False, num_devices=1)
    w = {n: nc.dram_tensor("in_" + n, a.shape, mybir.dt.from_np(a.dtype), kind="ExternalInput").ap() for n, a in arrays.items()}
    out = nc.dram_tensor("out", (B, SEQ, D), F32, kind="ExternalOutput").ap()
    build(nc, w, out)
    r = run_bass_kernel_spmd(nc, [{"in_" + n: a for n, a in arrays.items()}], core_ids=[0])
    return r.results[0]["out"]
```
